# Optimizing a Trainium2 kernel written in Bass

```python
import numpy as np
import jax
import jax.numpy as jnp

def _softmax(x, axis=-1):
    return jax.nn.softmax(x, axis=axis)

def _gelu(x):
    return jax.nn.gelu(x, approximate=True)

def _silu(x):
    return jax.nn.silu(x)

def _sigmoid(x):
    return jax.nn.sigmoid(x)

def _layernorm(x, axis=-1, eps=1e-05):
    m = jnp.mean(x, axis=axis, keepdims=True)
    v = jnp.var(x, axis=axis, keepdims=True)
    return (x - m) / jnp.sqrt(v + eps)

def _scatter_add(tgt, idx, src, axis=0):
    return tgt.at[idx].add(src)

def _segment_sum(src, seg, n):
    return jax.ops.segment_sum(src, seg, n)
kernel_name = 'mk_gnn_resnorm_d2_gnn_r64_5ae1d5'

def setup_inputs(seed: int=0):
    np.random.seed(seed)
    _w = jnp.asarray

    def _rec_inputs():
        import jax
        import jax.numpy as jnp
        _gk = jax.random.key(seed)
        x = -0.0003713 + 1 * jax.random.normal(jax.random.fold_in(_gk, 1), (50000, 128), jnp.float32)
        src = jax.random.randint(jax.random.fold_in(_gk, 2), (12500,), 0, 50000, jnp.int32)
        dst = jax.random.randint(jax.random.fold_in(_gk, 3), (12500,), 0, 50000, jnp.int32)
        _o = jnp.argsort(dst, stable=True)
        src = src[_o]
        dst = dst[_o]
        edge_attr_128 = -6.74381e-05 + 0.999835 * jax.random.normal(jax.random.fold_in(_gk, 11), (12500, 128), jnp.float32)
        return (x, src, dst, edge_attr_128)
    x, src, dst, edge_attr_128 = _rec_inputs()

    def _L0_gnn_setup():
        import jax, jax.numpy as jnp
        import numpy as np
        ALPHA = 0.2
        EPS = 1e-16

        def gat_layer(x, W, a, src, dst, n_nodes, concat):
            h = x @ W
            f = h.shape[-1]
            s_src = h @ a[:f]
            s_dst = h @ a[f:]
            score = s_src[src] + s_dst[dst]
            edge_e = jnp.exp(-jax.nn.leaky_relu(score, ALPHA))
            rowsum = jax.ops.segment_sum(edge_e, src, num_segments=n_nodes)
            msg = jax.ops.segment_sum(edge_e[:, None] * h[dst], src, num_segments=n_nodes)
            h_prime = msg / (rowsum[:, None] + EPS)
            return jax.nn.elu(h_prime) if concat else h_prime
        key = jax.random.key(seed)
        ks = jax.random.split(key, 6)
        N, E = (100000, 50000)
        nfeat, nhid, nout, nheads = (128, 64, 128, 8)
        x = jax.random.normal(ks[0], (N, nfeat), jnp.float32)
        edge_index = jax.random.randint(ks[1], (2, E), 0, N)
        W1 = jax.random.normal(ks[2], (nheads, nfeat, nhid), jnp.float32) * (1.0 / np.sqrt(nfeat))
        a1 = jax.random.normal(ks[3], (nheads, 2 * nhid), jnp.float32) * 0.1
        W2 = jax.random.normal(ks[4], (nheads * nhid, nout), jnp.float32) * (1.0 / np.sqrt(nheads * nhid))
        a2 = jax.random.normal(ks[5], (2 * nout,), jnp.float32) * 0.1
        return {'x': x, 'edge_index': edge_index, 'W1': W1, 'a1': a1, 'W2': W2, 'a2': a2}
    _L0_gnn_all = _L0_gnn_setup()
    _L0_gnn_in = {k: v for k, v in _L0_gnn_all.items() if k in ('W1', 'a1', 'W2', 'a2')}
    del _L0_gnn_all

    def _L1_gnn_setup():
        import jax, jax.numpy as jnp
        import numpy as np
        N, E, D, H = (50000, 625000, 128, 256)
        MP_THRESHOLD = 0.5
        COS_EPS = 1e-08
        key = jax.random.key(seed)
        ks = jax.random.split(key, 6)
        x = jax.random.normal(ks[0], (N, D), jnp.float32)
        edge_attr = jax.random.normal(ks[1], (E, D), jnp.float32)
        W1 = jax.random.normal(ks[2], (D, H), jnp.float32) / np.sqrt(D).astype(np.float32)
        b1 = jnp.zeros((H,), jnp.float32)
        W2 = jax.random.normal(ks[3], (H, D), jnp.float32) / np.sqrt(H).astype(np.float32)
        b2 = jnp.zeros((D,), jnp.float32)
        eps = jnp.zeros((), jnp.float32)
        edge_index = jax.random.randint(ks[4], (2, E), 0, N)
        return dict(x=x, edge_attr=edge_attr, W1=W1, b1=b1, W2=W2, b2=b2, eps=eps, edge_index=edge_index)
    _L1_gnn_all = _L1_gnn_setup()
    _L1_gnn_in = {k: v for k, v in _L1_gnn_all.items() if k in ('W1', 'b1', 'W2', 'b2', 'eps')}
    del _L1_gnn_all
    return {'x': x, 'src': src, 'dst': dst, 'edge_attr_128': edge_attr_128, 'L0_gnn_W1': _L0_gnn_in['W1'], 'L0_gnn_a1': _L0_gnn_in['a1'], 'L0_gnn_W2': _L0_gnn_in['W2'], 'L0_gnn_a2': _L0_gnn_in['a2'], 'L1_gnn_W1': _L1_gnn_in['W1'], 'L1_gnn_b1': _L1_gnn_in['b1'], 'L1_gnn_W2': _L1_gnn_in['W2'], 'L1_gnn_b2': _L1_gnn_in['b2'], 'L1_gnn_eps': _L1_gnn_in['eps']}

def reference(x, src, dst, edge_attr_128, L0_gnn_W1, L0_gnn_a1, L0_gnn_W2, L0_gnn_a2, L1_gnn_W1, L1_gnn_b1, L1_gnn_W2, L1_gnn_b2, L1_gnn_eps):
    import jax
    import jax.numpy as jnp

    def _L0_gnn_ref(x, edge_index, W1, a1, W2, a2):
        import jax, jax.numpy as jnp
        import numpy as np
        ALPHA = 0.2
        EPS = 1e-16

        def gat_layer(x, W, a, src, dst, n_nodes, concat):
            h = x @ W
            f = h.shape[-1]
            s_src = h @ a[:f]
            s_dst = h @ a[f:]
            score = s_src[src] + s_dst[dst]
            edge_e = jnp.exp(-jax.nn.leaky_relu(score, ALPHA))
            rowsum = jax.ops.segment_sum(edge_e, src, num_segments=n_nodes)
            msg = jax.ops.segment_sum(edge_e[:, None] * h[dst], src, num_segments=n_nodes)
            h_prime = msg / (rowsum[:, None] + EPS)
            return jax.nn.elu(h_prime) if concat else h_prime
        N = x.shape[0]
        src, dst = (edge_index[0], edge_index[1])
        deg = jax.ops.segment_sum(jnp.ones(src.shape[0], jnp.float32), src, num_segments=N)
        heads = [gat_layer(x, W1[i], a1[i], src, dst, N, True) for i in range(W1.shape[0])]
        x_ = jnp.concatenate(heads, axis=1)
        h = gat_layer(x_, W2, a2, src, dst, N, False)
        h = jnp.where((deg == 0.0)[:, None], x, h)
        return jax.nn.elu(h)

    def _L1_gnn_ref(x, edge_attr, W1, b1, W2, b2, eps, edge_index):
        import jax, jax.numpy as jnp
        import numpy as np
        N, E, D, H = (50000, 625000, 128, 256)
        MP_THRESHOLD = 0.5
        COS_EPS = 1e-08
        src, dst = (edge_index[0], edge_index[1])
        x_src = x[src]
        x_dst = x[dst]
        num = jnp.sum(x_src * x_dst, axis=-1)
        den = jnp.maximum(jnp.linalg.norm(x_src, axis=-1), COS_EPS) * jnp.maximum(jnp.linalg.norm(x_dst, axis=-1), COS_EPS)
        sim = num / den
        mask = ((sim + 1.0) * 0.5 >= MP_THRESHOLD).astype(x.dtype)
        msg = jax.nn.relu(x_src + edge_attr) * mask[:, None]
        agg = jax.ops.segment_sum(msg, dst, num_segments=x.shape[0])
        h = (1.0 + eps) * x + agg
        return jax.nn.relu(h @ W1 + b1) @ W2 + b2
    edge_index = jnp.stack([src, dst])
    x = _layernorm(x + _L0_gnn_ref(x, edge_index, L0_gnn_W1, L0_gnn_a1, L0_gnn_W2, L0_gnn_a2), axis=-1)
    x = _layernorm(x + _L1_gnn_ref(x, edge_attr_128, L1_gnn_W1, L1_gnn_b1, L1_gnn_W2, L1_gnn_b2, L1_gnn_eps, edge_index), axis=-1)
    return x

_drawn_inputs = setup_inputs


def setup_inputs(seed=0):
    import zlib

    import numpy as np

    out = dict(_drawn_inputs(seed))
    spreads = {'L1_gnn_b1': (0.0, 0.1), 'L1_gnn_b2': (0.0, 0.1)}
    factors = {'L0_gnn_a1': 4.192, 'L0_gnn_a2': 4.647}
    for name, (base, spread) in spreads.items():
        noise = np.random.default_rng([zlib.crc32(name.encode()), seed]).standard_normal(out[name].shape)
        drawn = base * np.exp(spread * noise) if base else spread * noise
        out[name] = jnp.asarray(drawn.astype(out[name].dtype))
    for name, factor in factors.items():
        out[name] = (out[name] * factor).astype(out[name].dtype)
    return out
```

```python
import math
import concourse.bass as bass
from concourse import mybir
from concourse.alu_op_type import AluOpType as ALU
from contextlib import ExitStack

F32 = mybir.dt.float32
BF16 = mybir.dt.bfloat16
I32 = mybir.dt.int32
ACT = mybir.ActivationFunctionType
AX = mybir.AxisListType
ds = bass.ds


def build_gnn(nc, x, src, dst, edge_attr, W1g, a1g, W2g, a2g, W1m, b1m, W2m, b2m, epsm, out):
    N, D = x.shape
    E = src.shape[0]
    P = 125
    T = E // P
    U = 4
    TURNS = T // U
    LO = 256
    HI = -(-N // LO)
    HH = HI // 2
    assert P * T == E and U * TURNS == T and 2 * HH == HI
    HEADS, _, FH = W1g.shape
    C2 = HEADS * FH // 128
    CHUNKS = N // (P * U)
    assert CHUNKS * P * U == N and CHUNKS % 4 == 0 and FH * HEADS == 512
    NONE = float(E)
    ROUND = float(1.5 * 2 ** 23)

    ctx = ExitStack()
    with ctx:
        def sb(name, shape, dt=F32):
            return ctx.enter_context(nc.sbuf_tensor(name, shape, dt))

        def bank(name, shape, dt=F32):
            return ctx.enter_context(nc.psum_tensor(name, shape, dt))

        def sem(name):
            return ctx.enter_context(nc.semaphore(name))

        def dram(name, shape, dt=F32):
            return nc.dram_tensor(name, shape, dt, kind="Internal").ap()

        xs_room = sb("xs_room", [128, T * D])
        xs_all = xs_room[0:P, :]
        room = {"early": 0, "late": 0}

        def carve(when, rows, *shape):
            size = math.prod(shape)
            at = room[when]
            room[when] = at + size
            assert at + size <= T * D
            flat = xs_room[0:rows, at:at + size]
            names = "abcd"[:len(shape)]
            return flat.rearrange(f"p ({' '.join(names)}) -> p {' '.join(names)}", **dict(zip(names, shape))) if len(shape) > 1 else flat

        def early(rows, *shape):
            return carve("early", rows, *shape)

        def late(rows, *shape):
            return carve("late", rows, *shape)

        ident = sb("ident", [128, 128])
        ident16 = sb("ident16", [128, 128], BF16)
        earlier = sb("earlier", [P, P])
        above = sb("above", [128, 128])
        ones = sb("ones", [128, 512])
        digits = sb("digits", [P, LO], BF16)
        slot_no = sb("slot_no", [P, T])
        edge_no = sb("edge_no", [P, T])

        key_i = sb("key_i", [P, 2, T], I32)
        digit_i = sb("digit_i", [P, 2, 2, T], I32)
        key = sb("key", [P, 2, T])
        digit = sb("digit", [P, 2, 2, T])

        meta_src = [dram(f"meta_src_{k}", (E, 4)) for k in range(2)]
        meta_dst = [dram(f"meta_dst_{k}", (E, 4)) for k in range(2)]

        pb = [bank(f"pb{k}", [128, 512]) for k in range(8)]

        consts_ready = sem("consts_ready")
        pool_step = sem("pool_step")
        pool_go = sem("pool_go")
        keys_loaded = sem("keys_loaded")
        digits_int = sem("digits_int")
        digits_ready = sem("digits_ready")

        hot = sb("hot", [P, U, 2, HI + LO], BF16)
        count_hot_ready = sem("count_hot_ready")
        count_hot_used = sem("count_hot_used")
        degrees_ready = sem("degrees_ready")
        hist_open = sem("hist_open")
        deg = early(HH, 2, 2, LO)
        cum = early(HH, 2, 2, LO)
        rowsum = sb("rowsum", [HH, 2, 2])
        base = sb("base", [HH, 2, 2])
        start_tab = early(HH, 2, 2, LO)
        end_tab = early(HH, 2, LO)
        ends_tmp = early(HH, 2, 2, LO)
        table_step = sem("table_step")
        bases_ready = sem("bases_ready")
        tables_ready = sem("tables_ready")

        hot_ready = sem("hot_ready")
        hot_t_psum = sem("hot_t_psum")
        hot_t_ready = sem("hot_t_ready")
        rows_ready = sem("rows_ready")
        end_found = sem("end_found")
        run_found = sem("run_found")
        found_used = sem("found_used")
        ranks_done = sem("ranks_done")
        run_updated = sem("run_updated")
        run_copied = sem("run_copied")
        found_ready = sem("found_ready")
        found_kept = sem("found_kept")
        hot_t = sb("hot_t", [HH, 2, 4, 128])
        found = sb("found", [P, U, 6])
        keep = sb("keep", [P, T, 6])
        keycol = sb("keycol", [P, U, 2])
        keycol_ready = sem("keycol_ready")
        junk = sb("junk", [P, 2, 4, LO], BF16)
        junk2 = sb("junk2", [P, 2, 2, P], BF16)

        pos = sb("pos", [P, 2, T])
        q = sb("q", [P, 2, T])
        addr_i = sb("addr_i", [P, 2, T], I32)
        rowdata = early(P, 2, T, 4)
        bulk_step = sem("bulk_step")
        rows_to_move = sem("rows_to_move")
        zero = sb("zero", [P, 4 * T])
        meta_zeroed = sem("meta_zeroed")
        SC = 10
        move_idx = sb("move_idx", [P, 2, SC], I32)
        move_row = sb("move_row", [P, 2, SC, 4])
        move_slots = sem("move_slots")
        moved = [[sem(f"moved_{k}{h}") for h in range(2)] for k in range(2)]
        meta_in = early(P, 2, 2, T, 4)
        meta = sb("meta", [P, 2, T, 4])
        meta_loaded = sem("meta_loaded")
        meta_ready = sem("meta_ready")

        w1g = sb("w1g", [D, HEADS, FH])
        w2g = sb("w2g", [128, C2, D + 2])
        wa = sb("wa", [D, 2, HEADS])
        wa_tmp = early(D, 2, HEADS, FH)
        a1b = sb("a1b", [D, HEADS, 2 * FH])
        a2b = sb("a2b", [128, 2 * D])
        w2_tmp = early(128, 2, C2, D)
        w1m = sb("w1m", [D, 2, 128])
        w2m = sb("w2m", [128, 2, D])
        b1 = sb("b1", [128, 2])
        b2 = sb("b2", [1, D])
        eps1 = sb("eps1", [128, 1])
        ln_eps = sb("ln_eps", [128, 1])
        weights_loaded = sem("weights_loaded")
        weights_step = sem("weights_step")
        weights_ready = sem("weights_ready")

        g2 = dram("g2", (E + 1, D + 2))
        x1_rows = dram("x1_rows", (2 * E, D))
        zero_row_stored = sem("zero_row_stored")

        xin = sb("xin", [P, 4, U, D])
        xex = sb("xex", [P, 4, U, D])
        res = sb("res", [P, 4, U, D])
        hin_t = sb("hin_t", [D, U * P])
        hid = sb("hid", [128, 2, U * P])
        post_sum = sb("post_sum", [P, 2, U, D])
        outb = sb("outb", [P, 4, U, D])
        stats = sb("stats", [P, 4, U, 6])
        moment = sb("moment", [P, 4, U, 2])
        rstd = sb("rstd", [P, 4, U])
        post_stat = sb("post_stat", [P, 4, U, 6])
        post_moment = sb("post_moment", [P, 4, U, 2])
        post_rstd = sb("post_rstd", [P, 4, U])
        x_loaded = [sem(f"x_loaded_{k}") for k in range(4)]
        out_stored = [sem(f"out_stored_{k}") for k in range(4)]
        x_exp = sem("x_exp")
        x_half = sem("x_half")
        x_plus_elu = sem("x_plus_elu")
        x_stats = sem("x_stats")
        x_moments = sem("x_moments")
        x_log = sem("x_log")
        x_rstd = sem("x_rstd")
        x1_ready = sem("x1_ready")
        hin_turned = sem("hin_turned")
        hin_t_ready = sem("hin_t_ready")
        hid_psum = sem("hid_psum")
        hid_ready = sem("hid_ready")
        y_psum = sem("y_psum")
        y_sum = sem("y_sum")
        y_stats = sem("y_stats")
        y_moments = sem("y_moments")
        y_log = sem("y_log")
        y_rstd = sem("y_rstd")
        y_out = sem("y_out")

        key_pad = sb("key_pad", [P, 2, T + 2])
        meta_i = sb("meta_i", [P, 2, T, 4], I32)
        next_key = sb("next_key", [P, 2, T])
        out_row = sb("out_row", [P, 2, T], I32)
        shift = sb("shift", [P, P])
        wrap = sb("wrap", [P, P])
        pick_last = sb("pick_last", [P, P])
        pick_first = sb("pick_first", [P, P])
        lists_step = sem("lists_step")
        next_psum = sem("next_psum")
        lists_ready = sem("lists_ready")

        slots_a = sb("slots_a", [P, U, 2], I32)
        xs = sb("xs", [P, U, D])
        xd = sb("xd", [P, U, D])
        xt = sb("xt", [D, 2, U * P])
        lr = sb("lr", [P, U, HEADS])
        key_now = sb("key_now", [P, U + 1])
        key_now_ready = sem("key_now_ready")
        dve_go = sem("dve_go")
        same = sb("same", [P, U, P])
        carry = sb("carry", [P, U, P])
        msg = sb("msg", [P, 2, HEADS * FH])
        esc = sb("esc", [P, U, HEADS])
        agg = sb("agg", [P, U, HEADS * FH + HEADS])
        hp = sb("hp", [P, 2, HEADS * FH])
        hex_ = sb("hex_", [P, 2, HEADS * FH])
        rsum = sb("rsum", [P, U, HEADS])
        xx_t = sb("xx_t", [128, C2, P])
        g2s = sb("g2s", [P, U, D + 2])
        s2_all = sb("s2_all", [P, T])
        aslots_ready = sem("aslots_ready")
        x_in = [sem(f"x_in_{j}") for j in range(U)]
        x_turned = sem("x_turned")
        xt_ready = sem("xt_ready")
        key_rows = sem("key_rows")
        scores_psum = sem("scores_psum")
        lr_half = sem("lr_half")
        lr_ready = sem("lr_ready")
        esc_ready = sem("esc_ready")
        same_ready = sem("same_ready")
        h_psum = sem("h_psum")
        msg_ready = sem("msg_ready")
        agg_psum = sem("agg_psum")
        agg_ready = sem("agg_ready")
        rsum_step = sem("rsum_step")
        rsum_ready = sem("rsum_ready")
        hp_ready = sem("hp_ready")
        hex_ready = sem("hex_ready")
        helu_half = sem("helu_half")
        helu_ready = sem("helu_ready")
        xx_psum = sem("xx_psum")
        xx_ready = sem("xx_ready")
        g2_psum = sem("g2_psum")
        g2_ready = sem("g2_ready")
        g2_stored = sem("g2_stored")
        xs_kept = sem("xs_kept")
        pe_x_stored = sem("pe_x_stored")

        s2_rows = sem("s2_rows")
        s2_step = sem("s2_step")
        s2_ready = sem("s2_ready")
        ends2 = sb("ends2", [P, 2, 2, T + 1])
        cont = sb("cont", [P, T])
        cover = sb("cover", [P, T])
        tail = sb("tail", [P, T])
        after = sb("after", [P, T])
        s2_src = sb("s2_src", [P, T])
        slots_b = sb("slots_b", [P, U], I32)
        g = sb("g", [P, U, D + 2])
        sc2 = sb("sc2", [P, 2, U])
        msg2 = sb("msg2", [P, U, D + 1])
        agg2 = sb("agg2", [P, U, D + 1])
        rs2 = sb("rs2", [P, 2, U])
        g_in = [sem(f"g_in_{j}") for j in range(U)]
        bslots_ready = sem("bslots_ready")
        sc2_a = sem("sc2_a")
        sc2_b = sem("sc2_b")
        sc2_ready = sem("sc2_ready")
        e2_ready = sem("e2_ready")
        x1_stored = sem("x1_stored")

        slots_c = sb("slots_c", [P, U], I32)
        slots_d = sb("slots_d", [P, U, 3], I32)
        cslots_ready = sem("cslots_ready")
        dslots_ready = sem("dslots_ready")
        row_out = sem("row_out")
        ra = late(P, U, D)
        ea = late(P, U, D)
        sqr = late(P, 3, U, D)
        dots = sb("dots", [P, 3, U])
        simt = sb("simt", [P, 4, U])
        hin_d = late(P, U, D)
        abe_in = [sem(f"abe_in_{j}") for j in range(U)]
        squares = sem("squares")
        dots_ready = sem("dots_ready")
        norm_log = sem("norm_log")
        norm_ready = sem("norm_ready")
        sim_step = sem("sim_step")
        relu_step = sem("relu_step")
        hin_ready = sem("hin_ready")
        xs_free = sem("xs_free")
        plain_free = sem("plain_free")
        g2_free = sem("g2_free")
        x1_free = sem("x1_free")
        row_free = sem("row_free")
        out_free = sem("out_free")
        c_loaded = sem("c_loaded")

        hot_t_ps = pb[2][:].bitcast(BF16)
        block = ctx.enter_context(nc.Block())

        @block.sync
        def _(sp):
            sp.dma_start(key_i[:, 0], src.rearrange("(p t) -> p t", t=T)).then_inc(keys_loaded, 16)
            sp.dma_start(key_i[:, 1], dst.rearrange("(p t) -> p t", t=T)).then_inc(keys_loaded, 16)
            sp.wait_ge(consts_ready, 1)
            for tab in meta_src + meta_dst:
                sp.dma_start(tab.rearrange("(p t) c -> p (t c)", p=P), zero[:]).then_inc(meta_zeroed, 16)
            sp.dma_start(w1g[:], W1g.rearrange("h d f -> d h f")).then_inc(weights_loaded, 16)
            sp.dma_start(a1b[:].rearrange("p h f -> p (h f)"), a1g.rearrange("h f -> (h f)").partition_broadcast(D)).then_inc(weights_loaded, 16)
            sp.dma_start(w2g[:, :, 0:D], W2g.rearrange("(c p) f -> p c f", p=128)).then_inc(weights_loaded, 16)
            sp.dma_start(a2b[:], a2g.partition_broadcast(128)).then_inc(weights_loaded, 16)
            sp.dma_start(w1m[:], W1m.rearrange("d (c f) -> d c f", c=2)).then_inc(weights_loaded, 16)
            sp.dma_start(w2m[:], W2m.rearrange("(c p) f -> p c f", p=128)).then_inc(weights_loaded, 16)
            sp.dma_start(b1[:], b1m.rearrange("(c p) -> p c", p=128), allow_slow_non_contiguous=True).then_inc(weights_loaded, 16)
            sp.dma_start(b2[:], b2m.rearrange("(o f) -> o f", o=1)).then_inc(weights_loaded, 16)
            sp.dma_start(eps1[:], epsm.partition_broadcast(128)).then_inc(weights_loaded, 16)
            sp.wait_ge(consts_ready, 1)
            sp.dma_start(g2[E:E + 1, :], zero[0:1, 0:D + 2]).then_inc(zero_row_stored, 16)
            x_chunks = x.rearrange("(n p u) d -> n p (u d)", p=P, u=U)
            out_chunks = out.rearrange("(n p u) d -> n p (u d)", p=P, u=U)

            def chunk(tensor, n):
                return tensor[ds(n, 1)].rearrange("o p f -> (o p) f")

            for k in range(4):
                sp.dma_start(xin[:, k].rearrange("p u d -> p (u d)"), x_chunks[k]).then_inc(x_loaded[k], 16)

            def node_turn(turn, load):
                for k in range(4):
                    n = turn * 4 + k
                    if load:
                        sp.wait_ge(x_plus_elu, n + 1)
                        sp.dma_start(xin[:, k].rearrange("p u d -> p (u d)"), chunk(x_chunks, n + 4)).then_inc(x_loaded[k], 16)
                    sp.wait_ge(y_out, n + 1)
                    sp.dma_start(chunk(out_chunks, n), outb[:, k].rearrange("p u d -> p (u d)")).then_inc(out_stored[k], 16)
                    sp.wait_ge(out_stored[k], turn * 16 + 16)
                    sp.sem_inc(out_free, 1)

            with sp.Fori(0, CHUNKS // 4 - 1) as turn:
                node_turn(turn, True)
            node_turn(CHUNKS // 4 - 1, False)

            for k, tabs in enumerate((meta_src, meta_dst)):
                for h in range(2):
                    sp.wait_ge(moved[k][h], 16 * T // 2)
            for k, tabs in enumerate((meta_src, meta_dst)):
                for h in range(2):
                    sp.dma_start(meta_in[:, k, h].rearrange("p t c -> p (t c)"),
                                 tabs[h].rearrange("(p t) c -> p (t c)", p=P)).then_inc(meta_loaded, 16)

            with sp.Fori(0, TURNS) as turn:
                for j in range(U):
                    sp.wait_ge(x_in[j], turn * 32 + 32)
                sp.dma_start(xs_all[:, ds(turn * (U * D), U * D)], xs[:].rearrange("p u d -> p (u d)")).then_inc(xs_kept, 16)
                sp.wait_ge(x1_ready, turn + CHUNKS + 1)
                sp.dma_start(x1_rows[ds(turn * (U * P) + E, U * P)].rearrange("(u p) d -> p u d", p=P),
                             res[:, 0]).then_inc(pe_x_stored, 16)
                sp.wait_ge(g2_ready, turn * U + 2 * U)
                sp.dma_start(g2[ds(turn * (U * P), U * P)].rearrange("(u p) d -> p u d", p=P),
                             g2s[:]).then_inc(g2_stored, 16)
                for stored, free in ((xs_kept, xs_free), (pe_x_stored, plain_free), (g2_stored, g2_free)):
                    sp.wait_ge(stored, turn * 16 + 16)
                    sp.sem_inc(free, 1)
            with sp.Fori(0, TURNS) as turn:
                sp.wait_ge(x1_ready, turn + CHUNKS + TURNS + 1)
                sp.dma_start(x1_rows[ds(turn * (U * P), U * P)].rearrange("(u p) d -> p u d", p=P),
                             res[:, 1]).then_inc(x1_stored, 16)
                sp.wait_ge(x1_stored, turn * 16 + 16)
                sp.sem_inc(x1_free, 1)
            with sp.Fori(0, TURNS) as turn:
                sp.wait_ge(y_sum, turn + CHUNKS + 1)
                sp.wait_ge(x1_stored, 16 * TURNS)
                sp.dma_start(res[:, 2], x1_rows[ds(turn * (U * P), U * P)].rearrange("(u p) d -> p u d", p=P)).then_inc(c_loaded, 16)

        @block.gpsimd
        def _(pool):
            gp = nc.gpsimd
            gp.memset(zero[:], 0.0)
            gp.memset(ones[:], 1.0)
            gp.memset(ident[:], 0.0).then_inc(pool_step, 1)
            pool.wait_ge(pool_step, 1)
            gp.affine_select(out=ident[:], in_=ident[:], compare_op=ALU.not_equal, fill=1.0, base=0,
                            pattern=[[-1, 128]], channel_multiplier=1)
            gp.affine_select(out=earlier[:], in_=ones[0:P, 0:P], compare_op=ALU.is_gt, fill=0.0, base=0,
                            pattern=[[-1, P]], channel_multiplier=1)
            gp.affine_select(out=above[:], in_=ones[:, 0:128], compare_op=ALU.is_gt, fill=0.0, base=0,
                            pattern=[[1, 128]], channel_multiplier=-1)
            gp.affine_select(out=shift[:], in_=ones[0:P, 0:P], compare_op=ALU.is_equal, fill=0.0, base=-1,
                            pattern=[[-1, P]], channel_multiplier=1)
            gp.affine_select(out=wrap[:], in_=ones[0:P, 0:P], compare_op=ALU.is_equal, fill=0.0, base=P - 1,
                            pattern=[[-1, P]], channel_multiplier=P)
            gp.affine_select(out=pick_last[:], in_=ones[0:P, 0:P], compare_op=ALU.is_equal, fill=0.0, base=-(P - 1),
                            pattern=[[0, P]], channel_multiplier=1)
            gp.affine_select(out=pick_first[:], in_=ones[0:P, 0:P], compare_op=ALU.is_equal, fill=0.0, base=0,
                            pattern=[[0, P]], channel_multiplier=1)
            gp.memset(ln_eps[:], 1e-5)
            gp.memset(ends2[:], -2.0)
            gp.memset(agg[:], 0.0)
            gp.memset(agg2[:], 0.0)
            gp.memset(key_pad[:], -1.0)
            gp.iota(digits[:], [[1, LO]], base=0, channel_multiplier=0, allow_small_or_imprecise_dtypes=True)
            gp.iota(slot_no[:], [[P, T]], base=0, channel_multiplier=1, allow_small_or_imprecise_dtypes=True)
            gp.iota(edge_no[:], [[1, T]], base=0, channel_multiplier=T,
                   allow_small_or_imprecise_dtypes=True).then_inc(pool_step, 1)
            pool.wait_ge(pool_step, 2)
            gp.tensor_copy(ident16[:], ident[:]).then_inc(consts_ready, 1)
            pool.wait_ge(rows_to_move, 1)
            pool.wait_ge(meta_zeroed, 64)
            with pool.Fori(0, T // SC) as turn:
                t0 = turn * SC
                for k in range(2):
                    gp.tensor_copy(move_idx[:, k], addr_i[:, k, ds(t0, SC)])
                    last = gp.tensor_copy(move_row[:, k], rowdata[:, k, ds(t0, SC), :])
                last.then_inc(move_slots, 1)
                pool.wait_ge(move_slots, turn + 1)
                pool.sem_inc(pool_go, 1)
                for j in range(SC):
                    for k, tabs in enumerate((meta_src, meta_dst)):
                        if j >= 2:
                            pool.wait_ge(moved[k][j % 2], turn * (8 * SC) + 16 * (j // 2))
                            pool.sem_inc(pool_go, 1)
                        gp.indirect_dma_start(
                            out=tabs[j % 2], out_offset=bass.IndirectOffsetOnAxis(ap=move_idx[:, k, j:j + 1], axis=0),
                            in_=move_row[:, k, j], in_offset=None).then_inc(moved[k][j % 2], 16)
                for k in range(2):
                    for h in range(2):
                        pool.wait_ge(moved[k][h], turn * (8 * SC) + 8 * SC)
                        pool.sem_inc(pool_go, 1)


            pool.wait_ge(lists_ready, 1)
            with pool.Fori(0, TURNS) as turn:
                pool.wait_ge(xt_ready, turn * 2 + 1)
                pool.sem_inc(pool_go, 1)
                gp.tensor_copy(slots_a[:], meta_i[:, 0, ds(turn * U, U), 0:2]).then_inc(aslots_ready, 1)
                pool.wait_ge(aslots_ready, turn + 1)
                pool.sem_inc(pool_go, 1)
                pool.wait_ge(x_plus_elu, turn + CHUNKS)
                pool.sem_inc(pool_go, 1)
                pool.wait_ge(xs_free, turn + 1)
                pool.sem_inc(pool_go, 1)
                for j in range(U):
                    for k, rows in enumerate((xs, xd)):
                        gp.indirect_dma_start(
                            out=rows[:, j], out_offset=None, in_=x,
                            in_offset=bass.IndirectOffsetOnAxis(ap=slots_a[:, j, k:k + 1], axis=0)).then_inc(x_in[j], 16)
            pool.wait_ge(g2_stored, 16 * TURNS)
            pool.sem_inc(pool_go, 1)
            pool.wait_ge(zero_row_stored, 16)
            pool.sem_inc(pool_go, 1)
            with pool.Fori(0, TURNS) as turn:
                pool.wait_ge(msg_ready, turn + T + 1)
                pool.sem_inc(pool_go, 1)
                gp.tensor_copy(slots_b[:], meta_i[:, 0, ds(turn * U, U), 2]).then_inc(bslots_ready, 1)
                pool.wait_ge(bslots_ready, turn + 1)
                pool.sem_inc(pool_go, 1)
                for j in range(U):
                    gp.indirect_dma_start(
                        out=g[:, j], out_offset=None, in_=g2,
                        in_offset=bass.IndirectOffsetOnAxis(ap=slots_b[:, j:j + 1], axis=0)).then_inc(g_in[j], 16)
            for k in range(4):
                pool.wait_ge(out_stored[k], 16 * (CHUNKS // 4))

            def put_rows(turn, list_no, group):
                gp.tensor_copy(slots_c[:], out_row[:, list_no, ds(turn * U, U)]).then_inc(cslots_ready, 1)
                pool.wait_ge(cslots_ready, turn + TURNS * list_no + 1)
                pool.wait_ge(y_out, turn + group + 1)
                pool.sem_inc(pool_go, 1)
                for j in range(U):
                    gp.indirect_dma_start(
                        out=out, out_offset=bass.IndirectOffsetOnAxis(ap=slots_c[:, j:j + 1], axis=0),
                        in_=outb[:, 0, j], in_offset=None, bounds_check=N - 1, oob_is_err=False).then_inc(row_out, 16)
                    pool.wait_ge(row_out, (turn * U + j) * 16 + (16 * T * list_no + 16))
                    pool.sem_inc(row_free, 1)

            with pool.Fori(0, TURNS) as turn:
                put_rows(turn, 0, CHUNKS)
            pool.wait_ge(pe_x_stored, 16 * TURNS)
            with pool.Fori(0, TURNS) as turn:
                pool.wait_ge(y_sum, turn + CHUNKS + TURNS + 1)
                pool.sem_inc(pool_go, 1)
                gp.tensor_copy(slots_d[:], meta_i[:, 1, ds(turn * U, U), 1:4]).then_inc(dslots_ready, 1)
                pool.wait_ge(dslots_ready, turn + 1)
                pool.sem_inc(pool_go, 1)
                for j in range(U):
                    for k, (rows, table) in enumerate(((ra[:, j], x1_rows), (res[:, 3, j], x1_rows), (ea[:, j], edge_attr))):
                        gp.indirect_dma_start(
                            out=rows, out_offset=None, in_=table,
                            in_offset=bass.IndirectOffsetOnAxis(ap=slots_d[:, j, k:k + 1], axis=0)).then_inc(abe_in[j], 16)
                put_rows(turn, 1, CHUNKS + TURNS)

        @block.vector
        def _(dve):
            v = nc.vector

            def node_sum(n, xv, ex, u):
                flat = "p u d -> p (u d)"
                xv, ex, u = xv.rearrange(flat), ex.rearrange(flat), u.rearrange(flat)
                dve.wait_ge(x_exp, n + 1)
                v.scalar_tensor_tensor(u, ex, 1.0, xv, ALU.min, ALU.add).then_inc(x_half, 1)
                dve.wait_ge(x_half, n + 1)
                v.scalar_tensor_tensor(u, xv, 0.0, u, ALU.max, ALU.add).then_inc(x_plus_elu, 1)
                dve.wait_ge(x_plus_elu, n + 1)
                node_stats(n, u.rearrange("p (u d) -> p u d", d=D), None)

            def node_stats(n, u, k):
                for j in range(U):
                    last = v.bn_stats(stats[:, 0, j], u[:, j])
                last.then_inc(x_stats, 1)

            def node_moments(n, k):
                dve.wait_ge(x_stats, n + 1)
                dve.sem_inc(dve_go, 1)
                for j in range(U):
                    last = v.bn_aggr(moment[:, k, j], stats[:, 0, j])
                last.then_inc(x_moments, 1)

            def node_x1(n, u, k):
                dve.wait_ge(x_rstd, n + 1)
                for j in range(U):
                    last = v.tensor_scalar(u[:, j], u[:, j], moment[:, k, j, 0:1], rstd[:, k, j:j + 1],
                                           ALU.subtract, ALU.mult)
                last.then_inc(x1_ready, 1)

            def result_sum(n, r, k):
                dve.wait_ge(y_psum, n + 1)
                v.tensor_tensor(post_sum[:, k % 2].rearrange("p u d -> p (u d)"), pb[7][0:P, :], r.rearrange("p u d -> p (u d)"), ALU.add).then_inc(y_sum, 1)
                dve.wait_ge(y_sum, n + 2)
                for j in range(U):
                    last = v.bn_stats(post_stat[:, 0, j], post_sum[:, k % 2, j])
                last.then_inc(y_stats, 1)
                dve.wait_ge(y_stats, n + 1)
                dve.sem_inc(dve_go, 1)
                for j in range(U):
                    last = v.bn_aggr(post_moment[:, k, j], post_stat[:, 0, j])
                last.then_inc(y_moments, 1)

            def result(n, k):
                dve.wait_ge(y_rstd, n + 1)
                for j in range(U):
                    last = v.tensor_scalar(outb[:, k, j], post_sum[:, k % 2, j], post_moment[:, k, j, 0:1],
                                           post_rstd[:, k, j:j + 1], ALU.subtract, ALU.mult)
                last.then_inc(y_out, 1)

            dve.wait_ge(keys_loaded, 32)
            v.tensor_scalar(digit_i[:, :, 0], key_i[:], 8, None, ALU.logical_shift_right)
            v.tensor_scalar(digit_i[:, :, 1], key_i[:], LO - 1, None, ALU.bitwise_and).then_inc(digits_int, 1)
            v.tensor_copy(key[:], key_i[:])
            dve.wait_ge(digits_int, 1)
            v.tensor_copy(digit[:], digit_i[:]).then_inc(digits_ready, 1)
            dve.wait_ge(digits_ready, 1)
            dve.wait_ge(consts_ready, 1)

            def one_hots(turn, j, k):
                t = turn * U + j
                v.tensor_scalar(hot[:, j, k, 0:HI], digits[:, 0:HI], digit[:, k, 0, ds(t, 1)], None, ALU.is_equal)
                return v.tensor_scalar(hot[:, j, k, HI:], digits[:], digit[:, k, 1, ds(t, 1)], None, ALU.is_equal)

            with dve.Fori(0, TURNS) as turn:
                for j in range(U):
                    dve.wait_ge(count_hot_used, turn * U + j + 1)
                    for k in range(2):
                        last = one_hots(turn, j, k)
                    last.then_inc(count_hot_ready, 1)
            dve.wait_ge(degrees_ready, 1)
            for k in range(2):
                last = v.tensor_copy(deg[:, k].rearrange("p h l -> p (h l)"), pb[k][0:HH, :])
            last.then_inc(table_step, 1)
            dve.wait_ge(table_step, 1)
            for k in range(2):
                for h in range(2):
                    last = v.tensor_tensor_scan(cum[:, k, h], ones[0:HH, 0:LO], deg[:, k, h], 0.0, ALU.mult, ALU.add)
            last.then_inc(table_step, 1)
            dve.wait_ge(table_step, 2)
            v.tensor_copy(rowsum[:], cum[:, :, :, LO - 1]).then_inc(table_step, 1)
            dve.wait_ge(bases_ready, 1)
            v.tensor_copy(base[:], pb[2][0:HH, 0:4].rearrange("p (k h) -> p k h", k=2)).then_inc(table_step, 1)
            dve.wait_ge(table_step, 4)
            v.tensor_tensor(base[:, :, 1], base[:, :, 1], pb[2][0:HH, 4:6], ALU.add).then_inc(table_step, 1)
            dve.wait_ge(table_step, 5)
            for k in range(2):
                for h in range(2):
                    last = v.tensor_scalar(cum[:, k, h], cum[:, k, h], base[:, k, h:h + 1], None, ALU.add)
            last.then_inc(table_step, 1)
            dve.wait_ge(table_step, 6)
            v.tensor_tensor(start_tab[:], cum[:], deg[:], ALU.subtract)
            v.tensor_scalar(ends_tmp[:, 0], cum[:, 0], -1.0 - NONE, None, ALU.add)
            v.tensor_scalar(ends_tmp[:, 1], deg[:, 0], 0.0, None, ALU.is_gt).then_inc(table_step, 1)
            dve.wait_ge(table_step, 7)
            v.tensor_tensor(ends_tmp[:, 0], ends_tmp[:, 0], ends_tmp[:, 1], ALU.mult).then_inc(table_step, 1)
            dve.wait_ge(table_step, 8)
            v.tensor_scalar(end_tab[:], ends_tmp[:, 0], NONE, None, ALU.add).then_inc(tables_ready, 1)

            with dve.Fori(0, TURNS) as turn:
                v.tensor_copy(keycol[:], key[:, :, ds(turn * U, U)].rearrange("p k u -> p u k")).then_inc(keycol_ready, 1)
                for j in range(U):
                    dve.wait_ge(run_updated, turn * U + j + 1)
                    for k in range(2):
                        last = one_hots(turn, j, k)
                    last.then_inc(hot_ready, 1)
                dve.wait_ge(keycol_ready, turn + 1)
                dve.wait_ge(found_kept, turn + 1)
                for j in range(U):
                    dve.wait_ge(rows_ready, turn * U + j + 1)
                    dve.wait_ge(found_used, turn * U + j + 1)
                    for k in range(2):
                        row = pb[3][0:P, (2 * (j % 2) + k) * 128:][:, 0:P]
                        last = v.scalar_tensor_tensor(junk2[:, j % 2, k], row, keycol[:, j, k:k + 1], earlier[:],
                                               ALU.is_equal, ALU.mult, accum_out=found[:, j, 4 + k:5 + k])
                    last.then_inc(ranks_done, 1)
                    dve.wait_ge(run_found, turn * U + j + 1)
                    for c in range(4):
                        tab = pb[4 + c // 2 * 2 + j % 2][0:P, (c % 2) * LO:(c % 2 + 1) * LO]
                        last = v.tensor_tensor_reduce(out=junk[:, j % 2, c], in0=tab, in1=hot[:, j, c % 2, HI:], scale=1.0,
                                                      scalar=0.0, op0=ALU.mult, op1=ALU.add,
                                                      accum_out=found[:, j, c:c + 1])
                    last.then_inc(found_used, 1)
                    dve.wait_ge(run_updated, turn * U + j + U + 1)
                    for k in range(2):
                        run = start_tab[:, k].rearrange("p h l -> p (h l)")
                        last = v.tensor_tensor(run, pb[k][0:HH, :], run, ALU.add)
                    last.then_inc(run_copied, 1)
                dve.wait_ge(found_used, turn * U + U + 2)
                v.tensor_copy(keep[:, ds(turn * U, U), :], found[:]).then_inc(found_kept, 1)

            dve.wait_ge(found_kept, TURNS + 1)

            def step(ins, n):
                ins.then_inc(bulk_step, 1)
                dve.wait_ge(bulk_step, n)

            for k in range(2):
                last = v.tensor_tensor(pos[:, k], keep[:, :, k], keep[:, :, 4 + k], ALU.add)
            step(last, 1)
            step(v.tensor_scalar(q[:], pos[:], -float(P // 2), 1.0 / P, ALU.add, ALU.mult), 2)
            step(v.tensor_scalar(q[:], q[:], ROUND, None, ALU.add), 3)
            step(v.tensor_scalar(q[:], q[:], ROUND, None, ALU.subtract), 4)
            step(v.tensor_scalar(q[:], q[:], -(P * T - 1.0), None, ALU.mult), 5)
            step(v.scalar_tensor_tensor(q[:], pos[:], float(T), q[:], ALU.mult, ALU.add), 6)
            v.tensor_copy(addr_i[:], q[:])
            v.tensor_copy(rowdata[:, 0, :, 0], key[:, 0])
            v.tensor_copy(rowdata[:, 0, :, 1], key[:, 1])
            v.tensor_copy(rowdata[:, 0, :, 2], keep[:, :, 3])
            v.tensor_copy(rowdata[:, 0, :, 3], keep[:, :, 2])
            v.tensor_copy(rowdata[:, 1, :, 0], key[:, 1])
            v.tensor_copy(rowdata[:, 1, :, 1], keep[:, :, 2])
            v.tensor_copy(rowdata[:, 1, :, 3], edge_no[:])
            step(v.scalar_tensor_tensor(rowdata[:, 1, :, 2], keep[:, :, 3], NONE, pos[:, 0],
                                        ALU.is_equal, ALU.mult), 7)
            v.tensor_tensor(rowdata[:, 1, :, 2], rowdata[:, 1, :, 2], keep[:, :, 3], ALU.add).then_inc(rows_to_move, 1)

            dve.wait_ge(weights_loaded, 9 * 16)
            for k in range(2):
                v.tensor_tensor(wa_tmp[:, k], w1g[:], a1b[:, :, k * FH:(k + 1) * FH], ALU.mult)
                last = v.tensor_tensor(w2_tmp[:, k], w2g[:, :, 0:D],
                                       a2b[:, k * D:(k + 1) * D].unsqueeze(1).broadcast_to([128, C2, D]), ALU.mult)
            v.tensor_scalar(eps1[:], eps1[:], 1.0, None, ALU.add).then_inc(weights_step, 1)
            dve.wait_ge(weights_step, 1)
            for k in range(2):
                v.tensor_reduce(wa[:, k], wa_tmp[:, k], AX.X, ALU.add)
                last = v.tensor_reduce(w2g[:, :, D + k], w2_tmp[:, k], AX.X, ALU.add)
            last.then_inc(weights_ready, 1)

            def node_group(n, k, before):
                if before:
                    node_sum(n + 2, xin[:, (k + 2) % 4], xex[:, (k + 2) % 4], res[:, (k + 2) % 4])
                    node_moments(n + 2, (k + 2) % 4)
                result_sum(n, res[:, k], k)
                if before:
                    node_x1(n + 2, res[:, (k + 2) % 4], (k + 2) % 4)
                dve.wait_ge(out_free, n + 1)
                result(n, k)

            for n in range(2):
                node_sum(n, xin[:, n], xex[:, n], res[:, n])
                node_moments(n, n)
                node_x1(n, res[:, n], n)
            with dve.Fori(0, CHUNKS // 4 - 1) as turn:
                for k in range(4):
                    node_group(turn * 4 + k, k, True)
            for k in range(4):
                node_group(CHUNKS - 4 + k, k, k < 2)
            dve.wait_ge(meta_loaded, 64)
            v.tensor_tensor(meta[:], meta_in[:, :, 0], meta_in[:, :, 1], ALU.add).then_inc(meta_ready, 1)
            dve.wait_ge(meta_ready, 1)

            step(v.tensor_copy(key_pad[:, :, 1:T + 1], meta[:, :, :, 0]), 8)
            step(v.tensor_copy(meta_i[:], meta[:]), 9)
            dve.wait_ge(next_psum, 1)
            step(v.tensor_tensor(next_key[:], pb[2][0:P, 0:2 * T].rearrange("p (k t) -> p k t", k=2),
                                 key_pad[:, :, 1:T + 1], ALU.is_equal), 10)
            step(v.scalar_tensor_tensor(next_key[:], next_key[:], float(4 * N), key_pad[:, :, 1:T + 1],
                                        ALU.mult, ALU.add), 11)
            v.tensor_copy(out_row[:], next_key[:]).then_inc(lists_ready, 1)

            def same_keys(turn, list_no, rows, count):
                v.tensor_copy(key_now[:], key_pad[:, list_no, ds(turn * U, U + 1)]).then_inc(key_now_ready, 1)
                dve.wait_ge(key_now_ready, count)
                dve.wait_ge(key_rows, count)
                for j in range(U):
                    row = rows[0:P, j * P:(j + 1) * P]
                    v.tensor_scalar(same[:, j], row, key_now[:, j + 1:j + 2], None, ALU.is_equal)
                    last = v.tensor_scalar(carry[:, j], row, key_now[:, j:j + 1], pick_last[:, 0:1],
                                           ALU.is_equal, ALU.mult)
                last.then_inc(same_ready, 1)

            with dve.Fori(0, TURNS) as turn:
                group = turn + CHUNKS
                same_keys(turn, 0, pb[2], turn + 1)
                dve.wait_ge(scores_psum, turn + 1)
                scores = pb[3][0:P, 0:U * HEADS]
                v.tensor_scalar(lr[:].rearrange("p u h -> p (u h)"), scores, 0.2, None, ALU.mult).then_inc(lr_half, 1)
                dve.wait_ge(lr_half, turn + 1)
                v.tensor_tensor(lr[:].rearrange("p u h -> p (u h)"), lr[:].rearrange("p u h -> p (u h)"), scores,
                                ALU.max).then_inc(lr_ready, 1)
                dve.wait_ge(plain_free, turn + 1)
                node_sum(group, xd[:], xex[:, 0], res[:, 0])
                node_moments(group, 0)

                def message(j):
                    q = turn * U + j
                    dve.wait_ge(esc_ready, turn + 1)
                    dve.wait_ge(h_psum, q + 1)
                    v.tensor_tensor(msg[:, j % 2].rearrange("p (h f) -> p h f", h=HEADS),
                                    pb[4 + j % 2][0:P, :].rearrange("p (h f) -> p h f", h=HEADS),
                                    esc[:, j].unsqueeze(2).broadcast_to([P, HEADS, FH]), ALU.mult).then_inc(msg_ready, 1)

                def mean(j):
                    q = turn * U + j
                    dve.wait_ge(agg_ready, q + 2)
                    v.tensor_scalar(rsum[:, j], agg[:, j, HEADS * FH:], 1e-16, None, ALU.add).then_inc(rsum_step, 1)
                    dve.wait_ge(rsum_step, q + 1)
                    v.reciprocal(rsum[:, j], rsum[:, j]).then_inc(rsum_ready, 1)
                    dve.wait_ge(rsum_ready, q + 1)
                    v.tensor_tensor(hp[:, j % 2].rearrange("p (h f) -> p h f", h=HEADS),
                                    agg[:, j, 0:HEADS * FH].rearrange("p (h f) -> p h f", h=HEADS),
                                    rsum[:, j].unsqueeze(2).broadcast_to([P, HEADS, FH]), ALU.mult).then_inc(hp_ready, 1)

                def elu(j):
                    q = turn * U + j
                    dve.wait_ge(hex_ready, q + 1)
                    v.tensor_scalar(hex_[:, j % 2], hex_[:, j % 2], 1.0, -1.0, ALU.min, ALU.add).then_inc(helu_half, 1)
                    dve.wait_ge(helu_half, q + 1)
                    v.scalar_tensor_tensor(hex_[:, j % 2], hp[:, j % 2], 0.0, hex_[:, j % 2], ALU.max, ALU.add).then_inc(helu_ready, 1)

                message(0)
                message(1)
                mean(0)
                message(2)
                elu(0)
                mean(1)
                message(3)
                node_x1(group, res[:, 0], 0)
                elu(1)
                mean(2)
                elu(2)
                mean(3)
                elu(3)

            dve.wait_ge(s2_rows, 1)
            v.tensor_copy(ends2[:, 0, :, 0:T], pb[2][0:P, 0:2 * T].rearrange("p (k t) -> p k t", k=2))
            v.tensor_copy(ends2[:, 1, :, 0:T], pb[2][0:P, 2 * T:4 * T].rearrange("p (k t) -> p k t", k=2)).then_inc(s2_step, 1)
            dve.wait_ge(s2_step, 1)

            def s2_do(ins, n):
                ins.then_inc(s2_step, 1)
                dve.wait_ge(s2_step, n)

            v.tensor_tensor(cont[:], ends2[:, 0, 1, 0:T], ends2[:, 1, 1, 1:T + 1], ALU.is_equal)
            v.tensor_tensor(cover[:], ends2[:, 0, 1, 0:T], ends2[:, 0, 1, 1:T + 1], ALU.is_equal)
            s2_do(v.tensor_tensor(tail[:], ends2[:, 1, 0, 1:T + 1], ends2[:, 0, 0, 0:T], ALU.subtract), 2)
            s2_do(v.tensor_tensor(tail[:], tail[:], cont[:], ALU.mult), 3)
            s2_do(v.tensor_tensor(tail[:], tail[:], ends2[:, 0, 0, 0:T], ALU.add), 4)
            s2_do(v.tensor_scalar(cont[:], cover[:], -1.0, 1.0, ALU.mult, ALU.add), 5)
            s2_do(v.tensor_tensor(tail[:], tail[:], cont[:], ALU.mult), 6)
            v.tensor_copy(cont[:], cover[:, ::-1])
            s2_do(v.tensor_copy(ends2[:, 1, 0, 0:T], tail[:, ::-1]), 7)
            s2_do(v.tensor_tensor_scan(after[:], cont[:], ends2[:, 1, 0, 0:T], 0.0, ALU.mult, ALU.add), 8)
            s2_do(v.tensor_tensor(tail[:], after[:, ::-1], s2_all[:], ALU.subtract), 9)
            s2_do(v.tensor_tensor(cont[:], key_pad[:, 0, 1:T + 1], ends2[:, 0, 1, 0:T], ALU.is_equal), 10)
            s2_do(v.tensor_tensor(tail[:], tail[:], cont[:], ALU.mult), 11)
            v.tensor_tensor(s2_src[:], tail[:], s2_all[:], ALU.add).then_inc(s2_ready, 1)
            dve.wait_ge(s2_ready, 1)
            with dve.Fori(0, TURNS) as turn:
                group = turn + (CHUNKS + TURNS)
                same_keys(turn, 0, pb[2], turn + TURNS + 1)
                for j in range(U):
                    dve.wait_ge(g_in[j], turn * 16 + 16)
                v.tensor_tensor(sc2[:, 0], g[:, :, D + 1], s2_src[:, ds(turn * U, U)], ALU.add).then_inc(sc2_a, 1)
                dve.wait_ge(sc2_a, turn + 1)
                v.tensor_scalar(sc2[:, 1], sc2[:, 0], 0.2, None, ALU.mult).then_inc(sc2_b, 1)
                dve.wait_ge(sc2_b, turn + 1)
                v.tensor_tensor(sc2[:, 0], sc2[:, 0], sc2[:, 1], ALU.max).then_inc(sc2_ready, 1)
                dve.wait_ge(e2_ready, turn + 1)
                for j in range(U):
                    last = v.tensor_scalar(msg2[:, j, 0:D], g[:, j, 0:D], msg2[:, j, D:D + 1], None, ALU.mult)
                last.then_inc(msg_ready, 1)
                dve.wait_ge(agg_ready, (turn * U) + (T + U + 1))
                v.tensor_scalar(rs2[:, 0], agg2[:, :, D], 1e-16, None, ALU.add).then_inc(rsum_step, 1)
                dve.wait_ge(rsum_step, turn + T + 1)
                v.reciprocal(rs2[:, 1], rs2[:, 0]).then_inc(rsum_ready, 1)
                dve.wait_ge(rsum_ready, turn + T + 1)
                v.tensor_tensor(xd[:], agg2[:, :, 0:D], rs2[:, 1].unsqueeze(2).broadcast_to([P, U, D]),
                                ALU.mult).then_inc(hp_ready, 1)
                dve.wait_ge(x_exp, group + 1)
                dve.wait_ge(x1_free, turn + 1)
                flat = "p u d -> p (u d)"
                v.scalar_tensor_tensor(res[:, 1].rearrange(flat), xex[:, 0].rearrange(flat), 1.0,
                                       xs_all[:, ds(turn * (U * D), U * D)], ALU.min, ALU.add).then_inc(x_half, 1)
                dve.wait_ge(x_half, group + 1)
                v.scalar_tensor_tensor(res[:, 1].rearrange(flat), xd[:].rearrange(flat), 0.0, res[:, 1].rearrange(flat),
                                       ALU.max, ALU.add).then_inc(x_plus_elu, 1)
                dve.wait_ge(x_plus_elu, group + 1)
                node_stats(group, res[:, 1], 0)
                node_moments(group, 0)
                node_x1(group, res[:, 1], 0)

            dve.wait_ge(out_free, CHUNKS + 4)
            with dve.Fori(0, TURNS) as turn:
                dve.wait_ge(y_out, turn + CHUNKS)
                result_sum(turn + CHUNKS, res[:, 2], 0)
                dve.wait_ge(row_free, turn * U + 1)
                result(turn + CHUNKS, 0)

            with dve.Fori(0, TURNS) as turn:
                same_keys(turn, 1, pb[2], turn + 2 * TURNS + 1)
                for j in range(U):
                    dve.wait_ge(abe_in[j], turn * 48 + 48)
                v.tensor_tensor(sqr[:, 0], ra[:], res[:, 3], ALU.mult).then_inc(squares, 1)
                dve.wait_ge(squares, turn * 3 + 3)
                for k in range(3):
                    last = v.tensor_reduce(dots[:, k], sqr[:, k], AX.X, ALU.add)
                last.then_inc(dots_ready, 1)
                v.tensor_tensor(ea[:], ea[:], ra[:], ALU.add).then_inc(relu_step, 1)
                dve.wait_ge(dots_ready, turn + 1)
                v.tensor_scalar(simt[:, 0:2], dots[:, 1:3], 1e-16, None, ALU.max).then_inc(sim_step, 1)
                dve.wait_ge(norm_ready, turn + 1)
                v.reciprocal(simt[:, 0:2], simt[:, 2:4]).then_inc(sim_step, 1)
                dve.wait_ge(sim_step, turn * 6 + 2)
                v.tensor_tensor(simt[:, 0], simt[:, 0], simt[:, 1], ALU.mult).then_inc(sim_step, 1)
                dve.wait_ge(sim_step, turn * 6 + 3)
                v.tensor_tensor(simt[:, 0], simt[:, 0], dots[:, 0], ALU.mult).then_inc(sim_step, 1)
                dve.wait_ge(sim_step, turn * 6 + 4)
                v.tensor_scalar(simt[:, 0], simt[:, 0], 1.0, 0.5, ALU.add, ALU.mult).then_inc(sim_step, 1)
                dve.wait_ge(sim_step, turn * 6 + 5)
                v.tensor_scalar(simt[:, 1], simt[:, 0], 0.5, None, ALU.is_ge).then_inc(sim_step, 1)
                dve.wait_ge(sim_step, turn * 6 + 6)
                dve.wait_ge(relu_step, turn + 1)
                for j in range(U):
                    last = v.tensor_scalar(msg2[:, j, 0:D], ea[:, j], 0.0, simt[:, 1, j:j + 1], ALU.max, ALU.mult)
                last.then_inc(msg_ready, 1)
                dve.wait_ge(agg_ready, (turn * U) + (2 * T + U + 1))
                v.scalar_tensor_tensor(hin_d[:], res[:, 3], eps1[0:P, 0:1], agg2[:, :, 0:D], ALU.mult, ALU.add).then_inc(hin_ready, 1)
                dve.wait_ge(y_out, turn + (CHUNKS + TURNS))
                result_sum(turn + (CHUNKS + TURNS), res[:, 3], 0)
                dve.wait_ge(row_free, turn * U + T + 1)
                result(turn + (CHUNKS + TURNS), 0)


        @block.tensor
        def _(pe):
            te = nc.tensor
            pe.wait_ge(consts_ready, 1)
            pe.sem_inc(count_hot_used, U)
            pe.wait_ge(hist_open, 1)
            for k in range(2):
                te.matmul(pb[k][0:HH, :], zero[0:1, 0:HH], ones[0:1, :], start=True, stop=False)
            with pe.Fori(0, TURNS) as turn:
                for j in range(U):
                    pe.wait_ge(count_hot_ready, turn * U + j + 1)
                    for k in range(2):
                        for h in range(2):
                            last = te.matmul(pb[k][0:HH, h * LO:(h + 1) * LO], hot[:, j, k, h * HH:(h + 1) * HH],
                                             hot[:, j, k, HI:], start=False, stop=False)
                    last.then_inc(count_hot_used, 1)
            for k in range(2):
                last = te.matmul(pb[k][0:HH, :], zero[0:1, 0:HH], ones[0:1, :], start=False, stop=True)
            last.then_inc(degrees_ready, 1)
            pe.wait_ge(table_step, 3)
            te.matmul(pb[2][0:HH, 0:4], above[0:HH, 0:HH], rowsum[:].rearrange("p k h -> p (k h)"), start=True, stop=True)
            te.matmul(pb[2][0:HH, 4:6], ones[0:HH, 0:HH], rowsum[:, :, 0], start=True, stop=True).then_inc(bases_ready, 1)
            pe.wait_ge(tables_ready, 1)
            pe.sem_inc(run_updated, U)
            with pe.Fori(0, TURNS) as turn:
                def turn_digits(j):
                    pe.wait_ge(hot_ready, turn * U + j + 1)
                    pe.wait_ge(hot_t_ready, turn * U + j + 1)
                    for k in range(2):
                        for h in range(2):
                            o = 4 * (j % 2) + 2 * k + h
                            last = te.transpose(hot_t_ps[0:HH, o * 128:o * 128 + P], hot[:, j, k, h * HH:(h + 1) * HH],
                                                ident16[0:P, 0:P])
                    last.then_inc(hot_t_psum, 1)
                    pe.wait_ge(ranks_done, turn * U + j + 1)
                    for k in range(2):
                        o = 2 * (j % 2) + k
                        last = te.matmul(pb[3][0:P, o * 128:o * 128 + P],
                                         keycol[:, j, k:k + 1].broadcast_to([P, P]), ident[0:P, 0:P],
                                         start=True, stop=True)
                    last.then_inc(rows_ready, 1)

                pe.wait_ge(keycol_ready, turn + 1)
                turn_digits(0)
                for j in range(U):
                    if j + 1 < U:
                        turn_digits(j + 1)
                    pe.wait_ge(hot_t_ready, turn * U + j + 2)
                    pe.wait_ge(found_used, turn * U + j + 1)
                    for c in (1, 0):
                        if c == 0:
                            pe.wait_ge(run_copied, turn * U + j + 1)
                        for k in range(2):
                            for h in range(2):
                                tab = start_tab[:, k, h] if c == 0 else end_tab[:, h]
                                last = te.matmul(pb[4 + 2 * c + j % 2][0:P, k * LO:(k + 1) * LO],
                                                 hot_t[:, j % 2, 2 * k + h, 0:P], tab, start=(h == 0), stop=(h == 1))
                    last.then_inc(run_found, 1)
                    for k in range(2):
                        for h in range(2):
                            last = te.matmul(pb[k][0:HH, h * LO:(h + 1) * LO], hot[:, j, k, h * HH:(h + 1) * HH],
                                             hot[:, j, k, HI:], start=True, stop=True)
                    last.then_inc(run_updated, 1)

            pe.wait_ge(weights_ready, 1)

            def turn_hin(n, src_rows, ready, value):
                pe.wait_ge(ready, value)
                pe.wait_ge(hin_t_ready, n + 1)
                for j in range(U):
                    last = te.transpose(pb[4][:, j * P:(j + 1) * P], src_rows[:, j], ident[0:P, 0:P])
                last.then_inc(hin_turned, 1)

            def hidden(n):
                pe.wait_ge(hin_t_ready, n + 2)
                for c in range(2):
                    pe.wait_ge(hid_ready, n * 2 + c + 1)
                    te.matmul(pb[5 + c][:, 0:U * P], w1m[:, c], hin_t[:], start=True, stop=True).then_inc(hid_psum, 1)

            def output(n):
                pe.wait_ge(y_sum, n + 1)
                pe.wait_ge(hid_ready, n * 2 + 4)
                for j in range(U):
                    y = pb[7][0:P, j * D:(j + 1) * D]
                    te.matmul(y, ones[0:1, 0:P], b2[:], start=True, stop=False)
                    for c in range(2):
                        last = te.matmul(y, hid[:, c, j * P:(j + 1) * P], w2m[:, c], start=False, stop=(c == 1))
                last.then_inc(y_psum, 1)

            turn_hin(0, res[:, 0], x1_ready, 1)
            with pe.Fori(0, CHUNKS // 4 - 1) as turn:
                for k in range(4):
                    n = turn * 4 + k
                    hidden(n)
                    turn_hin(n + 1, res[:, (k + 1) % 4], x1_ready, n + 2)
                    output(n)
            for k in range(4):
                n = CHUNKS - 4 + k
                hidden(n)
                if k < 3:
                    turn_hin(n + 1, res[:, k + 1], x1_ready, n + 2)
                output(n)

            pe.wait_ge(bulk_step, 9)
            nxt = pb[2][0:P, 0:2 * T]
            te.matmul(nxt, shift[:], key_pad[:, :, 1:T + 1], start=True, stop=False)
            te.matmul(nxt, wrap[:], key_pad[:, :, 2:T + 2], start=False, stop=True).then_inc(next_psum, 1)

            def key_row(count):
                pe.wait_ge(key_now_ready, count)
                for j in range(U):
                    last = te.matmul(pb[2][0:P, j * P:(j + 1) * P],
                                     key_now[:, j + 1:j + 2].broadcast_to([P, P]),
                                     ident[0:P, 0:P], start=True, stop=True)
                last.then_inc(key_rows, 1)

            pe.wait_ge(lists_ready, 1)
            with pe.Fori(0, TURNS) as turn:
                for k, rows in enumerate((xs, xd)):
                    if k == 0:
                        for j in range(U):
                            pe.wait_ge(x_in[j], turn * 32 + 32)
                    pe.wait_ge(xx_ready, turn * U + 1)
                    pe.wait_ge(g2_ready, turn * U + U)
                    for j in range(U):
                        last = te.transpose(pb[k][:, j * P:(j + 1) * P], rows[:, j], ident[0:P, 0:P])
                    last.then_inc(x_turned, 1)
                key_row(turn + 1)
                pe.wait_ge(xt_ready, turn * 2 + 3)
                pe.wait_ge(lr_ready, turn + 1)
                for j in range(U):
                    for k in range(2):
                        last = te.matmul(pb[3][0:P, j * HEADS:(j + 1) * HEADS], xt[:, k, j * P:(j + 1) * P], wa[:, k],
                                         start=(k == 0), stop=(k == 1))
                last.then_inc(scores_psum, 1)

                def heads(j):
                    if j >= 2:
                        pe.wait_ge(msg_ready, turn * U + j)
                    te.matmul(pb[4 + j % 2][0:P, :], xt[:, 1, j * P:(j + 1) * P], w1g[:].rearrange("d h f -> d (h f)"),
                              start=True, stop=True).then_inc(h_psum, 1)

                def add_up(j):
                    q = turn * U + j
                    if j == 0:
                        pe.wait_ge(same_ready, turn + 2)
                        pe.wait_ge(esc_ready, turn + 1)
                    pe.wait_ge(msg_ready, q + 2)
                    pe.wait_ge(agg_ready, q + 1)
                    a0 = agg[:, (j - 1) % U]
                    for o, m, b in ((pb[6][0:P, :], msg[:, j % 2], a0[:, 0:512]), (pb[7][0:P, 0:HEADS], esc[:, j], a0[:, 512:])):
                        te.matmul(o, same[:, j], m, start=True, stop=False)
                        last = te.matmul(o, carry[:, j], b, start=False, stop=True)
                    last.then_inc(agg_psum, 1)

                def project(j):
                    q = turn * U + j
                    pe.wait_ge(helu_ready, q + 1)
                    if j > 0:
                        pe.wait_ge(xx_ready, q + 1)
                    for c in range(C2):
                        last = te.transpose(pb[0][:, c * P:(c + 1) * P], hex_[:, j % 2, c * 128:(c + 1) * 128], ident[0:P, 0:P])
                    last.then_inc(xx_psum, 1)
                    pe.wait_ge(xx_ready, q + 2)
                    if j > 0:
                        pe.wait_ge(g2_ready, q + U)
                    for c in range(C2):
                        last = te.matmul(pb[1][0:P, 0:D + 2], xx_t[:, c], w2g[:, c], start=(c == 0), stop=(c == C2 - 1))
                    last.then_inc(g2_psum, 1)

                heads(0)
                heads(1)
                add_up(0)
                heads(2)
                add_up(1)
                heads(3)
                project(0)
                add_up(2)
                project(1)
                add_up(3)
                project(2)
                project(3)

            pe.wait_ge(g2_ready, T + U)
            for o, pick in ((0, pick_last), (2, pick_first)):
                te.matmul(pb[2][0:P, o * T:(o + 1) * T], pick[:], s2_all[:], start=True, stop=True)
                last = te.matmul(pb[2][0:P, (o + 1) * T:(o + 2) * T], pick[:], key_pad[:, 0, 1:T + 1], start=True, stop=True)
            last.then_inc(s2_rows, 1)
            pe.wait_ge(s2_ready, 1)

            def add_up_rows(turn, width, round_no):
                pe.wait_ge(same_ready, turn + round_no * TURNS + 2)
                pe.wait_ge(msg_ready, turn + (T + (round_no - 1) * TURNS + 2))
                for j in range(U):
                    pe.wait_ge(agg_ready, turn * U + (round_no * T + j + 1))
                    o = pb[3][0:P, 0:width]
                    te.matmul(o, same[:, j], msg2[:, j, 0:width], start=True, stop=False)
                    te.matmul(o, carry[:, j], agg2[:, (j - 1) % U, 0:width], start=False, stop=True).then_inc(agg_psum, 1)

            with pe.Fori(0, TURNS) as turn:
                key_row(turn + (TURNS + 1))
                add_up_rows(turn, D + 1, 1)

            with pe.Fori(0, TURNS) as turn:
                n = turn + CHUNKS
                turn_hin(n, res[:, 2], c_loaded, turn * 16 + 16)
                hidden(n)
                output(n)

            with pe.Fori(0, TURNS) as turn:
                key_row(turn + (2 * TURNS + 1))
                add_up_rows(turn, D, 2)
                n = turn + (CHUNKS + TURNS)
                turn_hin(n, hin_d, hin_ready, turn + 1)
                hidden(n)
                output(n)

        @block.scalar
        def _(act):
            a = nc.scalar
            a.preload_act_table_set("natural_log_exp_and_others")
            act.sem_inc(hot_t_ready, 1)
            act.sem_inc(run_copied, 1)
            act.sem_inc(hist_open, 1)
            act.sem_inc(found_used, 2)
            act.sem_inc(found_kept, 1)
            act.sem_inc(ranks_done, 1)
            act.sem_inc(hin_t_ready, 1)
            act.sem_inc(hid_ready, 2)
            act.sem_inc(y_sum, 1)
            act.sem_inc(out_free, 4)
            act.sem_inc(g2_ready, U)
            for used in (xt_ready, xs_free, plain_free, g2_free, x1_free, row_free, same_ready, agg_ready, xx_ready, lr_ready, msg_ready):
                act.sem_inc(used, 1)
            with act.Fori(0, TURNS) as turn:
                for j in range(U):
                    act.wait_ge(hot_t_psum, turn * U + j + 1)
                    act.wait_ge(run_updated, turn * U + j + U - 1)
                    a.copy(hot_t[:, j % 2, :, 0:P], hot_t_ps[0:HH, (j % 2) * 512:(j % 2 + 1) * 512].rearrange(
                        "p (o e) -> p o e", o=4)[:, :, 0:P]).then_inc(hot_t_ready, 1)

            def exp_x(n, xv, k):
                a.activation(xex[:, k], xv, ACT.Exp).then_inc(x_exp, 1)

            def rstd_of(n, mom, r, moments, log, ready, k):
                act.wait_ge(moments, n + 1)
                a.activation(r[:, k], mom[:, k, :, 1], ACT.Ln, bias=ln_eps[0:P, 0:1]).then_inc(log, 1)
                act.wait_ge(log, n + 1)
                a.activation(r[:, k], r[:, k], ACT.Exp, scale=-0.5).then_inc(ready, 1)

            def x_rstd_of(n, k):
                rstd_of(n, moment, rstd, x_moments, x_log, x_rstd, k)

            def y_rstd_of(n, k):
                rstd_of(n, post_moment, post_rstd, y_moments, y_log, y_rstd, k)

            def copy_hin(n, scaled):
                act.wait_ge(hin_turned, n + 1)
                scale = eps1[:, 0:1] if scaled else 1.0
                a.activation(hin_t[:], pb[4][:, 0:U * P], ACT.Copy if not scaled else ACT.Identity, scale=scale).then_inc(hin_t_ready, 1)

            def relus(n):
                for c in range(2):
                    act.wait_ge(hid_psum, n * 2 + c + 1)
                    a.activation(hid[:, c], pb[5 + c][:, 0:U * P], ACT.Relu, bias=b1[:, c:c + 1]).then_inc(hid_ready, 1)

            act.wait_ge(weights_ready, 1)
            for n in range(3):
                act.wait_ge(x_loaded[n], 16)
                exp_x(n, xin[:, n], n)
            x_rstd_of(0, 0)
            x_rstd_of(1, 1)
            copy_hin(0, True)
            with act.Fori(0, CHUNKS // 4 - 1) as turn:
                for k in range(4):
                    n = turn * 4 + k
                    act.wait_ge(x_loaded[(k + 3) % 4], turn * 16 + (32 if k >= 1 else 16))
                    exp_x(n + 3, xin[:, (k + 3) % 4], (k + 3) % 4)
                    relus(n)
                    copy_hin(n + 1, True)
                    x_rstd_of(n + 2, (k + 2) % 4)
                    y_rstd_of(n, k)
            for k in range(4):
                n = CHUNKS - 4 + k
                if k < 1:
                    act.wait_ge(x_loaded[3], 16 * (CHUNKS // 4))
                    exp_x(n + 3, xin[:, 3], 3)
                relus(n)
                if k < 3:
                    copy_hin(n + 1, True)
                if k < 2:
                    x_rstd_of(n + 2, k + 2)
                y_rstd_of(n, k)

            with act.Fori(0, TURNS) as turn:
                for k in range(2):
                    act.wait_ge(x_turned, turn * 2 + k + 1)
                    a.copy(xt[:, k], pb[k][:, 0:U * P]).then_inc(xt_ready, 1)
                act.wait_ge(lr_ready, turn + 2)
                a.activation(esc[:], lr[:], ACT.Exp, scale=-1.0).then_inc(esc_ready, 1)
                exp_x(turn, xd[:], 0)
                x_rstd_of(turn + CHUNKS, 0)

                def copy_agg(j):
                    q = turn * U + j
                    act.wait_ge(agg_psum, q + 1)
                    a.copy(agg[:, j, 0:512], pb[6][0:P, :])
                    a.copy(agg[:, j, 512:], pb[7][0:P, 0:HEADS]).then_inc(agg_ready, 1)

                def exp_h(j):
                    act.wait_ge(hp_ready, turn * U + j + 1)
                    a.activation(hex_[:, j % 2], hp[:, j % 2], ACT.Exp).then_inc(hex_ready, 1)

                def copy_xx(j):
                    act.wait_ge(xx_psum, turn * U + j + 1)
                    a.copy(xx_t[:], pb[0][:, 0:C2 * P].rearrange("p (c e) -> p c e", c=C2)).then_inc(xx_ready, 1)

                def copy_g2(j):
                    q = turn * U + j
                    act.wait_ge(g2_psum, q + 1)
                    if j == 0:
                        act.wait_ge(g2_free, turn + 1)
                    a.copy(s2_all[:, ds(q, 1)], pb[1][0:P, D:D + 1])
                    a.copy(g2s[:, j], pb[1][0:P, 0:D + 2]).then_inc(g2_ready, 1)

                copy_agg(0)
                exp_h(0)
                copy_agg(1)
                copy_xx(0)
                exp_h(1)
                copy_g2(0)
                copy_agg(2)
                copy_xx(1)
                exp_h(2)
                copy_g2(1)
                copy_agg(3)
                copy_xx(2)
                exp_h(3)
                copy_g2(2)
                copy_xx(3)
                copy_g2(3)

            def copy_agg2(turn, width, round_no):
                for j in range(U):
                    act.wait_ge(agg_psum, turn * U + (round_no * T + j + 1))
                    a.copy(agg2[:, j, 0:width], pb[3][0:P, 0:width]).then_inc(agg_ready, 1)

            with act.Fori(0, TURNS) as turn:
                group = turn + (CHUNKS + TURNS)
                act.wait_ge(sc2_ready, turn + 1)
                a.activation(msg2[:, :, D], sc2[:, 0], ACT.Exp, scale=-1.0).then_inc(e2_ready, 1)
                copy_agg2(turn, D + 1, 1)
                act.wait_ge(hp_ready, turn + T + 1)
                exp_x(group, xd[:], 0)
                x_rstd_of(group, 0)

            with act.Fori(0, TURNS) as turn:
                n = turn + CHUNKS
                copy_hin(n, True)
                relus(n)
                y_rstd_of(n, 0)

            with act.Fori(0, TURNS) as turn:
                for j in range(U):
                    act.wait_ge(abe_in[j], turn * 48 + 48)
                a.activation(sqr[:, 1], ra[:], ACT.Square).then_inc(squares, 1)
                a.activation(sqr[:, 2], res[:, 3], ACT.Square).then_inc(squares, 1)
                act.wait_ge(sim_step, turn * 6 + 1)
                a.activation(simt[:, 2:4], simt[:, 0:2], ACT.Ln).then_inc(norm_log, 1)
                act.wait_ge(norm_log, turn + 1)
                a.activation(simt[:, 2:4], simt[:, 2:4], ACT.Exp, scale=0.5).then_inc(norm_ready, 1)
                copy_agg2(turn, D, 2)
                n = turn + (CHUNKS + TURNS)
                copy_hin(n, False)
                relus(n)
                y_rstd_of(n, 0)


_INS = ["x", "src", "dst", "edge_attr_128", "L0_gnn_W1", "L0_gnn_a1", "L0_gnn_W2", "L0_gnn_a2",
        "L1_gnn_W1", "L1_gnn_b1", "L1_gnn_W2", "L1_gnn_b2", "L1_gnn_eps"]


def kernel(**inputs):
    import numpy as _np
    import concourse.bacc as _bacc
    from concourse import mybir as _mybir
    from concourse.bass_utils import run_bass_kernel_spmd as _run

    nc = _bacc.Bacc("TRN2", target_bir_lowering=False, num_devices=1)
    arrays, args = {}, []
    for name in _INS:
        a = _np.ascontiguousarray(inputs[name])
        a = a.reshape(a.shape or (1,))
        arrays[f"in_{name}_dram"] = a
        args.append(nc.dram_tensor(f"in_{name}_dram", a.shape, _mybir.dt.from_np(a.dtype), kind="ExternalInput").ap())
    args.append(nc.dram_tensor("out_0_dram", (50000, 128), _mybir.dt.float32, kind="ExternalOutput").ap())
    build_gnn(nc, *args)
    r = _run(nc, [arrays], core_ids=[0])
    return r.results[0]["out_0_dram"]
```

```python
import math
import concourse.bass as bass
from concourse import mybir
from concourse.alu_op_type import AluOpType as ALU
from contextlib import ExitStack

F32 = mybir.dt.float32
BF16 = mybir.dt.bfloat16
I32 = mybir.dt.int32
ACT = mybir.ActivationFunctionType
AX = mybir.AxisListType
ds = bass.ds


def build_gnn(nc, x, src, dst, edge_attr, W1g, a1g, W2g, a2g, W1m, b1m, W2m, b2m, epsm, out):
    N, D = x.shape
    E = src.shape[0]
    P = 125
    T = E // P
    U = 4
    TURNS = T // U
    LO = 256
    HI = -(-N // LO)
    HH = HI // 2
    assert P * T == E and U * TURNS == T and 2 * HH == HI
    HEADS, _, FH = W1g.shape
    C2 = HEADS * FH // 128
    CHUNKS = N // (P * U)
    assert CHUNKS * P * U == N and CHUNKS % 4 == 0 and FH * HEADS == 512
    NONE = float(E)
    ROUND = float(1.5 * 2 ** 23)

    ctx = ExitStack()
    with ctx:
        def sb(name, shape, dt=F32):
            return ctx.enter_context(nc.sbuf_tensor(name, shape, dt))

        def bank(name, shape, dt=F32):
            return ctx.enter_context(nc.psum_tensor(name, shape, dt))

        def sem(name):
            return ctx.enter_context(nc.semaphore(name))

        def dram(name, shape, dt=F32):
            return nc.dram_tensor(name, shape, dt, kind="Internal").ap()

        xs_room = sb("xs_room", [128, T * D])
        xs_all = xs_room[0:P, :]
        room = {"early": 0, "late": 0}

        def carve(when, rows, *shape):
            size = math.prod(shape)
            at = room[when]
            room[when] = at + size
            assert at + size <= T * D
            flat = xs_room[0:rows, at:at + size]
            names = "abcd"[:len(shape)]
            return flat.rearrange(f"p ({' '.join(names)}) -> p {' '.join(names)}", **dict(zip(names, shape))) if len(shape) > 1 else flat

        def early(rows, *shape):
            return carve("early", rows, *shape)

        def late(rows, *shape):
            return carve("late", rows, *shape)

        ident = sb("ident", [128, 128])
        ident16 = sb("ident16", [128, 128], BF16)
        above = sb("above", [128, 128])
        ones = sb("ones", [128, 512])
        digits = sb("digits", [P, LO], BF16)
        slot_no = sb("slot_no", [P, T])
        edge_no = sb("edge_no", [P, T])

        key_i = sb("key_i", [P, 2, T], I32)
        digit_i = sb("digit_i", [P, 2, 2, T], I32)
        key = sb("key", [P, 2, T])
        digit = sb("digit", [P, 2, 2, T])

        meta_src = [dram(f"meta_src_{k}", (E, 4)) for k in range(2)]
        meta_dst = [dram(f"meta_dst_{k}", (E, 4)) for k in range(2)]

        pb = [bank(f"pb{k}", [128, 512]) for k in range(8)]

        consts_ready = sem("consts_ready")
        pool_step = sem("pool_step")
        pool_go = sem("pool_go")
        keys_loaded = sem("keys_loaded")
        digits_int = sem("digits_int")
        digits_ready = sem("digits_ready")

        hot = sb("hot", [P, 2, U, 2, HI + LO], BF16)
        count_hot_ready = sem("count_hot_ready")
        count_hot_used = sem("count_hot_used")
        degrees_ready = sem("degrees_ready")
        hist_open = sem("hist_open")
        deg = early(HH, 2, 2, LO)
        cum = early(HH, 2, 2, LO)
        rowsum = sb("rowsum", [HH, 2, 2])
        base = sb("base", [HH, 2, 2])
        start_tab = early(HH, 2, 2, LO)
        end_tab = early(HH, 2, LO)
        ends_tmp = early(HH, 2, 2, LO)
        table_step = sem("table_step")
        bases_ready = sem("bases_ready")
        tables_ready = sem("tables_ready")

        hot_ready = sem("hot_ready")
        hot_t_psum = sem("hot_t_psum")
        hot_t_ready = sem("hot_t_ready")
        counted = sem("counted")
        run_updated = sem("run_updated")
        run_cast = sem("run_cast")
        run_split = sem("run_split")
        rows_ready = sem("rows_ready")
        ranks_done = sem("ranks_done")
        end_found = sem("end_found")
        end_used = sem("end_used")
        run_found = sem("run_found")
        run_used = sem("run_used")
        found_kept = sem("found_kept")
        run16 = early(HH, 2 * 4 * LO).bitcast(BF16).rearrange("p (w d k h l) -> p w d k h l", w=2, d=2, k=2, h=2)
        end16 = early(HH, 2 * LO).bitcast(BF16).rearrange("p (d h l) -> p d h l", d=2, h=2)
        key16 = sb("key16", [P, 2, 2, T], BF16)
        hot_t = sb("hot_t", [HH, U, 4, 128], BF16)
        found = sb("found", [P, U, 6])
        keep = sb("keep", [P, T, 6])
        before = sb("before", [P, U * P])
        junk = sb("junk", [P, 2, 4, LO], BF16)
        junk2 = early(P, U * P * 2).bitcast(BF16).rearrange("p (w k e) -> p w k e", w=2, k=2)

        pos = sb("pos", [P, 2, T])
        q = sb("q", [P, 2, T])
        addr_i = sb("addr_i", [P, 2, T], I32)
        rowdata = early(P, 2, T, 4)
        bulk_step = sem("bulk_step")
        rows_to_move = sem("rows_to_move")
        zero = sb("zero", [P, 4 * T])
        meta_zeroed = sem("meta_zeroed")
        SC = 10
        move_idx = sb("move_idx", [P, 2, SC], I32)
        move_row = sb("move_row", [P, 2, SC, 4])
        move_slots = sem("move_slots")
        moved = [[sem(f"moved_{k}{h}") for h in range(2)] for k in range(2)]
        meta_in = early(P, 2, 2, T, 4)
        meta = sb("meta", [P, 2, T, 4])
        meta_loaded = sem("meta_loaded")
        meta_ready = sem("meta_ready")

        w1g = sb("w1g", [D, HEADS, FH])
        w2g = sb("w2g", [128, C2, D + 2])
        wa = sb("wa", [D, 2, HEADS])
        wa_tmp = early(D, 2, HEADS, FH)
        a1b = sb("a1b", [D, HEADS, 2 * FH])
        a2b = sb("a2b", [128, 2 * D])
        w2_tmp = early(128, 2, C2, D)
        w1m = sb("w1m", [D, 2, 128])
        w2m = sb("w2m", [128, 2, D])
        b1 = sb("b1", [128, 2])
        b2 = sb("b2", [3, D])
        b2_rest = sb("b2_rest", [3, 3, D])
        b2_part = sb("b2_part", [3, 3, D], BF16)
        b2_parts = sb("b2_parts", [3, D], BF16)
        ones16 = sb("ones16", [3, P], BF16)
        eps1 = sb("eps1", [128, 1])
        ln_eps = sb("ln_eps", [128, 1])
        weights_loaded = sem("weights_loaded")
        weights_step = sem("weights_step")
        weights_ready = sem("weights_ready")

        g2 = dram("g2", (E + 1, D + 2))
        x1_rows = dram("x1_rows", (2 * E, D))
        zero_row_stored = sem("zero_row_stored")

        xin = sb("xin", [P, 4, U, D])
        xex = sb("xex", [P, 4, U, D])
        res = sb("res", [P, 4, U, D])
        hin_t = sb("hin_t", [D, U * P])
        hid = sb("hid", [128, 2, 2, U * P])
        post_sum = sb("post_sum", [P, 2, U, D])
        outb = sb("outb", [P, 4, U, D])
        stats = sb("stats", [P, 4, U, 6])
        moment = sb("moment", [P, 4, U, 2])
        rstd = sb("rstd", [P, 4, U])
        post_bias = sb("post_bias", [P, 4, U])
        post_stat = sb("post_stat", [P, 4, U, 6])
        post_moment = sb("post_moment", [P, 4, U, 2])
        post_rstd = sb("post_rstd", [P, 4, U])
        x_loaded = [sem(f"x_loaded_{k}") for k in range(4)]
        out_stored = [sem(f"out_stored_{k}") for k in range(4)]
        x_exp = sem("x_exp")
        x_half = sem("x_half")
        x_plus_elu = sem("x_plus_elu")
        x_stats = sem("x_stats")
        x_moments = sem("x_moments")
        x_log = sem("x_log")
        x_rstd = sem("x_rstd")
        y_bias = sem("y_bias")
        x1_ready = sem("x1_ready")
        hin_turned = sem("hin_turned")
        hin_t_ready = sem("hin_t_ready")
        hid_psum = sem("hid_psum")
        hid_ready = sem("hid_ready")
        y_psum = sem("y_psum")
        y_sum = sem("y_sum")
        y_stats = sem("y_stats")
        y_moments = sem("y_moments")
        y_log = sem("y_log")
        y_rstd = sem("y_rstd")
        y_out = sem("y_out")

        key_pad = sb("key_pad", [P, 2, T + 2])
        meta_i = sb("meta_i", [P, 2, T, 4], I32)
        next_key = sb("next_key", [P, 2, T])
        out_row = sb("out_row", [P, 2, T], I32)
        shift = sb("shift", [P, P])
        wrap = sb("wrap", [P, P])
        pick_last = sb("pick_last", [P, P])
        pick_first = sb("pick_first", [P, P])
        lists_step = sem("lists_step")
        next_psum = sem("next_psum")
        lists_ready = sem("lists_ready")

        slots_a = sb("slots_a", [P, 2, U, 2], I32)
        xs = xin[:, 0:2]
        xd = xin[:, 2:4]
        h2 = sb("h2", [P, U, D])
        xt = sb("xt", [D, 2, U * P])
        lr = sb("lr", [P, U, HEADS])
        key_now = sb("key_now", [P, U + 1])
        key_now_ready = sem("key_now_ready")
        dve_go = sem("dve_go")
        same = sb("same", [P, U, P])
        carry = sb("carry", [P, U, P])
        msg = sb("msg", [P, 2, HEADS * FH])
        esc = sb("esc", [P, U, HEADS])
        agg = sb("agg", [P, U, HEADS * FH + HEADS])
        hp = sb("hp", [P, 2, HEADS * FH])
        hex_ = sb("hex_", [P, 2, HEADS * FH])
        rsum = sb("rsum", [P, U, HEADS])
        xx_t = sb("xx_t", [128, C2, P])
        g2s = sb("g2s", [P, U, D + 2])
        s2_all = sb("s2_all", [P, T])
        aslots_ready = sem("aslots_ready")
        x_in = [sem(f"x_in_{k}") for k in range(2)]
        x_turned = sem("x_turned")
        xt_ready = sem("xt_ready")
        key_rows = sem("key_rows")
        scores_psum = sem("scores_psum")
        lr_half = sem("lr_half")
        lr_ready = sem("lr_ready")
        esc_ready = sem("esc_ready")
        same_ready = sem("same_ready")
        h_psum = sem("h_psum")
        msg_ready = sem("msg_ready")
        agg_psum = sem("agg_psum")
        agg_ready = sem("agg_ready")
        rsum_step = sem("rsum_step")
        rsum_ready = sem("rsum_ready")
        hp_ready = sem("hp_ready")
        hex_ready = sem("hex_ready")
        helu_half = sem("helu_half")
        helu_ready = sem("helu_ready")
        xx_psum = sem("xx_psum")
        xx_ready = sem("xx_ready")
        g2_psum = sem("g2_psum")
        g2_ready = sem("g2_ready")
        g2_stored = sem("g2_stored")
        xs_kept = sem("xs_kept")
        pe_x_stored = sem("pe_x_stored")

        s2_rows = sem("s2_rows")
        s2_step = sem("s2_step")
        s2_ready = sem("s2_ready")
        ends2 = sb("ends2", [P, 2, 2, T + 1])
        cont = sb("cont", [P, T])
        cover = sb("cover", [P, T])
        tail = sb("tail", [P, T])
        after = sb("after", [P, T])
        s2_src = sb("s2_src", [P, T])
        slots_b = sb("slots_b", [P, 2, U], I32)
        g = agg[:].rearrange("p u f -> p (u f)")[:, 0:2 * U * (D + 2)].rearrange("p (w u f) -> p w u f", w=2, u=U)
        sc2 = sb("sc2", [P, 2, U])
        msg2 = sb("msg2", [P, U, D + 1])
        agg2 = sb("agg2", [P, U, D + 1])
        rs2 = sb("rs2", [P, 2, U])
        g_in = [sem(f"g_in_{k}") for k in range(2)]
        bslots_ready = sem("bslots_ready")
        sc2_a = sem("sc2_a")
        sc2_b = sem("sc2_b")
        sc2_ready = sem("sc2_ready")
        e2_ready = sem("e2_ready")
        x1_stored = sem("x1_stored")

        slots_c = sb("slots_c", [P, U], I32)
        slots_d = sb("slots_d", [P, 2, U, 3], I32)
        cslots_ready = sem("cslots_ready")
        dslots_ready = sem("dslots_ready")
        row_out = sem("row_out")
        ra = late(P, 2, U, D)
        ea = late(P, 2, U, D)
        sqr = late(P, 3, U, D)
        dots = sb("dots", [P, 3, U])
        simt = sb("simt", [P, 4, U])
        hin_d = late(P, U, D)
        ae_in = [sem(f"ae_in_{k}") for k in range(2)]
        b_in = [sem(f"b_in_{k}") for k in range(2)]
        squares = sem("squares")
        dots_ready = sem("dots_ready")
        norm_log = sem("norm_log")
        norm_ready = sem("norm_ready")
        sim_step = sem("sim_step")
        relu_step = sem("relu_step")
        hin_ready = sem("hin_ready")
        xs_free = sem("xs_free")
        plain_free = sem("plain_free")
        g2_free = sem("g2_free")
        x1_free = sem("x1_free")
        row_free = sem("row_free")
        out_free = sem("out_free")

        hot_t_ps = pb[2][:].bitcast(BF16)

        def pipelined(engine, step):
            step(0, 0, 0)
            with engine.Fori(0, TURNS // 2) as pair:
                for half in range(2):
                    step(pair * 2 + (1 + half), 1 - half, pair + half)

        def ahead(engine, first, step):
            first(0, 0, 0)
            with engine.Fori(0, TURNS // 2) as pair:
                for half in range(2):
                    step(pair * 2 + half, 1 - half, pair + half)
            step(TURNS - 1, None, None)

        def each_group(engine, step):
            for k in range(4):
                step(k, k, 0)
            with engine.Fori(0, CHUNKS // 4 - 3) as use:
                for k in range(4):
                    step(use * 4 + (4 + k), k, use + 1)
            for n in range(CHUNKS - 8, CHUNKS):
                step(n, n % 4, n // 4)

        def there(group, ahead_by):
            return not isinstance(group, int) or 0 <= group + ahead_by < CHUNKS

        block = ctx.enter_context(nc.Block())

        @block.sync
        def _(sp):
            sp.dma_start(key_i[:, 0], src.rearrange("(p t) -> p t", t=T)).then_inc(keys_loaded, 16)
            sp.dma_start(key_i[:, 1], dst.rearrange("(p t) -> p t", t=T)).then_inc(keys_loaded, 16)
            sp.wait_ge(consts_ready, 1)
            for tab in meta_src + meta_dst:
                sp.dma_start(tab.rearrange("(p t) c -> p (t c)", p=P), zero[:]).then_inc(meta_zeroed, 16)
            sp.dma_start(w1g[:], W1g.rearrange("h d f -> d h f")).then_inc(weights_loaded, 16)
            sp.dma_start(a1b[:].rearrange("p h f -> p (h f)"), a1g.rearrange("h f -> (h f)").partition_broadcast(D)).then_inc(weights_loaded, 16)
            sp.dma_start(w2g[:, :, 0:D], W2g.rearrange("(c p) f -> p c f", p=128)).then_inc(weights_loaded, 16)
            sp.dma_start(a2b[:], a2g.partition_broadcast(128)).then_inc(weights_loaded, 16)
            sp.dma_start(w1m[:], W1m.rearrange("d (c f) -> d c f", c=2)).then_inc(weights_loaded, 16)
            sp.dma_start(w2m[:], W2m.rearrange("(c p) f -> p c f", p=128)).then_inc(weights_loaded, 16)
            sp.dma_start(b1[:], b1m.rearrange("(c p) -> p c", p=128), allow_slow_non_contiguous=True).then_inc(weights_loaded, 16)
            sp.dma_start(b2[:], b2m.partition_broadcast(3)).then_inc(weights_loaded, 16)
            sp.dma_start(eps1[:], epsm.partition_broadcast(128)).then_inc(weights_loaded, 16)
            sp.wait_ge(consts_ready, 1)
            sp.dma_start(g2[E:E + 1, :], zero[0:1, 0:D + 2]).then_inc(zero_row_stored, 16)
            x_chunks = x.rearrange("(n p u) d -> n p (u d)", p=P, u=U)
            out_chunks = out.rearrange("(n p u) d -> n p (u d)", p=P, u=U)

            def chunk(tensor, n):
                return tensor[ds(n, 1)].rearrange("o p f -> (o p) f")

            for k in range(4):
                sp.dma_start(xin[:, k].rearrange("p u d -> p (u d)"), x_chunks[k]).then_inc(x_loaded[k], 16)

            def put_out(n, k):
                sp.wait_ge(y_out, n + 1)
                sp.dma_start(chunk(out_chunks, n), outb[:, k].rearrange("p u d -> p (u d)")).then_inc(out_stored[k], 16)

            def free_out(k, count):
                sp.wait_ge(out_stored[k], count * 16)
                sp.sem_inc(out_free, 1)

            def node_group(n, k, use):
                if there(n, 7):
                    load_x(n + 7, (k + 3) % 4)
                if there(n, -2):
                    put_out(n - 2, (k + 2) % 4)
                if there(n, -3):
                    free_out((k + 1) % 4, use + 1 if k == 3 else use)

            def load_x(n, k):
                sp.wait_ge(x_plus_elu, n - 3)
                sp.dma_start(xin[:, k].rearrange("p u d -> p (u d)"), chunk(x_chunks, n)).then_inc(x_loaded[k], 16)

            for n in range(4, 7):
                load_x(n, n % 4)
            each_group(sp, node_group)
            put_out(CHUNKS - 2, 2)
            put_out(CHUNKS - 1, 3)
            for k in range(1, 4):
                free_out(k, CHUNKS // 4)

            for k, tabs in enumerate((meta_src, meta_dst)):
                for h in range(2):
                    sp.wait_ge(moved[k][h], 16 * T // 2)
            for k, tabs in enumerate((meta_src, meta_dst)):
                for h in range(2):
                    sp.dma_start(meta_in[:, k, h].rearrange("p t c -> p (t c)"),
                                 tabs[h].rearrange("(p t) c -> p (t c)", p=P)).then_inc(meta_loaded, 16)

            def keep_next(turn, k, use):
                sp.wait_ge(x_in[k], use * (32 * U) + 32 * U)
                sp.dma_start(xs_all[:, ds(turn * (U * D), U * D)], xs[:, k].rearrange("p u d -> p (u d)")).then_inc(xs_kept, 16)
                sp.wait_ge(xs_kept, turn * 16 + 16)
                sp.sem_inc(xs_free, 1)
                sp.wait_ge(x1_ready, turn + (CHUNKS + 1))
                sp.dma_start(x1_rows[ds(turn * (U * P) + E, U * P)].rearrange("(u p) d -> p u d", p=P),
                             res[:, 0]).then_inc(pe_x_stored, 16)

            def layer1(turn, k, use):
                if k is not None:
                    keep_next(turn + 1, k, use)
                sp.wait_ge(g2_ready, turn * U + 2 * U)
                sp.dma_start(g2[ds(turn * (U * P), U * P)].rearrange("(u p) d -> p u d", p=P),
                             g2s[:]).then_inc(g2_stored, 16)
                if k is not None:
                    sp.wait_ge(pe_x_stored, turn * 16 + 32)
                    sp.sem_inc(plain_free, 1)
                sp.wait_ge(g2_stored, turn * 16 + 16)
                sp.sem_inc(g2_free, 1)

            keep_next(0, 0, 0)
            sp.wait_ge(pe_x_stored, 16)
            sp.sem_inc(plain_free, 1)
            ahead(sp, lambda turn, k, use: None, layer1)
            def store_x1(turn, k, use):
                sp.wait_ge(x1_ready, turn + (CHUNKS + TURNS + 1))
                sp.dma_start(x1_rows[ds(turn * (U * P), U * P)].rearrange("(u p) d -> p u d", p=P),
                             res[:, 1 + k]).then_inc(x1_stored, 16)
                sp.wait_ge(x1_stored, turn * 16 + 16)
                sp.sem_inc(x1_free, 1)

            pipelined(sp, store_x1)

        @block.gpsimd
        def _(pool):
            gp = nc.gpsimd
            gp.memset(zero[:], 0.0)
            gp.memset(ones[:], 1.0)
            gp.memset(ident[:], 0.0).then_inc(pool_step, 1)
            pool.wait_ge(pool_step, 1)
            gp.affine_select(out=ident[:], in_=ident[:], compare_op=ALU.not_equal, fill=1.0, base=0,
                            pattern=[[-1, 128]], channel_multiplier=1)
            gp.memset(before[:, 0:(U - 1) * P], 1.0)
            gp.affine_select(out=before[:, (U - 1) * P:], in_=ones[0:P, 0:P], compare_op=ALU.is_gt, fill=0.0, base=0,
                            pattern=[[-1, P]], channel_multiplier=1)
            gp.affine_select(out=above[:], in_=ones[:, 0:128], compare_op=ALU.is_gt, fill=0.0, base=0,
                            pattern=[[1, 128]], channel_multiplier=-1)
            gp.affine_select(out=shift[:], in_=ones[0:P, 0:P], compare_op=ALU.is_equal, fill=0.0, base=-1,
                            pattern=[[-1, P]], channel_multiplier=1)
            gp.affine_select(out=wrap[:], in_=ones[0:P, 0:P], compare_op=ALU.is_equal, fill=0.0, base=P - 1,
                            pattern=[[-1, P]], channel_multiplier=P)
            gp.affine_select(out=pick_last[:], in_=ones[0:P, 0:P], compare_op=ALU.is_equal, fill=0.0, base=-(P - 1),
                            pattern=[[0, P]], channel_multiplier=1)
            gp.affine_select(out=pick_first[:], in_=ones[0:P, 0:P], compare_op=ALU.is_equal, fill=0.0, base=0,
                            pattern=[[0, P]], channel_multiplier=1)
            gp.memset(ones16[:], 1.0)
            gp.memset(ln_eps[:], 1e-5)
            gp.memset(ends2[:], -2.0)
            gp.memset(agg[:], 0.0)
            gp.memset(agg2[:], 0.0)
            gp.memset(key_pad[:], -1.0)
            gp.iota(digits[:], [[1, LO]], base=0, channel_multiplier=0, allow_small_or_imprecise_dtypes=True)
            gp.iota(slot_no[:], [[P, T]], base=0, channel_multiplier=1, allow_small_or_imprecise_dtypes=True)
            gp.iota(edge_no[:], [[1, T]], base=0, channel_multiplier=T,
                   allow_small_or_imprecise_dtypes=True).then_inc(pool_step, 1)
            pool.wait_ge(pool_step, 2)
            gp.tensor_copy(ident16[:], ident[:]).then_inc(consts_ready, 1)
            def split_run(count, w):
                pool.wait_ge(run_cast, count)
                gp.tensor_tensor(run16[:, w, 1], start_tab, run16[:, w, 0], ALU.subtract).then_inc(run_split, 1)

            ahead(pool, lambda turn, w, use: split_run(1, w),
                  lambda turn, nxt, use: split_run(turn + 2, nxt) if nxt is not None else None)

            pool.wait_ge(rows_to_move, 1)
            pool.wait_ge(meta_zeroed, 64)
            with pool.Fori(0, T // SC) as turn:
                t0 = turn * SC
                for k in range(2):
                    gp.tensor_copy(move_idx[:, k], addr_i[:, k, ds(t0, SC)])
                    last = gp.tensor_copy(move_row[:, k], rowdata[:, k, ds(t0, SC), :])
                last.then_inc(move_slots, 1)
                pool.wait_ge(move_slots, turn + 1)
                pool.sem_inc(pool_go, 1)
                for j in range(SC):
                    for k, tabs in enumerate((meta_src, meta_dst)):
                        if j >= 2:
                            pool.wait_ge(moved[k][j % 2], turn * (8 * SC) + 16 * (j // 2))
                            pool.sem_inc(pool_go, 1)
                        gp.indirect_dma_start(
                            out=tabs[j % 2], out_offset=bass.IndirectOffsetOnAxis(ap=move_idx[:, k, j:j + 1], axis=0),
                            in_=move_row[:, k, j], in_offset=None).then_inc(moved[k][j % 2], 16)
                for k in range(2):
                    for h in range(2):
                        pool.wait_ge(moved[k][h], turn * (8 * SC) + 8 * SC)
                        pool.sem_inc(pool_go, 1)


            pool.wait_ge(lists_ready, 1)

            def get_x(turn, k, first):
                if not first:
                    pool.wait_ge(xt_ready, turn * 2 - 1)
                    pool.sem_inc(pool_go, 1)
                    pool.wait_ge(x_plus_elu, turn + (CHUNKS - 1))
                    pool.sem_inc(pool_go, 1)
                    pool.wait_ge(xs_free, turn)
                    pool.sem_inc(pool_go, 1)
                gp.tensor_copy(slots_a[:, k], meta_i[:, 0, ds(turn * U, U), 0:2]).then_inc(aslots_ready, 1)
                pool.wait_ge(aslots_ready, turn + 1)
                pool.sem_inc(pool_go, 1)
                for j in range(U):
                    for c, rows in enumerate((xs, xd)):
                        gp.indirect_dma_start(
                            out=rows[:, k, j], out_offset=None, in_=x,
                            in_offset=bass.IndirectOffsetOnAxis(ap=slots_a[:, k, j, c:c + 1], axis=0)).then_inc(x_in[k], 16)

            get_x(0, 0, True)
            get_x(1, 1, True)
            get_x(2, 0, False)
            with pool.Fori(0, TURNS // 2 - 1) as pair:
                for half in range(2):
                    get_x(pair * 2 + (half + 3), 1 - half, False)
            pool.wait_ge(g2_stored, 16 * TURNS)
            pool.sem_inc(pool_go, 1)
            pool.wait_ge(zero_row_stored, 16)
            pool.sem_inc(pool_go, 1)

            def g_slots(turn, k):
                pool.wait_ge(msg_ready, turn + T)
                pool.sem_inc(pool_go, 1)
                gp.tensor_copy(slots_b[:, k], meta_i[:, 0, ds(turn * U, U), 2]).then_inc(bslots_ready, 1)
                pool.wait_ge(bslots_ready, turn + 1)
                pool.sem_inc(pool_go, 1)

            def get_g(k, j):
                gp.indirect_dma_start(
                    out=g[:, k, j], out_offset=None, in_=g2,
                    in_offset=bass.IndirectOffsetOnAxis(ap=slots_b[:, k, j:j + 1], axis=0)).then_inc(g_in[k], 16)

            def out_slots(turn, list_no):
                gp.tensor_copy(slots_c[:], out_row[:, list_no, ds(turn * U, U)]).then_inc(cslots_ready, 1)
                pool.wait_ge(cslots_ready, turn + (TURNS * list_no + 1))
                pool.wait_ge(y_out, turn + (CHUNKS + TURNS * list_no + 1))
                pool.sem_inc(pool_go, 1)

            def put(turn, list_no, k, j, meanwhile):
                gp.indirect_dma_start(
                    out=out, out_offset=bass.IndirectOffsetOnAxis(ap=slots_c[:, j:j + 1], axis=0),
                    in_=outb[:, k, j], in_offset=None, bounds_check=N - 1, oob_is_err=False).then_inc(row_out, 16)
                meanwhile()
                pool.wait_ge(row_out, (turn * U + j) * 16 + (16 * T * list_no + 16))
                pool.sem_inc(row_free, 1)

            for turn in range(3):
                g_slots(turn, turn % 2)
                for j in range(U):
                    get_g(turn % 2, j)
            for k in range(4):
                pool.wait_ge(out_stored[k], 16 * (CHUNKS // 4))
            with pool.Fori(0, TURNS // 2 - 1) as pair:
                for k in range(2):
                    turn = pair * 2 + k
                    g_slots(turn + 3, 1 - k)
                    out_slots(turn, 0)
                    for j in range(U):
                        put(turn, 0, k, j, lambda: get_g(1 - k, j))

            def d_slots(turn, k, first):
                if not first:
                    pool.wait_ge(hin_ready, turn - 1)
                    pool.sem_inc(pool_go, 1)
                gp.tensor_copy(slots_d[:, k], meta_i[:, 1, ds(turn * U, U), 1:4]).then_inc(dslots_ready, 1)
                pool.wait_ge(dslots_ready, turn + 1)
                pool.sem_inc(pool_go, 1)

            def get_d(k, j, what, rows, table, arrived):
                gp.indirect_dma_start(
                    out=rows[:, j], out_offset=None, in_=table,
                    in_offset=bass.IndirectOffsetOnAxis(ap=slots_d[:, k, j, what:what + 1], axis=0)).then_inc(arrived[k], 16)

            def get_ae(k, j):
                get_d(k, j, 0, ra[:, k], x1_rows, ae_in)
                get_d(k, j, 2, ea[:, k], edge_attr, ae_in)

            def get_b(turn, k, first):
                if not first:
                    pool.wait_ge(y_sum, turn + (CHUNKS + TURNS))
                    pool.sem_inc(pool_go, 1)
                for j in range(U):
                    get_d(k, j, 1, res[:, 2 + k], x1_rows, b_in)

            turn = TURNS - 3
            out_slots(turn, 0)
            for j in range(U):
                put(turn, 0, turn % 2, j, lambda: None)
            pool.wait_ge(pe_x_stored, 16 * TURNS)
            pool.sem_inc(pool_go, 1)
            pool.wait_ge(x1_stored, 16 * TURNS)
            pool.sem_inc(pool_go, 1)
            d_slots(0, 0, True)
            for j in range(U):
                get_ae(0, j)
            pool.wait_ge(y_sum, CHUNKS + TURNS)
            pool.sem_inc(pool_go, 1)
            get_b(0, 0, True)
            for turn in range(2):
                d_slots(turn + 1, 1 - turn, turn == 0)
                out_slots(turn + TURNS - 2, 0)
                for j in range(U):
                    put(turn + TURNS - 2, 0, 1 - turn, j, lambda: get_ae(1 - turn, j))
                get_b(turn + 1, 1 - turn, turn == 0)
            with pool.Fori(0, TURNS // 2 - 1) as pair:
                for k in range(2):
                    turn = pair * 2 + k
                    d_slots(turn + 3, 1 - k, False)
                    out_slots(turn, 1)
                    for j in range(U):
                        put(turn, 1, 1 - k, j, lambda: get_ae(1 - k, j))
                    get_b(turn + 3, 1 - k, False)
            for turn in range(TURNS - 3, TURNS):
                out_slots(turn, 1)
                for j in range(U):
                    put(turn, 1, (turn + 1) % 2, j, lambda: None)

        @block.vector
        def _(dve):
            v = nc.vector

            def node_sum(n, xv, ex, u):
                flat = "p u d -> p (u d)"
                xv, ex, u = xv.rearrange(flat), ex.rearrange(flat), u.rearrange(flat)
                dve.wait_ge(x_exp, n + 1)
                v.scalar_tensor_tensor(u, ex, 1.0, xv, ALU.min, ALU.add).then_inc(x_half, 1)
                dve.wait_ge(x_half, n + 1)
                v.scalar_tensor_tensor(u, xv, 0.0, u, ALU.max, ALU.add).then_inc(x_plus_elu, 1)
                dve.wait_ge(x_plus_elu, n + 1)
                node_stats(n, u.rearrange("p (u d) -> p u d", d=D), None)

            def node_stats(n, u, k):
                for j in range(U):
                    last = v.bn_stats(stats[:, 0, j], u[:, j])
                last.then_inc(x_stats, 1)

            def node_moments(n, k):
                dve.wait_ge(x_stats, n + 1)
                dve.sem_inc(dve_go, 1)
                for j in range(U):
                    last = v.bn_aggr(moment[:, k, j], stats[:, 0, j])
                last.then_inc(x_moments, 1)

            def node_x1(n, u, k):
                dve.wait_ge(x_rstd, n + 1)
                for j in range(U):
                    last = v.tensor_scalar(u[:, j], u[:, j], moment[:, k, j, 0:1], rstd[:, k, j:j + 1],
                                           ALU.subtract, ALU.mult)
                last.then_inc(x1_ready, 1)

            def result_sum(n, r, k):
                dve.wait_ge(y_psum, n + 1)
                v.tensor_tensor(post_sum[:, k % 2].rearrange("p u d -> p (u d)"), pb[7][0:P, :], r.rearrange("p u d -> p (u d)"), ALU.add).then_inc(y_sum, 1)
                dve.wait_ge(y_sum, n + 2)
                for j in range(U):
                    last = v.bn_stats(post_stat[:, 0, j], post_sum[:, k % 2, j])
                last.then_inc(y_stats, 1)
                dve.wait_ge(y_stats, n + 1)
                dve.sem_inc(dve_go, 1)
                for j in range(U):
                    last = v.bn_aggr(post_moment[:, k, j], post_stat[:, 0, j])
                last.then_inc(y_moments, 1)

            def result(n, k):
                dve.wait_ge(y_rstd, n + 1)
                for j in range(U):
                    last = v.tensor_scalar(outb[:, k, j], post_sum[:, k % 2, j], post_moment[:, k, j, 0:1],
                                           post_rstd[:, k, j:j + 1], ALU.subtract, ALU.mult)
                last.then_inc(y_out, 1)

            dve.wait_ge(keys_loaded, 32)
            v.tensor_scalar(digit_i[:, :, 0], key_i[:], 8, None, ALU.logical_shift_right)
            v.tensor_scalar(digit_i[:, :, 1], key_i[:], LO - 1, None, ALU.bitwise_and).then_inc(digits_int, 1)
            v.tensor_copy(key[:], key_i[:])
            dve.wait_ge(digits_int, 1)
            v.tensor_copy(digit[:], digit_i[:]).then_inc(digits_ready, 1)
            dve.wait_ge(digits_ready, 1)
            v.tensor_copy(key16[:, 0], key[:]).then_inc(digits_ready, 1)
            dve.wait_ge(digits_ready, 2)
            v.tensor_tensor(key16[:, 1], key[:], key16[:, 0], ALU.subtract).then_inc(digits_ready, 1)
            dve.wait_ge(consts_ready, 1)

            def one_hots(turn, j, k, w):
                t = turn * U + j
                v.tensor_scalar(hot[:, w, j, k, 0:HI], digits[:, 0:HI], digit[:, k, 0, ds(t, 1)], None, ALU.is_equal)
                return v.tensor_scalar(hot[:, w, j, k, HI:], digits[:], digit[:, k, 1, ds(t, 1)], None, ALU.is_equal)

            with dve.Fori(0, TURNS) as turn:
                for j in range(U):
                    dve.wait_ge(count_hot_used, turn * U + j + 1)
                    for k in range(2):
                        last = one_hots(turn, j, k, 0)
                    last.then_inc(count_hot_ready, 1)
            dve.wait_ge(degrees_ready, 1)
            for k in range(2):
                last = v.tensor_copy(deg[:, k].rearrange("p h l -> p (h l)"), pb[k][0:HH, :])
            last.then_inc(table_step, 1)
            dve.wait_ge(table_step, 1)
            for k in range(2):
                for h in range(2):
                    last = v.tensor_tensor_scan(cum[:, k, h], ones[0:HH, 0:LO], deg[:, k, h], 0.0, ALU.mult, ALU.add)
            last.then_inc(table_step, 1)
            dve.wait_ge(table_step, 2)
            v.tensor_copy(rowsum[:], cum[:, :, :, LO - 1]).then_inc(table_step, 1)
            dve.wait_ge(bases_ready, 1)
            v.tensor_copy(base[:], pb[2][0:HH, 0:4].rearrange("p (k h) -> p k h", k=2)).then_inc(table_step, 1)
            dve.wait_ge(table_step, 4)
            v.tensor_tensor(base[:, :, 1], base[:, :, 1], pb[2][0:HH, 4:6], ALU.add).then_inc(table_step, 1)
            dve.wait_ge(table_step, 5)
            for k in range(2):
                for h in range(2):
                    last = v.tensor_scalar(cum[:, k, h], cum[:, k, h], base[:, k, h:h + 1], None, ALU.add)
            last.then_inc(table_step, 1)
            dve.wait_ge(table_step, 6)
            v.tensor_tensor(start_tab[:], cum[:], deg[:], ALU.subtract)
            v.tensor_scalar(ends_tmp[:, 0], cum[:, 0], -1.0 - NONE, None, ALU.add)
            v.tensor_scalar(ends_tmp[:, 1], deg[:, 0], 0.0, None, ALU.is_gt).then_inc(table_step, 1)
            dve.wait_ge(table_step, 7)
            v.tensor_tensor(ends_tmp[:, 0], ends_tmp[:, 0], ends_tmp[:, 1], ALU.mult).then_inc(table_step, 1)
            dve.wait_ge(table_step, 8)
            v.tensor_scalar(end_tab[:], ends_tmp[:, 0], NONE, None, ALU.add).then_inc(table_step, 1)
            dve.wait_ge(table_step, 9)
            v.tensor_copy(end16[:, 0], end_tab[:]).then_inc(table_step, 1)
            dve.wait_ge(table_step, 10)
            v.tensor_tensor(end16[:, 1], end_tab[:], end16[:, 0], ALU.subtract).then_inc(tables_ready, 1)

            def all_hots(turn, w):
                for j in range(U):
                    for k in range(2):
                        last = one_hots(turn, j, k, w)
                last.then_inc(hot_ready, 1)

            def places(turn, nxt, use):
                w = 0 if nxt is None else 1 - nxt
                dve.wait_ge(counted, turn + 1)
                dve.wait_ge(run_split, turn + 1)
                for k in range(2):
                    run = start_tab[:, k].rearrange("p h l -> p (h l)")
                    last = v.tensor_tensor(run, pb[k][0:HH, :], run, ALU.add)
                last.then_inc(run_updated, 1)
                if nxt is not None:
                    all_hots(turn + 1, nxt)
                dve.wait_ge(rows_ready, turn + 1)
                dve.wait_ge(found_kept, turn + 1)
                for j in range(U):
                    dve.wait_ge(ranks_done, turn * U + (j + 1))
                    for k in range(2):
                        last = v.scalar_tensor_tensor(junk2[:, j % 2, k, 0:(j + 1) * P], pb[3 + k][0:P, 0:(j + 1) * P],
                                                      key[:, k, ds(turn * U + j, 1)], before[:, (U - 1 - j) * P:],
                                                      ALU.is_equal, ALU.mult, accum_out=found[:, j, 4 + k:5 + k])
                    last.then_inc(ranks_done, 1)
                for j in range(U):
                    dve.wait_ge(run_used, turn * U + (j + 1))
                    dve.wait_ge(end_found, turn * U + (j + 1))
                    for c in (2, 3, 0, 1):
                        if c == 0:
                            last.then_inc(end_used, 1)
                            dve.wait_ge(run_found, turn * U + (j + 1))
                        tab = (pb[7] if c >= 2 else pb[5 + j % 2])[0:P, (c % 2) * LO:(c % 2 + 1) * LO]
                        last = v.tensor_tensor_reduce(out=junk[:, j % 2, c], in0=tab, in1=hot[:, w, j, c % 2, HI:], scale=1.0,
                                                      scalar=0.0, op0=ALU.mult, op1=ALU.add,
                                                      accum_out=found[:, j, c:c + 1])
                    last.then_inc(run_used, 1)
                dve.wait_ge(run_used, turn * U + (U + 2))
                v.tensor_copy(keep[:, ds(turn * U, U), :], found[:]).then_inc(found_kept, 1)

            dve.wait_ge(count_hot_used, T + U)
            ahead(dve, lambda turn, w, use: all_hots(turn, w), places)

            dve.wait_ge(found_kept, TURNS + 1)

            def step(ins, n):
                ins.then_inc(bulk_step, 1)
                dve.wait_ge(bulk_step, n)

            for k in range(2):
                last = v.tensor_tensor(pos[:, k], keep[:, :, k], keep[:, :, 4 + k], ALU.add)
            step(last, 1)
            step(v.tensor_scalar(q[:], pos[:], -float(P // 2), 1.0 / P, ALU.add, ALU.mult), 2)
            step(v.tensor_scalar(q[:], q[:], ROUND, None, ALU.add), 3)
            step(v.tensor_scalar(q[:], q[:], ROUND, None, ALU.subtract), 4)
            step(v.tensor_scalar(q[:], q[:], -(P * T - 1.0), None, ALU.mult), 5)
            step(v.scalar_tensor_tensor(q[:], pos[:], float(T), q[:], ALU.mult, ALU.add), 6)
            v.tensor_copy(addr_i[:], q[:])
            v.tensor_copy(rowdata[:, 0, :, 0], key[:, 0])
            v.tensor_copy(rowdata[:, 0, :, 1], key[:, 1])
            v.tensor_copy(rowdata[:, 0, :, 2], keep[:, :, 3])
            v.tensor_copy(rowdata[:, 0, :, 3], keep[:, :, 2])
            v.tensor_copy(rowdata[:, 1, :, 0], key[:, 1])
            v.tensor_copy(rowdata[:, 1, :, 1], keep[:, :, 2])
            v.tensor_copy(rowdata[:, 1, :, 3], edge_no[:])
            step(v.scalar_tensor_tensor(rowdata[:, 1, :, 2], keep[:, :, 3], NONE, pos[:, 0],
                                        ALU.is_equal, ALU.mult), 7)
            v.tensor_tensor(rowdata[:, 1, :, 2], rowdata[:, 1, :, 2], keep[:, :, 3], ALU.add).then_inc(rows_to_move, 1)

            dve.wait_ge(weights_loaded, 9 * 16)
            for k in range(2):
                v.tensor_tensor(wa_tmp[:, k], w1g[:], a1b[:, :, k * FH:(k + 1) * FH], ALU.mult)
                last = v.tensor_tensor(w2_tmp[:, k], w2g[:, :, 0:D],
                                       a2b[:, k * D:(k + 1) * D].unsqueeze(1).broadcast_to([128, C2, D]), ALU.mult)
            v.tensor_scalar(eps1[:], eps1[:], 1.0, None, ALU.add).then_inc(weights_step, 1)
            dve.wait_ge(weights_step, 1)
            for k in range(2):
                v.tensor_reduce(wa[:, k], wa_tmp[:, k], AX.X, ALU.add)
                last = v.tensor_reduce(w2g[:, :, D + k], w2_tmp[:, k], AX.X, ALU.add)

            def part_step(ins, n):
                ins.then_inc(weights_step, 1)
                dve.wait_ge(weights_step, n)

            part_step(v.tensor_copy(b2_part[:, 0], b2[:]), 2)
            part_step(v.tensor_tensor(b2_rest[:, 0], b2[:], b2_part[:, 0], ALU.subtract), 3)
            part_step(v.tensor_copy(b2_part[:, 1], b2_rest[:, 0]), 4)
            part_step(v.tensor_tensor(b2_rest[:, 1], b2_rest[:, 0], b2_part[:, 1], ALU.subtract), 5)
            part_step(v.tensor_scalar(b2_rest[:, 2], b2_part[:, 0], ident[0:3, 0:1], None, ALU.mult), 6)
            part_step(v.scalar_tensor_tensor(b2_rest[:, 2], b2_part[:, 1], ident[0:3, 1:2], b2_rest[:, 2], ALU.mult, ALU.add), 7)
            v.scalar_tensor_tensor(b2_parts[:], b2_rest[:, 1], ident[0:3, 2:3], b2_rest[:, 2], ALU.mult, ALU.add).then_inc(weights_ready, 1)

            def y_bias_of(n, k):
                dve.wait_ge(y_rstd, n + 1)
                v.scalar_tensor_tensor(post_bias[:, k], post_moment[:, k, :, 0], -1.0, post_rstd[:, k],
                                       ALU.mult, ALU.mult).then_inc(y_bias, 1)

            def x_sum(n, k):
                node_sum(n, xin[:, k], xex[:, k], res[:, k])
                node_moments(n, k)

            def node_group(n, k, use):
                if there(n, -1):
                    y_bias_of(n - 1, (k + 3) % 4)
                if there(n, -2):
                    dve.wait_ge(y_out, n - 1)
                result_sum(n, res[:, k], k)
                if there(n, 3):
                    node_x1(n + 3, res[:, (k + 3) % 4], (k + 3) % 4)
                if there(n, 4):
                    x_sum(n + 4, k)

            for n in range(4):
                x_sum(n, n)
                if n < 3:
                    node_x1(n, res[:, n], n)
            each_group(dve, node_group)
            y_bias_of(CHUNKS - 1, 3)
            dve.wait_ge(meta_loaded, 64)
            v.tensor_tensor(meta[:], meta_in[:, :, 0], meta_in[:, :, 1], ALU.add).then_inc(meta_ready, 1)
            dve.wait_ge(meta_ready, 1)

            step(v.tensor_copy(key_pad[:, :, 1:T + 1], meta[:, :, :, 0]), 8)
            step(v.tensor_copy(meta_i[:], meta[:]), 9)
            dve.wait_ge(next_psum, 1)
            step(v.tensor_tensor(next_key[:], pb[2][0:P, 0:2 * T].rearrange("p (k t) -> p k t", k=2),
                                 key_pad[:, :, 1:T + 1], ALU.is_equal), 10)
            step(v.scalar_tensor_tensor(next_key[:], next_key[:], float(4 * N), key_pad[:, :, 1:T + 1],
                                        ALU.mult, ALU.add), 11)
            v.tensor_copy(out_row[:], next_key[:]).then_inc(lists_ready, 1)

            def same_keys(turn, list_no, rows, count):
                v.tensor_copy(key_now[:], key_pad[:, list_no, ds(turn * U, U + 1)]).then_inc(key_now_ready, 1)
                dve.wait_ge(key_now_ready, count)
                dve.wait_ge(key_rows, count)
                for j in range(U):
                    row = rows[0:P, j * P:(j + 1) * P]
                    v.tensor_scalar(same[:, j], row, key_now[:, j + 1:j + 2], None, ALU.is_equal)
                    last = v.tensor_scalar(carry[:, j], row, key_now[:, j:j + 1], pick_last[:, 0:1],
                                           ALU.is_equal, ALU.mult)
                last.then_inc(same_ready, 1)

            def message(turn, j):
                dve.wait_ge(esc_ready, turn + 1)
                dve.wait_ge(h_psum, turn * U + (j + 1))
                v.tensor_tensor(msg[:, j % 2].rearrange("p (h f) -> p h f", h=HEADS),
                                pb[4 + j % 2][0:P, :].rearrange("p (h f) -> p h f", h=HEADS),
                                esc[:, j].unsqueeze(2).broadcast_to([P, HEADS, FH]), ALU.mult).then_inc(msg_ready, 1)

            def mean(turn, j):
                dve.wait_ge(agg_ready, turn * U + (j + 2))
                v.tensor_scalar(rsum[:, j], agg[:, j, HEADS * FH:], 1e-16, None, ALU.add).then_inc(rsum_step, 1)
                dve.wait_ge(rsum_step, turn * U + (j + 1))
                v.reciprocal(rsum[:, j], rsum[:, j]).then_inc(rsum_ready, 1)
                dve.wait_ge(rsum_ready, turn * U + (j + 1))
                v.tensor_tensor(hp[:, j % 2].rearrange("p (h f) -> p h f", h=HEADS),
                                agg[:, j, 0:HEADS * FH].rearrange("p (h f) -> p h f", h=HEADS),
                                rsum[:, j].unsqueeze(2).broadcast_to([P, HEADS, FH]), ALU.mult).then_inc(hp_ready, 1)

            def elu(turn, j):
                dve.wait_ge(hex_ready, turn * U + (j + 1))
                v.tensor_scalar(hex_[:, j % 2], hex_[:, j % 2], 1.0, -1.0, ALU.min, ALU.add).then_inc(helu_half, 1)
                dve.wait_ge(helu_half, turn * U + (j + 1))
                v.scalar_tensor_tensor(hex_[:, j % 2], hp[:, j % 2], 0.0, hex_[:, j % 2], ALU.max, ALU.add).then_inc(helu_ready, 1)

            def scores_of(turn):
                dve.wait_ge(scores_psum, turn + 1)
                scores = pb[3][0:P, 256:256 + U * HEADS]
                flat = lr[:].rearrange("p u h -> p (u h)")
                v.tensor_scalar(flat, scores, 0.2, None, ALU.mult).then_inc(lr_half, 1)
                dve.wait_ge(lr_half, turn + 1)
                v.tensor_tensor(flat, flat, scores, ALU.max).then_inc(lr_ready, 1)

            def plain_sum(turn, k):
                dve.wait_ge(plain_free, turn + 1)
                node_sum(turn + CHUNKS, xd[:, k], xex[:, 0], res[:, 0])
                node_moments(turn + CHUNKS, 0)

            def layer1_first(turn, k, use):
                same_keys(turn, 0, pb[2], turn + 1)
                scores_of(turn)
                plain_sum(turn, k)
                message(turn, 0)
                message(turn, 1)
                node_x1(turn + CHUNKS, res[:, 0], 0)

            def layer1(turn, k, use):
                mean(turn, 0)
                message(turn, 2)
                mean(turn, 1)
                elu(turn, 0)
                message(turn, 3)
                elu(turn, 1)
                mean(turn, 2)
                elu(turn, 2)
                mean(turn, 3)
                if k is None:
                    elu(turn, 3)
                    return
                same_keys(turn + 1, 0, pb[2], turn + 2)
                scores_of(turn + 1)
                elu(turn, 3)
                message(turn + 1, 0)
                plain_sum(turn + 1, k)
                message(turn + 1, 1)
                node_x1(turn + (CHUNKS + 1), res[:, 0], 0)

            ahead(dve, layer1_first, layer1)

            dve.wait_ge(s2_rows, 1)
            v.tensor_copy(ends2[:, 0, :, 0:T], pb[2][0:P, 0:2 * T].rearrange("p (k t) -> p k t", k=2))
            v.tensor_copy(ends2[:, 1, :, 0:T], pb[2][0:P, 2 * T:4 * T].rearrange("p (k t) -> p k t", k=2)).then_inc(s2_step, 1)
            dve.wait_ge(s2_step, 1)

            def s2_do(ins, n):
                ins.then_inc(s2_step, 1)
                dve.wait_ge(s2_step, n)

            v.tensor_tensor(cont[:], ends2[:, 0, 1, 0:T], ends2[:, 1, 1, 1:T + 1], ALU.is_equal)
            v.tensor_tensor(cover[:], ends2[:, 0, 1, 0:T], ends2[:, 0, 1, 1:T + 1], ALU.is_equal)
            s2_do(v.tensor_tensor(tail[:], ends2[:, 1, 0, 1:T + 1], ends2[:, 0, 0, 0:T], ALU.subtract), 2)
            s2_do(v.tensor_tensor(tail[:], tail[:], cont[:], ALU.mult), 3)
            s2_do(v.tensor_tensor(tail[:], tail[:], ends2[:, 0, 0, 0:T], ALU.add), 4)
            s2_do(v.tensor_scalar(cont[:], cover[:], -1.0, 1.0, ALU.mult, ALU.add), 5)
            s2_do(v.tensor_tensor(tail[:], tail[:], cont[:], ALU.mult), 6)
            v.tensor_copy(cont[:], cover[:, ::-1])
            s2_do(v.tensor_copy(ends2[:, 1, 0, 0:T], tail[:, ::-1]), 7)
            s2_do(v.tensor_tensor_scan(after[:], cont[:], ends2[:, 1, 0, 0:T], 0.0, ALU.mult, ALU.add), 8)
            s2_do(v.tensor_tensor(tail[:], after[:, ::-1], s2_all[:], ALU.subtract), 9)
            s2_do(v.tensor_tensor(cont[:], key_pad[:, 0, 1:T + 1], ends2[:, 0, 1, 0:T], ALU.is_equal), 10)
            s2_do(v.tensor_tensor(tail[:], tail[:], cont[:], ALU.mult), 11)
            v.tensor_tensor(s2_src[:], tail[:], s2_all[:], ALU.add).then_inc(s2_ready, 1)
            dve.wait_ge(s2_ready, 1)

            def old_sum(turn, list_no, k, r):
                dve.wait_ge(y_out, turn + (CHUNKS + TURNS * list_no))
                result_sum(turn + (CHUNKS + TURNS * list_no), r, k)

            def old_result(turn, list_no, k):
                dve.wait_ge(row_free, turn * U + (T * list_no + 1))
                result(turn + (CHUNKS + TURNS * list_no), k)

            def layer2(turn, k, use):
                group = turn + (CHUNKS + TURNS)
                old = not isinstance(turn, int)
                same_keys(turn, 0, pb[2], turn + (TURNS + 1))
                dve.wait_ge(g_in[k], use * (16 * U) + 16 * U)
                v.tensor_tensor(sc2[:, 0], g[:, k, :, D + 1], s2_src[:, ds(turn * U, U)], ALU.add).then_inc(sc2_a, 1)
                dve.wait_ge(sc2_a, turn + 1)
                v.tensor_scalar(sc2[:, 1], sc2[:, 0], 0.2, None, ALU.mult).then_inc(sc2_b, 1)
                dve.wait_ge(sc2_b, turn + 1)
                v.tensor_tensor(sc2[:, 0], sc2[:, 0], sc2[:, 1], ALU.max).then_inc(sc2_ready, 1)
                dve.wait_ge(e2_ready, turn + 1)
                for j in range(U):
                    last = v.tensor_scalar(msg2[:, j, 0:D], g[:, k, j, 0:D], msg2[:, j, D:D + 1], None, ALU.mult)
                last.then_inc(msg_ready, 1)
                if old:
                    old_sum(turn - 1, 0, 1 - k, res[:, 2 - k])
                dve.wait_ge(agg_ready, (turn * U) + (T + U + 1))
                v.tensor_scalar(rs2[:, 0], agg2[:, :, D], 1e-16, None, ALU.add).then_inc(rsum_step, 1)
                dve.wait_ge(rsum_step, turn + T + 1)
                v.reciprocal(rs2[:, 1], rs2[:, 0]).then_inc(rsum_ready, 1)
                dve.wait_ge(rsum_ready, turn + T + 1)
                v.tensor_tensor(h2[:], agg2[:, :, 0:D], rs2[:, 1].unsqueeze(2).broadcast_to([P, U, D]),
                                ALU.mult).then_inc(hp_ready, 1)
                if old:
                    old_result(turn - 1, 0, 1 - k)
                dve.wait_ge(x_exp, group + 1)
                dve.wait_ge(x1_free, turn + 1)
                flat = "p u d -> p (u d)"
                x1 = res[:, 1 + k]
                v.scalar_tensor_tensor(x1.rearrange(flat), xex[:, 0].rearrange(flat), 1.0,
                                       xs_all[:, ds(turn * (U * D), U * D)], ALU.min, ALU.add).then_inc(x_half, 1)
                dve.wait_ge(x_half, group + 1)
                v.scalar_tensor_tensor(x1.rearrange(flat), h2[:].rearrange(flat), 0.0, x1.rearrange(flat),
                                       ALU.max, ALU.add).then_inc(x_plus_elu, 1)
                dve.wait_ge(x_plus_elu, group + 1)
                node_stats(group, x1, 0)
                node_moments(group, 0)
                node_x1(group, x1, 0)

            dve.wait_ge(out_free, CHUNKS + 4)
            pipelined(dve, layer2)

            def network2(turn, k, use):
                same_keys(turn, 1, pb[2], turn + (2 * TURNS + 1))
                dve.wait_ge(ae_in[k], use * (32 * U) + 32 * U)
                dve.wait_ge(b_in[k], use * (16 * U) + 16 * U)
                v.tensor_tensor(sqr[:, 0], ra[:, k], res[:, 2 + k], ALU.mult).then_inc(squares, 1)
                v.tensor_tensor(ea[:, k], ea[:, k], ra[:, k], ALU.add).then_inc(relu_step, 1)
                dve.wait_ge(squares, turn * 3 + 3)
                v.tensor_reduce(dots[:], sqr[:], AX.X, ALU.add).then_inc(dots_ready, 1)
                dve.wait_ge(dots_ready, turn + 1)
                v.tensor_scalar(simt[:, 0:2], dots[:, 1:3], 1e-16, None, ALU.max).then_inc(sim_step, 1)
                dve.wait_ge(norm_ready, turn + 1)
                v.reciprocal(simt[:, 0:2], simt[:, 2:4]).then_inc(sim_step, 1)
                dve.wait_ge(sim_step, turn * 6 + 2)
                v.tensor_tensor(simt[:, 0], simt[:, 0], simt[:, 1], ALU.mult).then_inc(sim_step, 1)
                dve.wait_ge(sim_step, turn * 6 + 3)
                v.tensor_tensor(simt[:, 0], simt[:, 0], dots[:, 0], ALU.mult).then_inc(sim_step, 1)
                dve.wait_ge(sim_step, turn * 6 + 4)
                v.tensor_scalar(simt[:, 0], simt[:, 0], 1.0, 0.5, ALU.add, ALU.mult).then_inc(sim_step, 1)
                dve.wait_ge(sim_step, turn * 6 + 5)
                v.tensor_scalar(simt[:, 1], simt[:, 0], 0.5, None, ALU.is_ge).then_inc(sim_step, 1)
                dve.wait_ge(sim_step, turn * 6 + 6)
                dve.wait_ge(relu_step, turn + 1)
                for j in range(U):
                    last = v.tensor_scalar(msg2[:, j, 0:D], ea[:, k, j], 0.0, simt[:, 1, j:j + 1], ALU.max, ALU.mult)
                last.then_inc(msg_ready, 1)
                if isinstance(turn, int):
                    old_sum(TURNS - 1, 0, (TURNS - 1) % 2, res[:, 1])
                else:
                    old_sum(turn - 1, 1, k, res[:, 3 - k])
                dve.wait_ge(agg_ready, (turn * U) + (2 * T + U + 1))
                dve.wait_ge(hin_turned, turn + (CHUNKS + TURNS))
                v.scalar_tensor_tensor(hin_d[:], res[:, 2 + k], eps1[0:P, 0:1], agg2[:, :, 0:D], ALU.mult, ALU.add).then_inc(hin_ready, 1)
                if isinstance(turn, int):
                    old_result(TURNS - 1, 0, (TURNS - 1) % 2)
                else:
                    old_result(turn - 1, 1, k)

            pipelined(dve, network2)
            old_sum(TURNS - 1, 1, TURNS % 2, res[:, 2])
            old_result(TURNS - 1, 1, TURNS % 2)

        @block.tensor
        def _(pe):
            te = nc.tensor
            pe.wait_ge(consts_ready, 1)
            pe.sem_inc(count_hot_used, U)
            pe.wait_ge(hist_open, 1)
            for k in range(2):
                te.matmul(pb[k][0:HH, :], zero[0:1, 0:HH], ones[0:1, :], start=True, stop=False)
            with pe.Fori(0, TURNS) as turn:
                for j in range(U):
                    pe.wait_ge(count_hot_ready, turn * U + j + 1)
                    for k in range(2):
                        for h in range(2):
                            last = te.matmul(pb[k][0:HH, h * LO:(h + 1) * LO], hot[:, 0, j, k, h * HH:(h + 1) * HH],
                                             hot[:, 0, j, k, HI:], start=False, stop=False)
                    last.then_inc(count_hot_used, 1)
            for k in range(2):
                last = te.matmul(pb[k][0:HH, :], zero[0:1, 0:HH], ones[0:1, :], start=False, stop=True)
            last.then_inc(degrees_ready, 1)
            pe.wait_ge(table_step, 3)
            te.matmul(pb[2][0:HH, 0:4], above[0:HH, 0:HH], rowsum[:].rearrange("p k h -> p (k h)"), start=True, stop=True)
            te.matmul(pb[2][0:HH, 4:6], ones[0:HH, 0:HH], rowsum[:, :, 0], start=True, stop=True).then_inc(bases_ready, 1)
            def turn_digits(turn, w, half):
                pe.wait_ge(hot_t_ready, turn * 2 + (half + 1))
                for j in range(2):
                    for k in range(2):
                        for h in range(2):
                            o = 4 * j + 2 * k + h
                            last = te.transpose(hot_t_ps[0:HH, o * 128:o * 128 + P],
                                                hot[:, w, half * 2 + j, k, h * HH:(h + 1) * HH], ident16[0:P, 0:P])
                last.then_inc(hot_t_psum, 1)

            def look_up(out_bank, j, tables):
                for k in range(2):
                    for h in range(2):
                        for d in range(2):
                            last = te.matmul(out_bank[0:P, k * LO:(k + 1) * LO], hot_t[:, j, 2 * k + h, 0:P], tables(d, k, h),
                                             start=(h == 0 and d == 0), stop=(h == 1 and d == 1))
                return last

            def places(turn, nxt, use):
                w = 0 if nxt is None else 1 - nxt
                pe.wait_ge(hot_ready, turn + 1)
                turn_digits(turn, w, 0)
                pe.wait_ge(run_updated, turn + 1)
                for k in range(2):
                    for h in range(2):
                        for j in range(U):
                            last = te.matmul(pb[k][0:HH, h * LO:(h + 1) * LO], hot[:, w, j, k, h * HH:(h + 1) * HH],
                                             hot[:, w, j, k, HI:], start=(j == 0), stop=(j == U - 1))
                last.then_inc(counted, 1)
                turn_digits(turn, w, 1)
                pe.wait_ge(ranks_done, turn * U + 2)
                for k in range(2):
                    for j in range(U):
                        for part in range(2):
                            last = te.matmul(pb[3 + k][0:P, j * P:(j + 1) * P],
                                             key16[:, part, k, ds(turn * U + j, 1)].broadcast_to([P, P]),
                                             ident16[0:P, 0:P], start=(part == 0), stop=(part == 1))
                last.then_inc(rows_ready, 1)
                for j in range(U):
                    if j % 2 == 0:
                        pe.wait_ge(hot_t_ready, turn * 2 + (j // 2 + 2))
                    pe.wait_ge(end_used, turn * U + (j + 1))
                    look_up(pb[7], j, lambda d, k, h: end16[:, d, h]).then_inc(end_found, 1)
                    if j == 0:
                        pe.wait_ge(run_split, turn + 1)
                    pe.wait_ge(run_used, turn * U + (j + 1))
                    look_up(pb[5 + j % 2], j, lambda d, k, h: run16[:, w, d, k, h]).then_inc(run_found, 1)

            pe.wait_ge(tables_ready, 1)
            ahead(pe, lambda turn, w, use: None, places)

            pe.wait_ge(weights_ready, 1)

            def turn_hin(n, src_rows, ready, value):
                pe.wait_ge(ready, value)
                pe.wait_ge(hin_t_ready, n + 1)
                for j in range(U):
                    last = te.transpose(pb[4][:, j * P:(j + 1) * P], src_rows[:, j], ident[0:P, 0:P])
                last.then_inc(hin_turned, 1)

            def hidden(n, k=0):
                pe.wait_ge(hin_t_ready, n + 2)
                for c in range(2):
                    pe.wait_ge(hid_ready, n * 2 + c + 1)
                    te.matmul(pb[5 + c][:, 0:U * P], w1m[:, c], hin_t[:], start=True, stop=True).then_inc(hid_psum, 1)

            def output_tile(n, j, k=0):
                if j == 0:
                    pe.wait_ge(y_sum, n + 1)
                    pe.wait_ge(hid_ready, n * 2 + 4)
                    te.matmul(pb[7][0:P, :], ones16[:], b2_parts[:].unsqueeze(1).broadcast_to([3, U, D]), start=True, stop=False)
                for c in range(2):
                    last = te.matmul(pb[7][0:P, j * D:(j + 1) * D], hid[:, k, c, j * P:(j + 1) * P], w2m[:, c],
                                     start=False, stop=(j == U - 1 and c == 1))
                if j == U - 1:
                    last.then_inc(y_psum, 1)

            def output(n, k=0):
                for j in range(U):
                    output_tile(n, j, k)

            def node_group(n, k, use):
                if there(n, 1):
                    hidden(n + 1)
                output(n, k % 2)
                if there(n, 2):
                    turn_hin(n + 2, res[:, (k + 2) % 4], x1_ready, n + 3)

            for n in range(2):
                turn_hin(n, res[:, n], x1_ready, n + 1)
                if n == 0:
                    hidden(0)
            each_group(pe, node_group)

            pe.wait_ge(bulk_step, 9)
            nxt = pb[2][0:P, 0:2 * T]
            te.matmul(nxt, shift[:], key_pad[:, :, 1:T + 1], start=True, stop=False)
            te.matmul(nxt, wrap[:], key_pad[:, :, 2:T + 2], start=False, stop=True).then_inc(next_psum, 1)

            def key_row(count):
                pe.wait_ge(key_now_ready, count)
                for j in range(U):
                    last = te.matmul(pb[2][0:P, j * P:(j + 1) * P],
                                     key_now[:, j + 1:j + 2].broadcast_to([P, P]),
                                     ident[0:P, 0:P], start=True, stop=True)
                last.then_inc(key_rows, 1)

            pe.wait_ge(lists_ready, 1)

            def turn_x(turn, c, rows):
                pe.wait_ge(xt_ready, turn * 2 + (c + 1))
                for j in range(U):
                    last = te.transpose(pb[1][:, j * P:(j + 1) * P], rows[:, j], ident[0:P, 0:P])
                last.then_inc(x_turned, 1)

            def scores_of(turn):
                pe.wait_ge(xt_ready, turn * 2 + 3)
                for j in range(U):
                    for k in range(2):
                        last = te.matmul(pb[3][0:P, 256 + j * HEADS:256 + (j + 1) * HEADS], xt[:, k, j * P:(j + 1) * P], wa[:, k],
                                         start=(k == 0), stop=(k == 1))
                last.then_inc(scores_psum, 1)

            def heads(turn, j):
                pe.wait_ge(msg_ready, turn * U + j if j else turn * U + 1)
                te.matmul(pb[4 + j % 2][0:P, :], xt[:, 1, j * P:(j + 1) * P], w1g[:].rearrange("d h f -> d (h f)"),
                          start=True, stop=True).then_inc(h_psum, 1)

            def add_up(turn, j):
                if j == 0:
                    pe.wait_ge(same_ready, turn + 2)
                    pe.wait_ge(esc_ready, turn + 1)
                pe.wait_ge(msg_ready, turn * U + (j + 2))
                pe.wait_ge(agg_ready, turn * U + (j + 1))
                a0 = agg[:, (j - 1) % U]
                for o, m, b in ((pb[6][0:P, :], msg[:, j % 2], a0[:, 0:512]), (pb[7][0:P, 0:HEADS], esc[:, j], a0[:, 512:])):
                    te.matmul(o, same[:, j], m, start=True, stop=False)
                    last = te.matmul(o, carry[:, j], b, start=False, stop=True)
                last.then_inc(agg_psum, 1)

            def turn_xx(turn, j):
                pe.wait_ge(helu_ready, turn * U + (j + 1))
                pe.wait_ge(xx_ready, turn * U + (j + 1))
                for c in range(C2):
                    last = te.transpose(pb[0][:, c * P:(c + 1) * P], hex_[:, j % 2, c * 128:(c + 1) * 128], ident[0:P, 0:P])
                last.then_inc(xx_psum, 1)

            def project(turn, j):
                pe.wait_ge(xx_ready, turn * U + (j + 2))
                pe.wait_ge(g2_ready, turn * U + (j + U))
                for c in range(C2):
                    last = te.matmul(pb[3][0:P, 0:D + 2], xx_t[:, c], w2g[:, c], start=(c == 0), stop=(c == C2 - 1))
                last.then_inc(g2_psum, 1)

            def layer1_first(turn, k, use):
                pe.wait_ge(x_in[k], 32 * U)
                turn_x(turn, 0, xs[:, k])
                key_row(turn + 1)
                turn_x(turn, 1, xd[:, k])
                scores_of(turn)
                heads(turn, 0)
                heads(turn, 1)

            def layer1(turn, k, use):
                more = k is not None
                add_up(turn, 0)
                heads(turn, 2)
                if more:
                    pe.wait_ge(x_in[k], use * (32 * U) + 32 * U)
                    turn_x(turn + 1, 0, xs[:, k])
                add_up(turn, 1)
                heads(turn, 3)
                turn_xx(turn, 0)
                if more:
                    turn_x(turn + 1, 1, xd[:, k])
                project(turn, 0)
                add_up(turn, 2)
                turn_xx(turn, 1)
                add_up(turn, 3)
                project(turn, 1)
                if more:
                    key_row(turn + 2)
                    pe.wait_ge(g2_ready, turn * U + (U + 2))
                    scores_of(turn + 1)
                turn_xx(turn, 2)
                if more:
                    heads(turn + 1, 0)
                    pe.wait_ge(lr_ready, turn + 3)
                project(turn, 2)
                if more:
                    heads(turn + 1, 1)
                turn_xx(turn, 3)
                project(turn, 3)

            ahead(pe, layer1_first, layer1)

            pe.wait_ge(g2_ready, T + U)
            for o, pick in ((0, pick_last), (2, pick_first)):
                te.matmul(pb[2][0:P, o * T:(o + 1) * T], pick[:], s2_all[:], start=True, stop=True)
                last = te.matmul(pb[2][0:P, (o + 1) * T:(o + 2) * T], pick[:], key_pad[:, 0, 1:T + 1], start=True, stop=True)
            last.then_inc(s2_rows, 1)
            pe.wait_ge(s2_ready, 1)

            def add_up_rows(turn, width, round_no, meanwhile):
                pe.wait_ge(same_ready, turn + (round_no * TURNS + 2))
                pe.wait_ge(msg_ready, turn + (T + (round_no - 1) * TURNS + 2))
                for j in range(U):
                    pe.wait_ge(agg_ready, turn * U + (round_no * T + j + 1))
                    o = pb[3][0:P, 0:width]
                    te.matmul(o, same[:, j], msg2[:, j, 0:width], start=True, stop=False)
                    te.matmul(o, carry[:, j], agg2[:, (j - 1) % U, 0:width], start=False, stop=True).then_inc(agg_psum, 1)
                    meanwhile(j)

            def layer2(turn, k, use):
                n = turn + (CHUNKS - 1)
                old = not isinstance(turn, int)
                key_row(turn + (TURNS + 1))
                if old:
                    turn_hin(n, res[:, 2 - k], x1_ready, turn + (CHUNKS + TURNS))
                    hidden(n)
                add_up_rows(turn, D + 1, 1, lambda j: output_tile(n, j) if old else None)

            pipelined(pe, layer2)

            def network2(turn, k, use):
                n = turn + (CHUNKS + TURNS - 1)
                key_row(turn + (2 * TURNS + 1))
                if isinstance(turn, int):
                    turn_hin(n, res[:, 1], x1_ready, CHUNKS + 2 * TURNS)
                else:
                    turn_hin(n, hin_d, hin_ready, turn)
                hidden(n)
                add_up_rows(turn, D, 2, lambda j: output_tile(n, j))

            pipelined(pe, network2)
            n = CHUNKS + 2 * TURNS - 1
            turn_hin(n, hin_d, hin_ready, TURNS)
            hidden(n)
            output(n)

        @block.scalar
        def _(act):
            a = nc.scalar
            a.preload_act_table_set("natural_log_exp_and_others")
            act.sem_inc(hist_open, 1)
            for used in (hot_t_ready, run_updated, end_used, found_kept):
                act.sem_inc(used, 1)
            act.sem_inc(run_used, 2)
            act.sem_inc(ranks_done, 2)
            act.sem_inc(hin_t_ready, 1)
            act.sem_inc(hid_ready, 2)
            act.sem_inc(y_sum, 1)
            act.sem_inc(out_free, 4)
            act.sem_inc(x1_free, 2)
            act.sem_inc(row_free, U + 1)
            act.sem_inc(g2_ready, U)
            for used in (xt_ready, xs_free, plain_free, g2_free, same_ready, agg_ready, xx_ready, lr_ready, msg_ready):
                act.sem_inc(used, 1)

            def cast_run(w):
                a.copy(run16[:, w, 0], start_tab).then_inc(run_cast, 1)

            def first_tables(turn, w, use):
                act.wait_ge(tables_ready, 1)
                cast_run(w)

            def places(turn, nxt, use):
                for half in range(2):
                    act.wait_ge(hot_t_psum, turn * 2 + (half + 1))
                    a.copy(hot_t[:, 2 * half:2 * half + 2, :, 0:P],
                           hot_t_ps[0:HH, :].rearrange("p (u o e) -> p u o e", u=2, o=4)[:, :, :, 0:P]).then_inc(hot_t_ready, 1)
                if nxt is not None:
                    act.wait_ge(run_updated, turn + 2)
                    cast_run(nxt)

            ahead(act, first_tables, places)

            def exp_x(n, xv, k):
                a.activation(xex[:, k], xv, ACT.Exp).then_inc(x_exp, 1)

            def rstd_of(n, mom, r, moments, log, ready, k):
                act.wait_ge(moments, n + 1)
                a.activation(r[:, k], mom[:, k, :, 1], ACT.Ln, bias=ln_eps[0:P, 0:1]).then_inc(log, 1)
                act.wait_ge(log, n + 1)
                a.activation(r[:, k], r[:, k], ACT.Exp, scale=-0.5).then_inc(ready, 1)

            def x_rstd_of(n, k):
                rstd_of(n, moment, rstd, x_moments, x_log, x_rstd, k)

            def y_rstd_of(n, k):
                rstd_of(n, post_moment, post_rstd, y_moments, y_log, y_rstd, k)

            def copy_hin(n, scaled):
                act.wait_ge(hin_turned, n + 1)
                scale = eps1[:, 0:1] if scaled else 1.0
                a.activation(hin_t[:], pb[4][:, 0:U * P], ACT.Copy if not scaled else ACT.Identity, scale=scale).then_inc(hin_t_ready, 1)

            def relus(n, k=0):
                for c in range(2):
                    act.wait_ge(hid_psum, n * 2 + c + 1)
                    a.activation(hid[:, k, c], pb[5 + c][:, 0:U * P], ACT.Relu, bias=b1[:, c:c + 1]).then_inc(hid_ready, 1)

            act.wait_ge(weights_ready, 1)

            def result(n, k):
                act.wait_ge(y_bias, n + 1)
                act.wait_ge(out_free, n + 1)
                for j in range(U):
                    last = a.activation(outb[:, k, j], post_sum[:, k % 2, j], ACT.Identity, bias=post_bias[:, k, j:j + 1],
                                        scale=post_rstd[:, k, j:j + 1])
                last.then_inc(y_out, 1)

            def node_group(n, k, use):
                if there(n, 1):
                    relus(n + 1, (k + 1) % 2)
                if there(n, 2):
                    copy_hin(n + 2, True)
                if there(n, 3):
                    x_rstd_of(n + 3, (k + 3) % 4)
                if there(n, 5):
                    act.wait_ge(x_loaded[(k + 1) % 4], use * 16 + (48 if k == 3 else 32))
                    exp_x(n + 5, xin[:, (k + 1) % 4], (k + 1) % 4)
                if there(n, -1):
                    result(n - 1, (k + 3) % 4)
                y_rstd_of(n, k)

            for n in range(4):
                act.wait_ge(x_loaded[n], 16)
                exp_x(n, xin[:, n], n)
                if n < 3:
                    x_rstd_of(n, n)
            act.wait_ge(x_loaded[0], 32)
            exp_x(4, xin[:, 0], 0)
            copy_hin(0, True)
            relus(0, 0)
            copy_hin(1, True)
            each_group(act, node_group)
            result(CHUNKS - 1, 3)

            def copy_xt(turn, c):
                act.wait_ge(x_turned, turn * 2 + (c + 1))
                a.copy(xt[:, c], pb[1][:, 0:U * P]).then_inc(xt_ready, 1)

            def exp_scores(turn):
                act.wait_ge(lr_ready, turn + 2)
                a.activation(esc[:], lr[:], ACT.Exp, scale=-1.0).then_inc(esc_ready, 1)

            def copy_agg(turn, j):
                act.wait_ge(agg_psum, turn * U + (j + 1))
                a.copy(agg[:, j, 0:512], pb[6][0:P, :])
                a.copy(agg[:, j, 512:], pb[7][0:P, 0:HEADS]).then_inc(agg_ready, 1)

            def exp_h(turn, j):
                act.wait_ge(hp_ready, turn * U + (j + 1))
                a.activation(hex_[:, j % 2], hp[:, j % 2], ACT.Exp).then_inc(hex_ready, 1)

            def copy_xx(turn, j):
                act.wait_ge(xx_psum, turn * U + (j + 1))
                a.copy(xx_t[:], pb[0][:, 0:C2 * P].rearrange("p (c e) -> p c e", c=C2)).then_inc(xx_ready, 1)

            def copy_g2(turn, j):
                act.wait_ge(g2_psum, turn * U + (j + 1))
                if j == 0:
                    act.wait_ge(g2_free, turn + 1)
                a.copy(s2_all[:, ds(turn * U + j, 1)], pb[3][0:P, D:D + 1])
                a.copy(g2s[:, j], pb[3][0:P, 0:D + 2]).then_inc(g2_ready, 1)

            def layer1_first(turn, k, use):
                copy_xt(turn, 0)
                copy_xt(turn, 1)
                exp_x(turn, xd[:, k], 0)
                exp_scores(turn)
                x_rstd_of(turn + CHUNKS, 0)

            def layer1(turn, k, use):
                more = k is not None
                copy_agg(turn, 0)
                if more:
                    copy_xt(turn + 1, 0)
                exp_h(turn, 0)
                copy_agg(turn, 1)
                exp_h(turn, 1)
                copy_xx(turn, 0)
                if more:
                    copy_xt(turn + 1, 1)
                copy_g2(turn, 0)
                copy_agg(turn, 2)
                copy_xx(turn, 1)
                exp_h(turn, 2)
                copy_agg(turn, 3)
                copy_g2(turn, 1)
                exp_h(turn, 3)
                if more:
                    exp_x(turn + 1, xd[:, k], 0)
                    exp_scores(turn + 1)
                copy_xx(turn, 2)
                copy_g2(turn, 2)
                copy_xx(turn, 3)
                if more:
                    x_rstd_of(turn + (CHUNKS + 1), 0)
                copy_g2(turn, 3)

            ahead(act, layer1_first, layer1)

            def copy_agg2(turn, width, round_no):
                for j in range(U):
                    act.wait_ge(agg_psum, turn * U + (round_no * T + j + 1))
                    a.copy(agg2[:, j, 0:width], pb[3][0:P, 0:width]).then_inc(agg_ready, 1)

            def layer2(turn, k, use):
                group = turn + (CHUNKS + TURNS)
                n = turn + (CHUNKS - 1)
                old = not isinstance(turn, int)
                if old:
                    copy_hin(n, True)
                act.wait_ge(sc2_ready, turn + 1)
                a.activation(msg2[:, :, D], sc2[:, 0], ACT.Exp, scale=-1.0).then_inc(e2_ready, 1)
                if old:
                    relus(n)
                copy_agg2(turn, D + 1, 1)
                if old:
                    y_rstd_of(n, 1 - k)
                act.wait_ge(hp_ready, turn + (T + 1))
                exp_x(group, h2[:], 0)
                x_rstd_of(group, 0)

            pipelined(act, layer2)

            def network2(turn, k, use):
                n = turn + (CHUNKS + TURNS - 1)
                copy_hin(n, isinstance(turn, int))
                act.wait_ge(ae_in[k], use * (32 * U) + 32 * U)
                a.activation(sqr[:, 1], ra[:, k], ACT.Square).then_inc(squares, 1)
                act.wait_ge(b_in[k], use * (16 * U) + 16 * U)
                a.activation(sqr[:, 2], res[:, 2 + k], ACT.Square).then_inc(squares, 1)
                relus(n)
                act.wait_ge(sim_step, turn * 6 + 1)
                a.activation(simt[:, 2:4], simt[:, 0:2], ACT.Ln).then_inc(norm_log, 1)
                act.wait_ge(norm_log, turn + 1)
                a.activation(simt[:, 2:4], simt[:, 2:4], ACT.Exp, scale=0.5).then_inc(norm_ready, 1)
                copy_agg2(turn, D, 2)
                y_rstd_of(n, (TURNS - 1) % 2 if isinstance(turn, int) else k)

            pipelined(act, network2)
            n = CHUNKS + 2 * TURNS - 1
            copy_hin(n, False)
            relus(n)
            y_rstd_of(n, TURNS % 2)


_INS = ["x", "src", "dst", "edge_attr_128", "L0_gnn_W1", "L0_gnn_a1", "L0_gnn_W2", "L0_gnn_a2",
        "L1_gnn_W1", "L1_gnn_b1", "L1_gnn_W2", "L1_gnn_b2", "L1_gnn_eps"]


def kernel(**inputs):
    import numpy as _np
    import concourse.bacc as _bacc
    from concourse import mybir as _mybir
    from concourse.bass_utils import run_bass_kernel_spmd as _run

    nc = _bacc.Bacc("TRN2", target_bir_lowering=False, num_devices=1)
    arrays, args = {}, []
    for name in _INS:
        a = _np.ascontiguousarray(inputs[name])
        a = a.reshape(a.shape or (1,))
        arrays[f"in_{name}_dram"] = a
        args.append(nc.dram_tensor(f"in_{name}_dram", a.shape, _mybir.dt.from_np(a.dtype), kind="ExternalInput").ap())
    args.append(nc.dram_tensor("out_0_dram", (50000, 128), _mybir.dt.float32, kind="ExternalOutput").ap())
    build_gnn(nc, *args)
    r = _run(nc, [arrays], core_ids=[0])
    return r.results[0]["out_0_dram"]
```

```python
import math
import concourse.bass as bass
from concourse import mybir
from concourse.alu_op_type import AluOpType as ALU
from contextlib import ExitStack

F32 = mybir.dt.float32
BF16 = mybir.dt.bfloat16
I32 = mybir.dt.int32
ACT = mybir.ActivationFunctionType
AX = mybir.AxisListType
ds = bass.ds


def build_gnn(nc, x, src, dst, edge_attr, W1g, a1g, W2g, a2g, W1m, b1m, W2m, b2m, epsm, out):
    N, D = x.shape
    E = src.shape[0]
    P = 125
    T = E // P
    U = 4
    TURNS = T // U
    LO = 256
    HI = -(-N // LO)
    HH = HI // 2
    assert P * T == E and U * TURNS == T and 2 * HH == HI
    HEADS, _, FH = W1g.shape
    C2 = HEADS * FH // 128
    CHUNKS = N // (P * U)
    assert CHUNKS * P * U == N and CHUNKS % 4 == 0 and FH * HEADS == 512
    NONE = float(E)
    ROUND = float(1.5 * 2 ** 23)

    ctx = ExitStack()
    with ctx:
        def sb(name, shape, dt=F32):
            return ctx.enter_context(nc.sbuf_tensor(name, shape, dt))

        def bank(name, shape, dt=F32):
            return ctx.enter_context(nc.psum_tensor(name, shape, dt))

        def sem(name):
            return ctx.enter_context(nc.semaphore(name))

        def dram(name, shape, dt=F32):
            return nc.dram_tensor(name, shape, dt, kind="Internal").ap()

        xs_room = sb("xs_room", [128, T * D])
        xs_all = xs_room[0:P, :]
        room = {"early": 0, "late": 0}

        def carve(when, rows, *shape):
            size = math.prod(shape)
            at = room[when]
            room[when] = at + size
            assert at + size <= T * D
            flat = xs_room[0:rows, at:at + size]
            names = "abcd"[:len(shape)]
            return flat.rearrange(f"p ({' '.join(names)}) -> p {' '.join(names)}", **dict(zip(names, shape))) if len(shape) > 1 else flat

        def early(rows, *shape):
            return carve("early", rows, *shape)

        def late(rows, *shape):
            return carve("late", rows, *shape)

        ident = sb("ident", [128, 128])
        ident16 = sb("ident16", [128, 128], BF16)
        above = sb("above", [128, 128])
        ones = sb("ones", [128, 512])
        digits = sb("digits", [P, LO], BF16)
        slot_no = sb("slot_no", [P, T])
        edge_no = sb("edge_no", [P, T])

        key_i = sb("key_i", [P, 2, T], I32)
        digit_i = sb("digit_i", [P, 2, 2, T], I32)
        key = sb("key", [P, 2, T])
        digit = sb("digit", [P, 2, 2, T])

        meta_src = [dram(f"meta_src_{k}", (E, 4)) for k in range(2)]
        meta_dst = [dram(f"meta_dst_{k}", (E, 4)) for k in range(2)]

        pb = [bank(f"pb{k}", [128, 512]) for k in range(8)]

        consts_ready = sem("consts_ready")
        pool_step = sem("pool_step")
        pool_go = sem("pool_go")
        keys_loaded = sem("keys_loaded")
        digits_int = sem("digits_int")
        digits_ready = sem("digits_ready")

        hot = sb("hot", [P, 2, U, 2, HI + LO], BF16)
        count_hot_ready = sem("count_hot_ready")
        count_hot_used = sem("count_hot_used")
        degrees_ready = sem("degrees_ready")
        hist_open = sem("hist_open")
        deg = early(HH, 2, 2, LO)
        cum = early(HH, 2, 2, LO)
        rowsum = sb("rowsum", [HH, 2, 2])
        base = sb("base", [HH, 2, 2])
        start_tab = early(HH, 2, 2, LO)
        end_tab = early(HH, 2, LO)
        ends_tmp = early(HH, 2, 2, LO)
        table_step = sem("table_step")
        bases_ready = sem("bases_ready")
        tables_ready = sem("tables_ready")

        hot_ready = sem("hot_ready")
        apart = sb("apart", [P, 2, 2, HI], BF16)
        apart_ready = sem("apart_ready")
        high_ready = sem("high_ready")
        hot_t_psum = sem("hot_t_psum")
        hot_t_ready = sem("hot_t_ready")
        counted = sem("counted")
        run_updated = sem("run_updated")
        run_cast = sem("run_cast")
        run_split = sem("run_split")
        rows_ready = sem("rows_ready")
        ranks_done = sem("ranks_done")
        end_found = sem("end_found")
        end_used = sem("end_used")
        run_found = sem("run_found")
        run_used = sem("run_used")
        found_kept = sem("found_kept")
        run16 = early(HH, 2 * 4 * LO).bitcast(BF16).rearrange("p (w d k h l) -> p w d k h l", w=2, d=2, k=2, h=2)
        end16 = early(HH, 2 * LO).bitcast(BF16).rearrange("p (d h l) -> p d h l", d=2, h=2)
        key16 = sb("key16", [P, 2, 2, T], BF16)
        hot_t = sb("hot_t", [HH, U, 4, 128], BF16)
        found = sb("found", [P, U, 6])
        keep = sb("keep", [P, T, 6])
        before = sb("before", [P, U * P])
        junk = sb("junk", [P, 2, 4, LO], BF16)
        junk2 = early(P, U * P * 2).bitcast(BF16).rearrange("p (w k e) -> p w k e", w=2, k=2)

        pos = sb("pos", [P, 2, T])
        q = sb("q", [P, 2, T])
        addr_i = sb("addr_i", [P, 2, T], I32)
        rowdata = early(P, 2, T, 4)
        bulk_step = sem("bulk_step")
        rows_to_move = sem("rows_to_move")
        zero = sb("zero", [P, 4 * T])
        meta_zeroed = sem("meta_zeroed")
        SC = 10
        move_idx = sb("move_idx", [P, 2, SC], I32)
        move_row = sb("move_row", [P, 2, SC, 4])
        move_slots = sem("move_slots")
        moved = [[sem(f"moved_{k}{h}") for h in range(2)] for k in range(2)]
        meta_in = early(P, 2, 2, T, 4)
        meta = sb("meta", [P, 2, T, 4])
        meta_loaded = sem("meta_loaded")
        meta_ready = sem("meta_ready")

        w1g = sb("w1g", [D, HEADS, FH])
        w2g = sb("w2g", [128, C2, D + 2])
        wa = sb("wa", [D, 2, HEADS])
        wa_tmp = early(D, 2, HEADS, FH)
        a1b = sb("a1b", [D, HEADS, 2 * FH])
        a2b = sb("a2b", [128, 2 * D])
        w2_tmp = early(128, 2, C2, D)
        w1m = sb("w1m", [D, 2, 128])
        w2m = sb("w2m", [128, 2, D])
        b1 = sb("b1", [128, 2])
        b2 = sb("b2", [3, D])
        b2_rest = sb("b2_rest", [3, 3, D])
        b2_part = sb("b2_part", [3, 3, D], BF16)
        b2_parts = sb("b2_parts", [3, D], BF16)
        ones16 = sb("ones16", [3, P], BF16)
        eps1 = sb("eps1", [128, 1])
        ln_eps = sb("ln_eps", [128, 1])
        weights_loaded = sem("weights_loaded")
        weights_step = sem("weights_step")
        weights_ready = sem("weights_ready")

        g2 = dram("g2", (E + 1, D + 2))
        x1_rows = dram("x1_rows", (2 * E, D))
        zero_row_stored = sem("zero_row_stored")

        xin = sb("xin", [P, 4, U, D])
        xex = sb("xex", [P, 4, U, D])
        res = sb("res", [P, 4, U, D])
        hin_t = sb("hin_t", [D, U * P])
        hid = sb("hid", [128, 2, 2, U * P])
        post_sum = sb("post_sum", [P, 2, U, D])
        outb = sb("outb", [P, 4, U, D])
        stats = sb("stats", [P, 4, U, 6])
        moment = sb("moment", [P, 4, U, 2])
        rstd = sb("rstd", [P, 4, U])
        post_bias = sb("post_bias", [P, 4, U])
        post_stat = sb("post_stat", [P, 4, U, 6])
        post_moment = sb("post_moment", [P, 4, U, 2])
        post_rstd = sb("post_rstd", [P, 4, U])
        x_loaded = [sem(f"x_loaded_{k}") for k in range(4)]
        out_stored = [sem(f"out_stored_{k}") for k in range(4)]
        x_exp = sem("x_exp")
        x_half = sem("x_half")
        x_plus_elu = sem("x_plus_elu")
        x_stats = sem("x_stats")
        x_moments = sem("x_moments")
        x_log = sem("x_log")
        x_rstd = sem("x_rstd")
        y_bias = sem("y_bias")
        x1_ready = sem("x1_ready")
        hin_turned = sem("hin_turned")
        hin_t_ready = sem("hin_t_ready")
        hid_psum = sem("hid_psum")
        hid_ready = sem("hid_ready")
        y_psum = sem("y_psum")
        y_sum = sem("y_sum")
        y_stats = sem("y_stats")
        y_moments = sem("y_moments")
        y_log = sem("y_log")
        y_rstd = sem("y_rstd")
        y_out = sem("y_out")

        key_pad = sb("key_pad", [P, 2, T + 2])
        meta_i = sb("meta_i", [P, 2, T, 4], I32)
        next_key = sb("next_key", [P, 2, T])
        out_row = sb("out_row", [P, 2, T], I32)
        shift = sb("shift", [P, P])
        wrap = sb("wrap", [P, P])
        pick_last = sb("pick_last", [P, P])
        pick_first = sb("pick_first", [P, P])
        next_psum = sem("next_psum")
        lists_ready = sem("lists_ready")

        slots_a = sb("slots_a", [P, 2, U, 2], I32)
        xs = xin[:, 0:2]
        xd = xin[:, 2:4]
        h2 = sb("h2", [P, U, D])
        xt = sb("xt", [D, 2, U * P])
        lr = sb("lr", [P, U, HEADS])
        dve_go = sem("dve_go")
        same = sb("same", [P, U, P])
        carry = sb("carry", [P, U, P])
        msg = sb("msg", [P, 2, HEADS * FH])
        same_of = (same, msg[:, 0, 0:U * P].rearrange("p (u e) -> p u e", u=U))
        carry_of = (carry, msg[:, 1, 0:U * P].rearrange("p (u e) -> p u e", u=U))
        esc = sb("esc", [P, U, HEADS])
        agg = sb("agg", [P, U, HEADS * FH + HEADS])
        hp = sb("hp", [P, 2, HEADS * FH])
        hex_ = sb("hex_", [P, 2, HEADS * FH])
        rsum = sb("rsum", [P, U, HEADS])
        xx_t = sb("xx_t", [128, C2, P])
        g2s = sb("g2s", [P, U, D + 2])
        s2_all = sb("s2_all", [P, T])
        aslots_ready = sem("aslots_ready")
        x_in = [sem(f"x_in_{k}") for k in range(2)]
        x_turned = sem("x_turned")
        xt_ready = sem("xt_ready")
        key_rows = sem("key_rows")
        scores_psum = sem("scores_psum")
        lr_half = sem("lr_half")
        lr_ready = sem("lr_ready")
        esc_ready = sem("esc_ready")
        same_ready = sem("same_ready")
        h_psum = sem("h_psum")
        msg_ready = sem("msg_ready")
        agg_psum = sem("agg_psum")
        agg_ready = sem("agg_ready")
        rsum_step = sem("rsum_step")
        rsum_ready = sem("rsum_ready")
        hp_ready = sem("hp_ready")
        hex_ready = sem("hex_ready")
        helu_half = sem("helu_half")
        helu_ready = sem("helu_ready")
        xx_psum = sem("xx_psum")
        xx_ready = sem("xx_ready")
        g2_psum = sem("g2_psum")
        g2_ready = sem("g2_ready")
        g2_stored = sem("g2_stored")
        xs_kept = sem("xs_kept")
        plain_stored = sem("plain_stored")

        s2_rows = sem("s2_rows")
        s2_step = sem("s2_step")
        s2_ready = sem("s2_ready")
        ends2 = sb("ends2", [P, 2, 2, T + 1])
        cont = sb("cont", [P, T])
        cover = sb("cover", [P, T])
        tail = sb("tail", [P, T])
        after = sb("after", [P, T])
        s2_src = sb("s2_src", [P, T])
        slots_b = sb("slots_b", [P, 2, U], I32)
        g = agg[:].rearrange("p u f -> p (u f)")[:, 0:2 * U * (D + 2)].rearrange("p (w u f) -> p w u f", w=2, u=U)
        sc2 = sb("sc2", [P, 2, U])
        msg2 = sb("msg2", [P, U, D + 1])
        agg2 = sb("agg2", [P, U, D + 1])
        rs2 = sb("rs2", [P, 2, U])
        g_in = [sem(f"g_in_{k}") for k in range(2)]
        bslots_ready = sem("bslots_ready")
        sc2_a = sem("sc2_a")
        sc2_b = sem("sc2_b")
        sc2_ready = sem("sc2_ready")
        e2_ready = sem("e2_ready")
        x1_stored = sem("x1_stored")

        slots_c = sb("slots_c", [P, U], I32)
        slots_d = sb("slots_d", [P, 2, U, 2], I32)
        cslots_ready = sem("cslots_ready")
        dslots_ready = sem("dslots_ready")
        row_out = sem("row_out")
        ra = late(P, 2, U, D)
        ea = late(P, 2, U, D)
        sqr = late(P, 3, U, D)
        dots = sb("dots", [P, 3, U])
        simt = sb("simt", [P, 4, U])
        hin_d = late(P, U, D)
        a_in = [sem(f"a_in_{k}") for k in range(2)]
        e_in = [sem(f"e_in_{k}") for k in range(2)]
        ea_rows = dram("ea_rows", (E, D))
        slots_e = sb("slots_e", [P, 2, U], I32)
        eslots_ready = sem("eslots_ready")
        ef = outb[:, 2:4]
        ef_in = [sem(f"ef_in_{k}") for k in range(2)]
        ef_stored = sem("ef_stored")
        ef_free = sem("ef_free")
        b_in = [sem(f"b_in_{k}") for k in range(2)]
        xb = xin[:, 0:2]
        xb_kept = xin[:, 2:4]
        b_kept = sem("b_kept")
        squares = sem("squares")
        dots_ready = sem("dots_ready")
        norm_log = sem("norm_log")
        norm_ready = sem("norm_ready")
        sim_step = sem("sim_step")
        relu_step = sem("relu_step")
        hin_ready = sem("hin_ready")
        xs_free = sem("xs_free")
        plain_free = sem("plain_free")
        g2_free = sem("g2_free")
        x1_free = sem("x1_free")
        row_free = sem("row_free")
        out_free = sem("out_free")

        hot_t_ps = pb[2][:].bitcast(BF16)

        def pipelined(engine, step):
            step(0, 0, 0)
            step(1, 1, 0)
            with engine.Fori(0, TURNS // 2 - 1) as pair:
                for k in range(2):
                    step(pair * 2 + (2 + k), k, pair + 1)
            step(TURNS - 1, 0, TURNS // 2)

        def ahead(engine, first, step):
            first(0, 0, 0)
            with engine.Fori(0, TURNS // 2) as pair:
                for half in range(2):
                    step(pair * 2 + half, 1 - half, pair + half)
            step(TURNS - 1, None, None)

        def each_group(engine, step, lists=lambda: None):
            for k in range(4):
                step(k, k, 0)
            with engine.Fori(0, CHUNKS // 4 - 3) as use:
                for k in range(4):
                    step(use * 4 + (4 + k), k, use + 1)
            lists()
            for n in range(CHUNKS - 8, CHUNKS):
                step(n, n % 4, n // 4)

        def there(group, ahead_by):
            return not isinstance(group, int) or 0 <= group + ahead_by < CHUNKS

        block = ctx.enter_context(nc.Block())

        @block.sync
        def _(sp):
            sp.dma_start(key_i[:, 0], src.rearrange("(p t) -> p t", t=T)).then_inc(keys_loaded, 16)
            sp.dma_start(key_i[:, 1], dst.rearrange("(p t) -> p t", t=T)).then_inc(keys_loaded, 16)
            sp.wait_ge(consts_ready, 1)
            for tab in meta_src + meta_dst:
                sp.dma_start(tab.rearrange("(p t) c -> p (t c)", p=P), zero[:]).then_inc(meta_zeroed, 16)
            sp.dma_start(w1g[:], W1g.rearrange("h d f -> d h f")).then_inc(weights_loaded, 16)
            sp.dma_start(a1b[:].rearrange("p h f -> p (h f)"), a1g.rearrange("h f -> (h f)").partition_broadcast(D)).then_inc(weights_loaded, 16)
            sp.dma_start(w2g[:, :, 0:D], W2g.rearrange("(c p) f -> p c f", p=128)).then_inc(weights_loaded, 16)
            sp.dma_start(a2b[:], a2g.partition_broadcast(128)).then_inc(weights_loaded, 16)
            sp.dma_start(w1m[:], W1m.rearrange("d (c f) -> d c f", c=2)).then_inc(weights_loaded, 16)
            sp.dma_start(w2m[:], W2m.rearrange("(c p) f -> p c f", p=128)).then_inc(weights_loaded, 16)
            sp.dma_start(b1[:], b1m.rearrange("(c p) -> p c", p=128), allow_slow_non_contiguous=True).then_inc(weights_loaded, 16)
            sp.dma_start(b2[:], b2m.partition_broadcast(3)).then_inc(weights_loaded, 16)
            sp.dma_start(eps1[:], epsm.partition_broadcast(128)).then_inc(weights_loaded, 16)
            sp.wait_ge(consts_ready, 1)
            sp.dma_start(g2[E:E + 1, :], zero[0:1, 0:D + 2]).then_inc(zero_row_stored, 16)
            x_chunks = x.rearrange("(n p u) d -> n p (u d)", p=P, u=U)
            out_chunks = out.rearrange("(n p u) d -> n p (u d)", p=P, u=U)

            def chunk(tensor, n):
                return tensor[ds(n, 1)].rearrange("o p f -> (o p) f")

            for k in range(4):
                sp.dma_start(xin[:, k].rearrange("p u d -> p (u d)"), x_chunks[k]).then_inc(x_loaded[k], 16)

            def put_out(n, k):
                sp.wait_ge(y_out, n + 1)
                sp.dma_start(chunk(out_chunks, n), outb[:, k].rearrange("p u d -> p (u d)")).then_inc(out_stored[k], 16)

            def free_out(k, count):
                sp.wait_ge(out_stored[k], count * 16)
                sp.sem_inc(out_free, 1)

            def node_group(n, k, use):
                if there(n, 7):
                    load_x(n + 7, (k + 3) % 4)
                if there(n, -2):
                    put_out(n - 2, (k + 2) % 4)
                if there(n, -3):
                    free_out((k + 1) % 4, use + 1 if k == 3 else use)

            def load_x(n, k):
                sp.wait_ge(x_plus_elu, n - 3)
                sp.dma_start(xin[:, k].rearrange("p u d -> p (u d)"), chunk(x_chunks, n)).then_inc(x_loaded[k], 16)

            for n in range(4, 7):
                load_x(n, n % 4)
            def reload_lists():
                for k, tabs in enumerate((meta_src, meta_dst)):
                    for h in range(2):
                        sp.wait_ge(moved[k][h], 16 * T // 2)
                for k, tabs in enumerate((meta_src, meta_dst)):
                    for h in range(2):
                        sp.dma_start(meta_in[:, k, h].rearrange("p t c -> p (t c)"),
                                     tabs[h].rearrange("(p t) c -> p (t c)", p=P)).then_inc(meta_loaded, 16)

            each_group(sp, node_group, reload_lists)
            put_out(CHUNKS - 2, 2)
            put_out(CHUNKS - 1, 3)
            for k in range(1, 4):
                free_out(k, CHUNKS // 4)

            def keep_next(turn, k, use):
                sp.wait_ge(x_in[k], use * (32 * U) + 32 * U)
                sp.dma_start(xs_all[:, ds(turn * (U * D), U * D)], xs[:, k].rearrange("p u d -> p (u d)")).then_inc(xs_kept, 16)
                sp.wait_ge(xs_kept, turn * 16 + 16)
                sp.sem_inc(xs_free, 1)
                sp.wait_ge(x1_ready, turn + (CHUNKS + 1))
                sp.dma_start(x1_rows[ds(turn * (U * P) + E, U * P)].rearrange("(u p) d -> p u d", p=P),
                             res[:, 0]).then_inc(plain_stored, 16)

            def layer1(turn, k, use):
                if k is not None:
                    keep_next(turn + 1, k, use)
                w = 0 if k is None else 1 - k
                ef_use = TURNS // 2 if k is None else use if k == 1 else use - 1
                sp.wait_ge(ef_in[w], ef_use * (16 * U) + 16 * U)
                sp.dma_start(ea_rows[ds(turn * (U * P), U * P)].rearrange("(u p) d -> p u d", p=P),
                             ef[:, w]).then_inc(ef_stored, 16)
                sp.wait_ge(g2_ready, turn * U + 2 * U)
                sp.dma_start(g2[ds(turn * (U * P), U * P)].rearrange("(u p) d -> p u d", p=P),
                             g2s[:]).then_inc(g2_stored, 16)
                if k is not None:
                    sp.wait_ge(plain_stored, turn * 16 + 32)
                    sp.sem_inc(plain_free, 1)
                sp.wait_ge(g2_stored, turn * 16 + 16)
                sp.sem_inc(g2_free, 1)
                sp.wait_ge(ef_stored, turn * 16 + 16)
                sp.sem_inc(ef_free, 1)

            keep_next(0, 0, 0)
            sp.wait_ge(plain_stored, 16)
            sp.sem_inc(plain_free, 1)
            ahead(sp, lambda turn, k, use: None, layer1)
            def store_x1(turn, k, use):
                sp.wait_ge(x1_ready, turn + (CHUNKS + TURNS + 1))
                sp.dma_start(x1_rows[ds(turn * (U * P), U * P)].rearrange("(u p) d -> p u d", p=P),
                             res[:, 1 + k]).then_inc(x1_stored, 16)
                sp.wait_ge(x1_stored, turn * 16 + 16)
                sp.sem_inc(x1_free, 1)

            pipelined(sp, store_x1)

            def load_ea(turn, k, use):
                if not isinstance(turn, int) or turn >= 2:
                    sp.wait_ge(msg_ready, turn + (T + TURNS))
                sp.dma_start(ea[:, k], ea_rows[ds(turn * (U * P), U * P)].rearrange("(u p) d -> p u d", p=P)).then_inc(e_in[k], 16)

            pipelined(sp, load_ea)

        @block.gpsimd
        def _(pool):
            gp = nc.gpsimd
            gp.memset(zero[:], 0.0)
            gp.memset(ones[:], 1.0)
            gp.memset(ident[:], 0.0).then_inc(pool_step, 1)
            pool.wait_ge(pool_step, 1)
            gp.affine_select(out=ident[:], in_=ident[:], compare_op=ALU.not_equal, fill=1.0, base=0,
                            pattern=[[-1, 128]], channel_multiplier=1)
            gp.memset(before[:, 0:(U - 1) * P], 1.0)
            gp.affine_select(out=before[:, (U - 1) * P:], in_=ones[0:P, 0:P], compare_op=ALU.is_gt, fill=0.0, base=0,
                            pattern=[[-1, P]], channel_multiplier=1)
            gp.affine_select(out=above[:], in_=ones[:, 0:128], compare_op=ALU.is_gt, fill=0.0, base=0,
                            pattern=[[1, 128]], channel_multiplier=-1)
            gp.affine_select(out=shift[:], in_=ones[0:P, 0:P], compare_op=ALU.is_equal, fill=0.0, base=-1,
                            pattern=[[-1, P]], channel_multiplier=1)
            gp.affine_select(out=wrap[:], in_=ones[0:P, 0:P], compare_op=ALU.is_equal, fill=0.0, base=P - 1,
                            pattern=[[-1, P]], channel_multiplier=P)
            gp.affine_select(out=pick_last[:], in_=ones[0:P, 0:P], compare_op=ALU.is_equal, fill=0.0, base=-(P - 1),
                            pattern=[[0, P]], channel_multiplier=1)
            gp.affine_select(out=pick_first[:], in_=ones[0:P, 0:P], compare_op=ALU.is_equal, fill=0.0, base=0,
                            pattern=[[0, P]], channel_multiplier=1)
            gp.memset(ones16[:], 1.0)
            gp.memset(ln_eps[:], 1e-5)
            gp.memset(ends2[:], -2.0)
            gp.memset(agg[:], 0.0)
            gp.memset(agg2[:], 0.0)
            gp.memset(key_pad[:], -1.0)
            gp.iota(digits[:], [[1, LO]], base=0, channel_multiplier=0, allow_small_or_imprecise_dtypes=True)
            gp.iota(slot_no[:], [[P, T]], base=0, channel_multiplier=1, allow_small_or_imprecise_dtypes=True)
            gp.iota(edge_no[:], [[1, T]], base=0, channel_multiplier=T,
                   allow_small_or_imprecise_dtypes=True).then_inc(pool_step, 1)
            pool.wait_ge(pool_step, 2)
            gp.tensor_copy(ident16[:], ident[:]).then_inc(consts_ready, 1)
            def split_run(count, w):
                pool.wait_ge(run_cast, count)
                gp.tensor_tensor(run16[:, w, 1], start_tab, run16[:, w, 0], ALU.subtract).then_inc(run_split, 1)

            ahead(pool, lambda turn, w, use: split_run(1, w),
                  lambda turn, nxt, use: split_run(turn + 2, nxt) if nxt is not None else None)

            pool.wait_ge(rows_to_move, 1)
            pool.wait_ge(meta_zeroed, 64)
            with pool.Fori(0, T // SC) as turn:
                t0 = turn * SC
                for k in range(2):
                    gp.tensor_copy(move_idx[:, k], addr_i[:, k, ds(t0, SC)])
                    last = gp.tensor_copy(move_row[:, k], rowdata[:, k, ds(t0, SC), :])
                last.then_inc(move_slots, 1)
                pool.wait_ge(move_slots, turn + 1)
                pool.sem_inc(pool_go, 1)
                for j in range(SC):
                    for k, tabs in enumerate((meta_src, meta_dst)):
                        if j >= 2:
                            pool.wait_ge(moved[k][j % 2], turn * (8 * SC) + 16 * (j // 2))
                            pool.sem_inc(pool_go, 1)
                        gp.indirect_dma_start(
                            out=tabs[j % 2], out_offset=bass.IndirectOffsetOnAxis(ap=move_idx[:, k, j:j + 1], axis=0),
                            in_=move_row[:, k, j], in_offset=None).then_inc(moved[k][j % 2], 16)
                for k in range(2):
                    for h in range(2):
                        pool.wait_ge(moved[k][h], turn * (8 * SC) + 8 * SC)
                        pool.sem_inc(pool_go, 1)


            pool.wait_ge(lists_ready, 1)

            def get_x(turn, k, first):
                if not first:
                    pool.wait_ge(xt_ready, turn * 2 - 1)
                    pool.sem_inc(pool_go, 1)
                    pool.wait_ge(x_plus_elu, turn + (CHUNKS - 1))
                    pool.sem_inc(pool_go, 1)
                    pool.wait_ge(xs_free, turn)
                    pool.sem_inc(pool_go, 1)
                gp.tensor_copy(slots_a[:, k], meta_i[:, 0, ds(turn * U, U), 0:2]).then_inc(aslots_ready, 1)
                pool.wait_ge(aslots_ready, turn + 1)
                pool.sem_inc(pool_go, 1)
                for j in range(U):
                    for c, rows in enumerate((xs, xd)):
                        gp.indirect_dma_start(
                            out=rows[:, k, j], out_offset=None, in_=x,
                            in_offset=bass.IndirectOffsetOnAxis(ap=slots_a[:, k, j, c:c + 1], axis=0)).then_inc(x_in[k], 16)

            def get_e(turn, k, first):
                if not first:
                    pool.wait_ge(ef_free, turn - 1)
                    pool.sem_inc(pool_go, 1)
                gp.tensor_copy(slots_e[:, k], meta_i[:, 1, ds(turn * U, U), 3]).then_inc(eslots_ready, 1)
                pool.wait_ge(eslots_ready, turn + 1)
                pool.sem_inc(pool_go, 1)
                for j in range(U):
                    gp.indirect_dma_start(
                        out=ef[:, k, j], out_offset=None, in_=edge_attr,
                        in_offset=bass.IndirectOffsetOnAxis(ap=slots_e[:, k, j:j + 1], axis=0)).then_inc(ef_in[k], 16)

            pool.wait_ge(x_plus_elu, CHUNKS)
            pool.sem_inc(pool_go, 1)
            get_x(0, 0, True)
            get_x(1, 1, True)
            for k in range(2, 4):
                pool.wait_ge(out_stored[k], 16 * (CHUNKS // 4))
                pool.sem_inc(pool_go, 1)
            get_e(0, 0, True)
            get_x(2, 0, False)
            get_e(1, 1, True)
            with pool.Fori(0, TURNS // 2 - 1) as pair:
                for half in range(2):
                    get_x(pair * 2 + (half + 3), 1 - half, False)
                    get_e(pair * 2 + (half + 2), half, False)
            get_e(TURNS - 1, 0, False)
            pool.wait_ge(g2_stored, 16 * TURNS)
            pool.sem_inc(pool_go, 1)
            pool.wait_ge(zero_row_stored, 16)
            pool.sem_inc(pool_go, 1)

            def g_slots(turn, k):
                pool.wait_ge(msg_ready, turn + T)
                pool.sem_inc(pool_go, 1)
                gp.tensor_copy(slots_b[:, k], meta_i[:, 0, ds(turn * U, U), 2]).then_inc(bslots_ready, 1)
                pool.wait_ge(bslots_ready, turn + 1)
                pool.sem_inc(pool_go, 1)

            def get_g(k, j):
                gp.indirect_dma_start(
                    out=g[:, k, j], out_offset=None, in_=g2,
                    in_offset=bass.IndirectOffsetOnAxis(ap=slots_b[:, k, j:j + 1], axis=0)).then_inc(g_in[k], 16)

            def out_slots(turn, list_no):
                gp.tensor_copy(slots_c[:], out_row[:, list_no, ds(turn * U, U)]).then_inc(cslots_ready, 1)
                pool.wait_ge(cslots_ready, turn + (TURNS * list_no + 1))
                pool.wait_ge(y_out, turn + (CHUNKS + TURNS * list_no + 1))
                pool.sem_inc(pool_go, 1)

            def put(turn, list_no, k, j, meanwhile):
                gp.indirect_dma_start(
                    out=out, out_offset=bass.IndirectOffsetOnAxis(ap=slots_c[:, j:j + 1], axis=0),
                    in_=outb[:, k, j], in_offset=None, bounds_check=N - 1, oob_is_err=False).then_inc(row_out, 16)
                meanwhile()
                pool.wait_ge(row_out, (turn * U + j) * 16 + (16 * T * list_no + 16))
                pool.sem_inc(row_free, 1)

            for turn in range(4):
                g_slots(turn, turn % 2)
                for j in range(U):
                    get_g(turn % 2, j)
            for k in range(4):
                pool.wait_ge(out_stored[k], 16 * (CHUNKS // 4))

            def put_get_g(turn, k):
                g_slots(turn + 4, k)
                out_slots(turn, 0)
                for j in range(U):
                    put(turn, 0, k, j, lambda: get_g(k, j))

            with pool.Fori(0, (TURNS - 5) // 2) as pair:
                for k in range(2):
                    put_get_g(pair * 2 + k, k)
            put_get_g(TURNS - 5, 0)

            def d_slots(turn, k):
                if not isinstance(turn, int) or turn >= 2:
                    pool.wait_ge(msg_ready, turn + (T + TURNS))
                    pool.sem_inc(pool_go, 1)
                gp.tensor_copy(slots_d[:, k], meta_i[:, 1, ds(turn * U, U), 1:3]).then_inc(dslots_ready, 1)
                pool.wait_ge(dslots_ready, turn + 1)
                pool.sem_inc(pool_go, 1)

            def get_d(turn, k, half):
                if half == 1 and (not isinstance(turn, int) or turn >= 2):
                    pool.wait_ge(hin_ready, turn - 1)
                    pool.sem_inc(pool_go, 1)
                    pool.wait_ge(b_kept, turn - 1)
                    pool.sem_inc(pool_go, 1)

                def tile(j):
                    gp.indirect_dma_start(
                        out=(ra, xb)[half][:, k, j], out_offset=None, in_=x1_rows,
                        in_offset=bass.IndirectOffsetOnAxis(ap=slots_d[:, k, j, half:half + 1], axis=0)).then_inc((a_in, b_in)[half][k], 16)
                return tile

            def put_and_get(turn, list_no, out_k, new_turn, k):
                out_slots(turn, list_no)
                for j in range(U):
                    if j % 2 == 0:
                        tile = get_d(new_turn, k, j // 2)
                    put(turn, list_no, out_k, j, lambda: (tile(j % 2 * 2), tile(j % 2 * 2 + 1)))

            for turn in (TURNS - 4, TURNS - 3):
                out_slots(turn, 0)
                for j in range(U):
                    put(turn, 0, turn % 2, j, lambda: None)
            pool.wait_ge(plain_stored, 16 * TURNS)
            pool.sem_inc(pool_go, 1)
            pool.wait_ge(x1_stored, 16 * TURNS)
            pool.sem_inc(pool_go, 1)
            for turn in range(2):
                d_slots(turn, turn)
                for half in range(2):
                    tile = get_d(turn, turn, half)
                    for j in range(U):
                        tile(j)
            for turn in range(2):
                d_slots(turn + 2, turn)
                put_and_get(turn + TURNS - 2, 0, 1 - turn, turn + 2, turn)

            def put_get_d(turn, k):
                d_slots(turn + 4, k)
                put_and_get(turn, 1, 1 - k, turn + 4, k)

            with pool.Fori(0, (TURNS - 5) // 2) as pair:
                for k in range(2):
                    put_get_d(pair * 2 + k, k)
            put_get_d(TURNS - 5, 0)
            for turn in range(TURNS - 4, TURNS):
                out_slots(turn, 1)
                for j in range(U):
                    put(turn, 1, (turn + 1) % 2, j, lambda: None)

        @block.vector
        def _(dve):
            v = nc.vector

            flat = "p u d -> p (u d)"

            def node_min(n, xv, ex, u):
                dve.wait_ge(x_exp, n + 1)
                v.scalar_tensor_tensor(u.rearrange(flat), ex.rearrange(flat), 1.0, xv.rearrange(flat),
                                       ALU.min, ALU.add).then_inc(x_half, 1)

            def node_max(n, xv, u):
                dve.wait_ge(x_half, n + 1)
                v.scalar_tensor_tensor(u.rearrange(flat), xv.rearrange(flat), 0.0, u.rearrange(flat),
                                       ALU.max, ALU.add).then_inc(x_plus_elu, 1)

            def node_sum(n, xv, ex, u):
                node_min(n, xv, ex, u)
                node_max(n, xv, u)
                dve.wait_ge(x_plus_elu, n + 1)
                node_stats(n, u)

            def node_stats(n, u):
                for j in range(U):
                    last = v.bn_stats(stats[:, 0, j], u[:, j])
                last.then_inc(x_stats, 1)

            def node_moments(n, k):
                dve.wait_ge(x_stats, n + 1)
                dve.sem_inc(dve_go, 1)
                for j in range(U):
                    last = v.bn_aggr(moment[:, k, j], stats[:, 0, j])
                last.then_inc(x_moments, 1)

            def node_x1(n, u, k):
                dve.wait_ge(x_rstd, n + 1)
                for j in range(U):
                    last = v.tensor_scalar(u[:, j], u[:, j], moment[:, k, j, 0:1], rstd[:, k, j:j + 1],
                                           ALU.subtract, ALU.mult)
                last.then_inc(x1_ready, 1)

            def result_add(n, r, k):
                dve.wait_ge(y_psum, n + 1)
                v.tensor_tensor(post_sum[:, k % 2].rearrange(flat), pb[7][0:P, :], r.rearrange(flat), ALU.add).then_inc(y_sum, 1)

            def result_stats(n, k):
                dve.wait_ge(y_sum, n + 2)
                for j in range(U):
                    last = v.bn_stats(post_stat[:, 0, j], post_sum[:, k % 2, j])
                last.then_inc(y_stats, 1)

            def result_moments(n, k):
                dve.wait_ge(y_stats, n + 1)
                dve.sem_inc(dve_go, 1)
                for j in range(U):
                    last = v.bn_aggr(post_moment[:, k, j], post_stat[:, 0, j])
                last.then_inc(y_moments, 1)

            def result_sum(n, r, k):
                result_add(n, r, k)
                result_stats(n, k)
                result_moments(n, k)

            def result(n, k):
                dve.wait_ge(y_rstd, n + 1)
                for j in range(U):
                    last = v.tensor_scalar(outb[:, k, j], post_sum[:, k % 2, j], post_moment[:, k, j, 0:1],
                                           post_rstd[:, k, j:j + 1], ALU.subtract, ALU.mult)
                last.then_inc(y_out, 1)

            dve.wait_ge(keys_loaded, 32)
            v.tensor_scalar(digit_i[:, :, 0], key_i[:], 8, None, ALU.logical_shift_right)
            v.tensor_scalar(digit_i[:, :, 1], key_i[:], LO - 1, None, ALU.bitwise_and).then_inc(digits_int, 1)
            v.tensor_copy(key[:], key_i[:])
            dve.wait_ge(digits_int, 1)
            v.tensor_copy(digit[:], digit_i[:]).then_inc(digits_ready, 1)
            dve.wait_ge(digits_ready, 1)
            v.tensor_copy(key16[:, 0], key[:]).then_inc(digits_ready, 1)
            dve.wait_ge(digits_ready, 2)
            v.tensor_tensor(key16[:, 1], key[:], key16[:, 0], ALU.subtract).then_inc(digits_ready, 1)
            dve.wait_ge(consts_ready, 1)

            def one_hots(turn, j, k, w):
                t = turn * U + j
                v.tensor_scalar(hot[:, w, j, k, 0:HI], digits[:, 0:HI], digit[:, k, 0, ds(t, 1)], None, ALU.is_equal)
                return v.tensor_scalar(hot[:, w, j, k, HI:], digits[:], digit[:, k, 1, ds(t, 1)], None, ALU.is_equal)

            with dve.Fori(0, TURNS) as turn:
                for j in range(U):
                    dve.wait_ge(count_hot_used, turn * U + j + 1)
                    for k in range(2):
                        last = one_hots(turn, j, k, 0)
                    last.then_inc(count_hot_ready, 1)
            dve.wait_ge(degrees_ready, 1)
            for k in range(2):
                last = v.tensor_copy(deg[:, k].rearrange("p h l -> p (h l)"), pb[k][0:HH, :])
            last.then_inc(table_step, 1)
            dve.wait_ge(table_step, 1)
            for k in range(2):
                for h in range(2):
                    last = v.tensor_tensor_scan(cum[:, k, h], ones[0:HH, 0:LO], deg[:, k, h], 0.0, ALU.mult, ALU.add)
            last.then_inc(table_step, 1)
            dve.wait_ge(table_step, 2)
            v.tensor_copy(rowsum[:], cum[:, :, :, LO - 1]).then_inc(table_step, 1)
            dve.wait_ge(bases_ready, 1)
            v.tensor_copy(base[:], pb[2][0:HH, 0:4].rearrange("p (k h) -> p k h", k=2)).then_inc(table_step, 1)
            dve.wait_ge(table_step, 4)
            v.tensor_tensor(base[:, :, 1], base[:, :, 1], pb[2][0:HH, 4:6], ALU.add).then_inc(table_step, 1)
            dve.wait_ge(table_step, 5)
            for k in range(2):
                for h in range(2):
                    last = v.tensor_scalar(cum[:, k, h], cum[:, k, h], base[:, k, h:h + 1], None, ALU.add)
            last.then_inc(table_step, 1)
            dve.wait_ge(table_step, 6)
            v.tensor_tensor(start_tab[:], cum[:], deg[:], ALU.subtract)
            v.tensor_scalar(ends_tmp[:, 0], cum[:, 0], -1.0 - NONE, None, ALU.add)
            v.tensor_scalar(ends_tmp[:, 1], deg[:, 0], 0.0, None, ALU.is_gt).then_inc(table_step, 1)
            dve.wait_ge(table_step, 7)
            v.tensor_tensor(ends_tmp[:, 0], ends_tmp[:, 0], ends_tmp[:, 1], ALU.mult).then_inc(table_step, 1)
            dve.wait_ge(table_step, 8)
            v.tensor_scalar(end_tab[:], ends_tmp[:, 0], NONE, None, ALU.add).then_inc(table_step, 1)
            dve.wait_ge(table_step, 9)
            v.tensor_copy(end16[:, 0], end_tab[:]).then_inc(table_step, 1)
            dve.wait_ge(table_step, 10)
            v.tensor_tensor(end16[:, 1], end_tab[:], end16[:, 0], ALU.subtract).then_inc(tables_ready, 1)

            def tile_hots(turn, j, w):
                for k in range(2):
                    last = v.tensor_scalar(hot[:, w, j, k, HI:], digits[:], digit[:, k, 1, ds(turn * U + j, 1)], None, ALU.is_equal)
                if j == U - 1:
                    last.then_inc(hot_ready, 1)

            def rank(turn, j):
                if j == 0:
                    dve.wait_ge(rows_ready, turn + 1)
                    dve.wait_ge(found_kept, turn + 1)
                dve.wait_ge(ranks_done, turn * U + (j + 1))
                for k in range(2):
                    last = v.scalar_tensor_tensor(junk2[:, j % 2, k, 0:(j + 1) * P], pb[3 + k][0:P, 0:(j + 1) * P],
                                                  key[:, k, ds(turn * U + j, 1)], before[:, (U - 1 - j) * P:],
                                                  ALU.is_equal, ALU.mult, accum_out=found[:, j, 4 + k:5 + k])
                last.then_inc(ranks_done, 1)

            def read_tables(turn, j, w):
                dve.wait_ge(run_used, turn * U + (j + 1))
                for tables, used, c0, tab_bank in ((end_found, end_used, 2, pb[7]), (run_found, run_used, 0, pb[5 + j % 2])):
                    dve.wait_ge(tables, turn * U + (j + 1))
                    for c in range(2):
                        last = v.tensor_tensor_reduce(out=junk[:, j % 2, c0 + c], in0=tab_bank[0:P, c * LO:(c + 1) * LO],
                                                      in1=hot[:, w, j, c, HI:], scale=1.0, scalar=0.0, op0=ALU.mult,
                                                      op1=ALU.add, accum_out=found[:, j, c0 + c:c0 + c + 1])
                    last.then_inc(used, 1)

            def places(turn, nxt, use):
                w = 0 if nxt is None else 1 - nxt

                def next_hots(j):
                    if nxt is not None:
                        tile_hots(turn + 1, j, nxt)

                next_hots(0)
                next_hots(1)
                dve.wait_ge(counted, turn + 1)
                dve.wait_ge(run_split, turn + 1)
                for k in range(2):
                    run = start_tab[:, k].rearrange("p h l -> p (h l)")
                    last = v.tensor_tensor(run, pb[k][0:HH, :], run, ALU.add)
                last.then_inc(run_updated, 1)
                for j in range(U):
                    rank(turn, j)
                    read_tables(turn, j, w)
                    if j < 2:
                        next_hots(2 + j)
                dve.wait_ge(run_used, turn * U + (U + 2))
                v.tensor_copy(keep[:, ds(turn * U, U), :], found[:]).then_inc(found_kept, 1)

            def first_hots(turn, w, use):
                for j in range(U):
                    tile_hots(turn, j, w)

            dve.wait_ge(count_hot_used, T + U)
            ahead(dve, first_hots, places)

            dve.wait_ge(found_kept, TURNS + 1)

            def step(ins, n):
                ins.then_inc(bulk_step, 1)
                dve.wait_ge(bulk_step, n)

            for k in range(2):
                last = v.tensor_tensor(pos[:, k], keep[:, :, k], keep[:, :, 4 + k], ALU.add)
            step(last, 1)
            step(v.tensor_scalar(q[:], pos[:], -float(P // 2), 1.0 / P, ALU.add, ALU.mult), 2)
            step(v.tensor_scalar(q[:], q[:], ROUND, None, ALU.add), 3)
            step(v.tensor_scalar(q[:], q[:], ROUND, None, ALU.subtract), 4)
            step(v.tensor_scalar(q[:], q[:], -(P * T - 1.0), None, ALU.mult), 5)
            step(v.scalar_tensor_tensor(q[:], pos[:], float(T), q[:], ALU.mult, ALU.add), 6)
            v.tensor_copy(addr_i[:], q[:])
            v.tensor_copy(rowdata[:, 0, :, 0], key[:, 0])
            v.tensor_copy(rowdata[:, 0, :, 1], key[:, 1])
            v.tensor_copy(rowdata[:, 0, :, 2], keep[:, :, 3])
            v.tensor_copy(rowdata[:, 0, :, 3], keep[:, :, 2])
            v.tensor_copy(rowdata[:, 1, :, 0], key[:, 1])
            v.tensor_copy(rowdata[:, 1, :, 1], keep[:, :, 2])
            v.tensor_copy(rowdata[:, 1, :, 3], edge_no[:])
            step(v.scalar_tensor_tensor(rowdata[:, 1, :, 2], keep[:, :, 3], NONE, pos[:, 0],
                                        ALU.is_equal, ALU.mult), 7)
            v.tensor_tensor(rowdata[:, 1, :, 2], rowdata[:, 1, :, 2], keep[:, :, 3], ALU.add).then_inc(rows_to_move, 1)

            dve.wait_ge(weights_loaded, 9 * 16)
            for k in range(2):
                v.tensor_tensor(wa_tmp[:, k], w1g[:], a1b[:, :, k * FH:(k + 1) * FH], ALU.mult)
                last = v.tensor_tensor(w2_tmp[:, k], w2g[:, :, 0:D],
                                       a2b[:, k * D:(k + 1) * D].unsqueeze(1).broadcast_to([128, C2, D]), ALU.mult)
            v.tensor_scalar(eps1[:], eps1[:], 1.0, None, ALU.add).then_inc(weights_step, 1)
            dve.wait_ge(weights_step, 1)
            for k in range(2):
                v.tensor_reduce(wa[:, k], wa_tmp[:, k], AX.X, ALU.add)
                last = v.tensor_reduce(w2g[:, :, D + k], w2_tmp[:, k], AX.X, ALU.add)

            def part_step(ins, n):
                ins.then_inc(weights_step, 1)
                dve.wait_ge(weights_step, n)

            part_step(v.tensor_copy(b2_part[:, 0], b2[:]), 2)
            part_step(v.tensor_tensor(b2_rest[:, 0], b2[:], b2_part[:, 0], ALU.subtract), 3)
            part_step(v.tensor_copy(b2_part[:, 1], b2_rest[:, 0]), 4)
            part_step(v.tensor_tensor(b2_rest[:, 1], b2_rest[:, 0], b2_part[:, 1], ALU.subtract), 5)
            part_step(v.tensor_scalar(b2_rest[:, 2], b2_part[:, 0], ident[0:3, 0:1], None, ALU.mult), 6)
            part_step(v.scalar_tensor_tensor(b2_rest[:, 2], b2_part[:, 1], ident[0:3, 1:2], b2_rest[:, 2], ALU.mult, ALU.add), 7)
            v.scalar_tensor_tensor(b2_parts[:], b2_rest[:, 1], ident[0:3, 2:3], b2_rest[:, 2], ALU.mult, ALU.add).then_inc(weights_ready, 1)

            def y_bias_of(n, k):
                dve.wait_ge(y_rstd, n + 1)
                v.scalar_tensor_tensor(post_bias[:, k], post_moment[:, k, :, 0], -1.0, post_rstd[:, k],
                                       ALU.mult, ALU.mult).then_inc(y_bias, 1)

            def x_sum(n, k):
                node_sum(n, xin[:, k], xex[:, k], res[:, k])
                node_moments(n, k)

            def node_group(n, k, use):
                if there(n, -1):
                    y_bias_of(n - 1, (k + 3) % 4)
                if there(n, -2):
                    dve.wait_ge(y_out, n - 1)
                result_add(n, res[:, k], k)
                if there(n, 3):
                    node_x1(n + 3, res[:, (k + 3) % 4], (k + 3) % 4)
                result_stats(n, k)
                if there(n, 4):
                    node_min(n + 4, xin[:, k], xex[:, k], res[:, k])
                result_moments(n, k)
                if there(n, 4):
                    node_max(n + 4, xin[:, k], res[:, k])
                    dve.wait_ge(x_plus_elu, n + 5)
                    node_stats(n + 4, res[:, k])
                    node_moments(n + 4, k)

            for n in range(4):
                x_sum(n, n)
                if n < 3:
                    node_x1(n, res[:, n], n)
            def lists():
                dve.wait_ge(meta_loaded, 64)
                v.tensor_tensor(meta[:], meta_in[:, :, 0], meta_in[:, :, 1], ALU.add).then_inc(meta_ready, 1)
                dve.wait_ge(meta_ready, 1)

                step(v.tensor_copy(key_pad[:, :, 1:T + 1], meta[:, :, :, 0]), 8)
                step(v.tensor_copy(meta_i[:], meta[:]), 9)
                dve.wait_ge(next_psum, 1)
                step(v.tensor_tensor(next_key[:], pb[2][0:P, 0:2 * T].rearrange("p (k t) -> p k t", k=2),
                                     key_pad[:, :, 1:T + 1], ALU.is_equal), 10)
                step(v.scalar_tensor_tensor(next_key[:], next_key[:], float(4 * N), key_pad[:, :, 1:T + 1],
                                            ALU.mult, ALU.add), 11)
                step(v.tensor_copy(key16[:, 0], key_pad[:, :, 1:T + 1]), 12)
                v.tensor_tensor(key16[:, 1], key_pad[:, :, 1:T + 1], key16[:, 0], ALU.subtract)
                v.tensor_copy(out_row[:], next_key[:]).then_inc(lists_ready, 1)

            each_group(dve, node_group, lists)
            y_bias_of(CHUNKS - 1, 3)

            def same_keys(turn, list_no, w, count):
                dve.wait_ge(key_rows, count)
                for j in range(U):
                    row = pb[2][0:P, j * P:(j + 1) * P]
                    v.tensor_scalar(same_of[w][:, j], row, key_pad[:, list_no, ds(turn * U + (j + 1), 1)], None, ALU.is_equal)
                    last = v.tensor_scalar(carry_of[w][:, j], row, key_pad[:, list_no, ds(turn * U + j, 1)], pick_last[:, 0:1],
                                           ALU.is_equal, ALU.mult)
                last.then_inc(same_ready, 1)

            def message(turn, j):
                dve.wait_ge(esc_ready, turn + 1)
                dve.wait_ge(h_psum, turn * U + (j + 1))
                v.tensor_tensor(msg[:, j % 2].rearrange("p (h f) -> p h f", h=HEADS),
                                pb[4 + j % 2][0:P, :].rearrange("p (h f) -> p h f", h=HEADS),
                                esc[:, j].unsqueeze(2).broadcast_to([P, HEADS, FH]), ALU.mult).then_inc(msg_ready, 1)

            def mean(turn, j):
                dve.wait_ge(agg_ready, turn * U + (j + 2))
                v.tensor_scalar(rsum[:, j], agg[:, j, HEADS * FH:], 1e-16, None, ALU.add).then_inc(rsum_step, 1)
                dve.wait_ge(rsum_step, turn * U + (j + 1))
                v.reciprocal(rsum[:, j], rsum[:, j]).then_inc(rsum_ready, 1)
                dve.wait_ge(rsum_ready, turn * U + (j + 1))
                v.tensor_tensor(hp[:, j % 2].rearrange("p (h f) -> p h f", h=HEADS),
                                agg[:, j, 0:HEADS * FH].rearrange("p (h f) -> p h f", h=HEADS),
                                rsum[:, j].unsqueeze(2).broadcast_to([P, HEADS, FH]), ALU.mult).then_inc(hp_ready, 1)

            def elu(turn, j):
                dve.wait_ge(hex_ready, turn * U + (j + 1))
                v.tensor_scalar(hex_[:, j % 2], hex_[:, j % 2], 1.0, -1.0, ALU.min, ALU.add).then_inc(helu_half, 1)
                dve.wait_ge(helu_half, turn * U + (j + 1))
                v.scalar_tensor_tensor(hex_[:, j % 2], hp[:, j % 2], 0.0, hex_[:, j % 2], ALU.max, ALU.add).then_inc(helu_ready, 1)

            def scores_of(turn):
                dve.wait_ge(scores_psum, turn + 1)
                scores = pb[3][0:P, 256:256 + U * HEADS]
                lr_flat = lr[:].rearrange("p u h -> p (u h)")
                v.tensor_scalar(lr_flat, scores, 0.2, None, ALU.mult).then_inc(lr_half, 1)
                dve.wait_ge(lr_half, turn + 1)
                v.tensor_tensor(lr_flat, lr_flat, scores, ALU.max).then_inc(lr_ready, 1)

            def plain_sum(turn, k):
                dve.wait_ge(plain_free, turn + 1)
                node_sum(turn + CHUNKS, xd[:, k], xex[:, 0], res[:, 0])
                node_moments(turn + CHUNKS, 0)

            def layer1_first(turn, k, use):
                same_keys(turn, 0, 0, turn + 1)
                scores_of(turn)
                plain_sum(turn, k)
                message(turn, 0)
                message(turn, 1)
                mean(turn, 0)
                node_x1(turn + CHUNKS, res[:, 0], 0)

            def layer1(turn, k, use):
                message(turn, 2)
                elu(turn, 0)
                mean(turn, 1)
                message(turn, 3)
                elu(turn, 1)
                mean(turn, 2)
                elu(turn, 2)
                mean(turn, 3)
                if k is None:
                    elu(turn, 3)
                    return
                scores_of(turn + 1)
                elu(turn, 3)
                same_keys(turn + 1, 0, 0, turn + 2)
                message(turn + 1, 0)
                message(turn + 1, 1)
                plain_sum(turn + 1, k)
                mean(turn + 1, 0)
                node_x1(turn + (CHUNKS + 1), res[:, 0], 0)

            ahead(dve, layer1_first, layer1)

            dve.wait_ge(s2_rows, 1)
            v.tensor_copy(ends2[:, 0, :, 0:T], pb[2][0:P, 0:2 * T].rearrange("p (k t) -> p k t", k=2))
            v.tensor_copy(ends2[:, 1, :, 0:T], pb[2][0:P, 2 * T:4 * T].rearrange("p (k t) -> p k t", k=2)).then_inc(s2_step, 1)
            dve.wait_ge(s2_step, 1)

            def s2_do(ins, n):
                ins.then_inc(s2_step, 1)
                dve.wait_ge(s2_step, n)

            v.tensor_tensor(cont[:], ends2[:, 0, 1, 0:T], ends2[:, 1, 1, 1:T + 1], ALU.is_equal)
            v.tensor_tensor(cover[:], ends2[:, 0, 1, 0:T], ends2[:, 0, 1, 1:T + 1], ALU.is_equal)
            s2_do(v.tensor_tensor(tail[:], ends2[:, 1, 0, 1:T + 1], ends2[:, 0, 0, 0:T], ALU.subtract), 2)
            s2_do(v.tensor_tensor(tail[:], tail[:], cont[:], ALU.mult), 3)
            s2_do(v.tensor_tensor(tail[:], tail[:], ends2[:, 0, 0, 0:T], ALU.add), 4)
            s2_do(v.tensor_scalar(cont[:], cover[:], -1.0, 1.0, ALU.mult, ALU.add), 5)
            s2_do(v.tensor_tensor(tail[:], tail[:], cont[:], ALU.mult), 6)
            v.tensor_copy(cont[:], cover[:, ::-1])
            s2_do(v.tensor_copy(ends2[:, 1, 0, 0:T], tail[:, ::-1]), 7)
            s2_do(v.tensor_tensor_scan(after[:], cont[:], ends2[:, 1, 0, 0:T], 0.0, ALU.mult, ALU.add), 8)
            s2_do(v.tensor_tensor(tail[:], after[:, ::-1], s2_all[:], ALU.subtract), 9)
            s2_do(v.tensor_tensor(cont[:], key_pad[:, 0, 1:T + 1], ends2[:, 0, 1, 0:T], ALU.is_equal), 10)
            s2_do(v.tensor_tensor(tail[:], tail[:], cont[:], ALU.mult), 11)
            v.tensor_tensor(s2_src[:], tail[:], s2_all[:], ALU.add).then_inc(s2_ready, 1)
            dve.wait_ge(s2_ready, 1)

            def old_sum(turn, list_no, k, r):
                dve.wait_ge(y_out, turn + (CHUNKS + TURNS * list_no))
                result_sum(turn + (CHUNKS + TURNS * list_no), r, k)

            def old_result(turn, list_no, k):
                dve.wait_ge(row_free, turn * U + (T * list_no + 1))
                result(turn + (CHUNKS + TURNS * list_no), k)

            def scores2_of(turn, k, use):
                dve.wait_ge(g_in[k], use * (16 * U) + 16 * U)
                v.tensor_tensor(sc2[:, 0], g[:, k, :, D + 1], s2_src[:, ds(turn * U, U)], ALU.add).then_inc(sc2_a, 1)
                dve.wait_ge(sc2_a, turn + 1)
                v.tensor_scalar(sc2[:, 1], sc2[:, 0], 0.2, None, ALU.mult).then_inc(sc2_b, 1)
                dve.wait_ge(sc2_b, turn + 1)
                v.tensor_tensor(sc2[:, 0], sc2[:, 0], sc2[:, 1], ALU.max).then_inc(sc2_ready, 1)

            def layer2(turn, k, use):
                group = turn + (CHUNKS + TURNS)
                old = not isinstance(turn, int) or turn >= 2
                dve.wait_ge(e2_ready, turn + 1)
                for j in range(U):
                    last = v.tensor_scalar(msg2[:, j, 0:D], g[:, k, j, 0:D], msg2[:, j, D:D + 1], None, ALU.mult)
                last.then_inc(msg_ready, 1)
                if old:
                    old_sum(turn - 2, 0, k, res[:, 1 + k])
                if isinstance(turn, int) and turn == TURNS - 1:
                    same_keys(0, 1, 1 - k, 2 * TURNS + 1)
                else:
                    same_keys(turn + 1, 0, 1 - k, turn + (TURNS + 2))
                dve.wait_ge(agg_ready, (turn * U) + (T + U + 1))
                v.tensor_scalar(rs2[:, 0], agg2[:, :, D], 1e-16, None, ALU.add).then_inc(rsum_step, 1)
                dve.wait_ge(rsum_step, turn + T + 1)
                v.reciprocal(rs2[:, 1], rs2[:, 0]).then_inc(rsum_ready, 1)
                dve.wait_ge(rsum_ready, turn + T + 1)
                v.tensor_tensor(h2[:], agg2[:, :, 0:D], rs2[:, 1].unsqueeze(2).broadcast_to([P, U, D]),
                                ALU.mult).then_inc(hp_ready, 1)
                if old:
                    old_result(turn - 2, 0, k)
                dve.wait_ge(x_exp, group + 1)
                dve.wait_ge(x1_free, turn + 1)
                x1 = res[:, 1 + k]
                v.scalar_tensor_tensor(x1.rearrange(flat), xex[:, 0].rearrange(flat), 1.0,
                                       xs_all[:, ds(turn * (U * D), U * D)], ALU.min, ALU.add).then_inc(x_half, 1)
                dve.wait_ge(x_half, group + 1)
                v.scalar_tensor_tensor(x1.rearrange(flat), h2[:].rearrange(flat), 0.0, x1.rearrange(flat),
                                       ALU.max, ALU.add).then_inc(x_plus_elu, 1)
                dve.wait_ge(x_plus_elu, group + 1)
                node_stats(group, x1)
                node_moments(group, 0)
                if not isinstance(turn, int) or turn < TURNS - 1:
                    scores2_of(turn + 1, 1 - k, use + k)
                node_x1(group, x1, 0)

            dve.wait_ge(out_free, CHUNKS + 4)
            same_keys(0, 0, 0, TURNS + 1)
            scores2_of(0, 0, 0)
            pipelined(dve, layer2)

            def edge_products(turn, k, use):
                dve.wait_ge(a_in[k], use * (16 * U) + 16 * U)
                dve.wait_ge(b_in[k], use * (16 * U) + 16 * U)
                v.tensor_tensor(sqr[:, 0], ra[:, k], xb[:, k], ALU.mult).then_inc(squares, 1)
                dve.wait_ge(e_in[k], use * 16 + 16)
                v.tensor_tensor(ea[:, k], ea[:, k], ra[:, k], ALU.add).then_inc(relu_step, 1)

            def edge_sums(turn):
                dve.wait_ge(squares, turn * 3 + 3)
                v.tensor_reduce(dots[:], sqr[:], AX.X, ALU.add).then_inc(dots_ready, 1)
                dve.wait_ge(dots_ready, turn + 1)
                v.tensor_scalar(simt[:, 0:2], dots[:, 1:3], 1e-16, None, ALU.max).then_inc(sim_step, 1)

            def edge_mask(turn):
                dve.wait_ge(norm_ready, turn + 1)
                v.reciprocal(simt[:, 0:2], simt[:, 2:4]).then_inc(sim_step, 1)
                dve.wait_ge(sim_step, turn * 6 + 2)
                v.tensor_tensor(simt[:, 0], simt[:, 0], simt[:, 1], ALU.mult).then_inc(sim_step, 1)
                dve.wait_ge(sim_step, turn * 6 + 3)
                v.tensor_tensor(simt[:, 0], simt[:, 0], dots[:, 0], ALU.mult).then_inc(sim_step, 1)
                dve.wait_ge(sim_step, turn * 6 + 4)
                v.tensor_scalar(simt[:, 0], simt[:, 0], 1.0, 0.5, ALU.add, ALU.mult).then_inc(sim_step, 1)
                dve.wait_ge(sim_step, turn * 6 + 5)
                v.tensor_scalar(simt[:, 1], simt[:, 0], 0.5, None, ALU.is_ge).then_inc(sim_step, 1)

            def edge_messages(turn, k):
                dve.wait_ge(sim_step, turn * 6 + 6)
                dve.wait_ge(relu_step, turn + 1)
                for j in range(U):
                    last = v.tensor_scalar(msg2[:, j, 0:D], ea[:, k, j], 0.0, simt[:, 1, j:j + 1], ALU.max, ALU.mult)
                last.then_inc(msg_ready, 1)

            def network2(turn, k, use):
                edge_products(turn, k, use)
                edge_sums(turn)
                edge_mask(turn)
                edge_messages(turn, k)
                if isinstance(turn, int) and turn < 2:
                    old_turn, old_list, x1 = turn + TURNS - 2, 0, res[:, 2 - k]
                else:
                    old_turn, old_list, x1 = turn - 2, 1, xb_kept[:, k]
                old_sum(old_turn, old_list, 1 - k, x1)
                if not isinstance(turn, int) or turn < TURNS - 1:
                    same_keys(turn + 1, 1, k, turn + (2 * TURNS + 2))
                old_result(old_turn, old_list, 1 - k)
                dve.wait_ge(agg_ready, (turn * U) + (2 * T + U + 1))
                dve.wait_ge(hin_turned, turn + (CHUNKS + TURNS))
                v.scalar_tensor_tensor(hin_d[:], xb[:, k], eps1[0:P, 0:1], agg2[:, :, 0:D], ALU.mult, ALU.add).then_inc(hin_ready, 1)

            pipelined(dve, network2)
            for turn in (TURNS - 2, TURNS - 1):
                old_sum(turn, 1, (turn + 1) % 2, xb_kept[:, turn % 2])
                old_result(turn, 1, (turn + 1) % 2)

        @block.tensor
        def _(pe):
            te = nc.tensor
            pe.wait_ge(consts_ready, 1)
            pe.sem_inc(count_hot_used, U)
            pe.wait_ge(hist_open, 1)
            for k in range(2):
                te.matmul(pb[k][0:HH, :], zero[0:1, 0:HH], ones[0:1, :], start=True, stop=False)
            with pe.Fori(0, TURNS) as turn:
                for j in range(U):
                    pe.wait_ge(count_hot_ready, turn * U + j + 1)
                    for k in range(2):
                        for h in range(2):
                            last = te.matmul(pb[k][0:HH, h * LO:(h + 1) * LO], hot[:, 0, j, k, h * HH:(h + 1) * HH],
                                             hot[:, 0, j, k, HI:], start=False, stop=False)
                    last.then_inc(count_hot_used, 1)
            for k in range(2):
                last = te.matmul(pb[k][0:HH, :], zero[0:1, 0:HH], ones[0:1, :], start=False, stop=True)
            last.then_inc(degrees_ready, 1)
            pe.wait_ge(table_step, 3)
            te.matmul(pb[2][0:HH, 0:4], above[0:HH, 0:HH], rowsum[:].rearrange("p k h -> p (k h)"), start=True, stop=True)
            te.matmul(pb[2][0:HH, 4:6], ones[0:HH, 0:HH], rowsum[:, :, 0], start=True, stop=True).then_inc(bases_ready, 1)
            def turn_digits(turn, w, half):
                pe.wait_ge(hot_t_ready, turn * 2 + (half + 1))
                for j in range(2):
                    for k in range(2):
                        for h in range(2):
                            o = 4 * j + 2 * k + h
                            last = te.transpose(hot_t_ps[0:HH, o * 128:o * 128 + P],
                                                hot[:, w, half * 2 + j, k, h * HH:(h + 1) * HH], ident16[0:P, 0:P])
                last.then_inc(hot_t_psum, 1)

            def look_up(out_bank, j, tables):
                for k in range(2):
                    for h in range(2):
                        for d in range(2):
                            last = te.matmul(out_bank[0:P, k * LO:(k + 1) * LO], hot_t[:, j, 2 * k + h, 0:P], tables(d, k, h),
                                             start=(h == 0 and d == 0), stop=(h == 1 and d == 1))
                return last

            def places(turn, nxt, use):
                w = 0 if nxt is None else 1 - nxt
                pe.wait_ge(hot_ready, turn + 1)
                pe.wait_ge(high_ready, turn * U + (U + 2))
                turn_digits(turn, w, 0)
                pe.wait_ge(run_updated, turn + 1)
                for k in range(2):
                    for h in range(2):
                        for j in range(U):
                            last = te.matmul(pb[k][0:HH, h * LO:(h + 1) * LO], hot[:, w, j, k, h * HH:(h + 1) * HH],
                                             hot[:, w, j, k, HI:], start=(j == 0), stop=(j == U - 1))
                last.then_inc(counted, 1)
                turn_digits(turn, w, 1)
                pe.wait_ge(ranks_done, turn * U + 2)
                for k in range(2):
                    for j in range(U):
                        for part in range(2):
                            last = te.matmul(pb[3 + k][0:P, j * P:(j + 1) * P],
                                             key16[:, part, k, ds(turn * U + j, 1)].broadcast_to([P, P]),
                                             ident16[0:P, 0:P], start=(part == 0), stop=(part == 1))
                last.then_inc(rows_ready, 1)
                for j in range(U):
                    if j % 2 == 0:
                        pe.wait_ge(hot_t_ready, turn * 2 + (j // 2 + 2))
                    pe.wait_ge(end_used, turn * U + (j + 1))
                    look_up(pb[7], j, lambda d, k, h: end16[:, d, h]).then_inc(end_found, 1)
                    if j == 0:
                        pe.wait_ge(run_split, turn + 1)
                    pe.wait_ge(run_used, turn * U + (j + 1))
                    look_up(pb[5 + j % 2], j, lambda d, k, h: run16[:, w, d, k, h]).then_inc(run_found, 1)

            pe.wait_ge(tables_ready, 1)
            ahead(pe, lambda turn, w, use: None, places)

            pe.wait_ge(weights_ready, 1)

            def turn_hin(n, src_rows, ready, value):
                pe.wait_ge(ready, value)
                pe.wait_ge(hin_t_ready, n + 1)
                for j in range(U):
                    last = te.transpose(pb[4][:, j * P:(j + 1) * P], src_rows[:, j], ident[0:P, 0:P])
                last.then_inc(hin_turned, 1)

            def hidden_half(n, c):
                pe.wait_ge(hin_t_ready, n + 2)
                pe.wait_ge(hid_ready, n * 2 + (c + 1))
                te.matmul(pb[5 + c][:, 0:U * P], w1m[:, c], hin_t[:], start=True, stop=True).then_inc(hid_psum, 1)

            def hidden(n):
                for c in range(2):
                    hidden_half(n, c)

            def output_tile(n, j, k=0):
                if j == 0:
                    pe.wait_ge(y_sum, n + 1)
                    pe.wait_ge(hid_ready, n * 2 + 4)
                    te.matmul(pb[7][0:P, :], ones16[:], b2_parts[:].unsqueeze(1).broadcast_to([3, U, D]), start=True, stop=False)
                for c in range(2):
                    last = te.matmul(pb[7][0:P, j * D:(j + 1) * D], hid[:, k, c, j * P:(j + 1) * P], w2m[:, c],
                                     start=False, stop=(j == U - 1 and c == 1))
                if j == U - 1:
                    last.then_inc(y_psum, 1)

            def output(n, k=0):
                for j in range(U):
                    output_tile(n, j, k)

            def node_group(n, k, use):
                if there(n, 1):
                    hidden(n + 1)
                output(n, k % 2)
                if there(n, 2):
                    turn_hin(n + 2, res[:, (k + 2) % 4], x1_ready, n + 3)

            for n in range(2):
                turn_hin(n, res[:, n], x1_ready, n + 1)
                if n == 0:
                    hidden(0)
            def next_keys():
                pe.wait_ge(bulk_step, 9)
                nxt = pb[2][0:P, 0:2 * T]
                te.matmul(nxt, shift[:], key_pad[:, :, 1:T + 1], start=True, stop=False)
                te.matmul(nxt, wrap[:], key_pad[:, :, 2:T + 2], start=False, stop=True).then_inc(next_psum, 1)

            each_group(pe, node_group, next_keys)

            def key_row(turn, list_no, count):
                pe.wait_ge(same_ready, count)
                for j in range(U):
                    for part in range(2):
                        last = te.matmul(pb[2][0:P, j * P:(j + 1) * P],
                                         key16[:, part, list_no, ds(turn * U + j, 1)].broadcast_to([P, P]),
                                         ident16[0:P, 0:P], start=(part == 0), stop=(part == 1))
                last.then_inc(key_rows, 1)

            pe.wait_ge(lists_ready, 1)

            def turn_x(turn, c, rows):
                pe.wait_ge(xt_ready, turn * 2 + (c + 1))
                for j in range(U):
                    last = te.transpose(pb[1][:, j * P:(j + 1) * P], rows[:, j], ident[0:P, 0:P])
                last.then_inc(x_turned, 1)

            def scores_of(turn):
                pe.wait_ge(xt_ready, turn * 2 + 3)
                for j in range(U):
                    for k in range(2):
                        last = te.matmul(pb[3][0:P, 256 + j * HEADS:256 + (j + 1) * HEADS], xt[:, k, j * P:(j + 1) * P], wa[:, k],
                                         start=(k == 0), stop=(k == 1))
                last.then_inc(scores_psum, 1)

            def heads(turn, j):
                pe.wait_ge(msg_ready, turn * U + j if j else turn * U + 1)
                te.matmul(pb[4 + j % 2][0:P, :], xt[:, 1, j * P:(j + 1) * P], w1g[:].rearrange("d h f -> d (h f)"),
                          start=True, stop=True).then_inc(h_psum, 1)

            def add_up(turn, j):
                if j == 0:
                    pe.wait_ge(same_ready, turn + 2)
                    pe.wait_ge(esc_ready, turn + 1)
                pe.wait_ge(msg_ready, turn * U + (j + 2))
                pe.wait_ge(agg_ready, turn * U + (j + 1))
                a0 = agg[:, (j - 1) % U]
                for o, m, b in ((pb[6][0:P, :], msg[:, j % 2], a0[:, 0:512]), (pb[7][0:P, 0:HEADS], esc[:, j], a0[:, 512:])):
                    te.matmul(o, same[:, j], m, start=True, stop=False)
                    last = te.matmul(o, carry[:, j], b, start=False, stop=True)
                last.then_inc(agg_psum, 1)

            def turn_xx(turn, j):
                pe.wait_ge(helu_ready, turn * U + (j + 1))
                pe.wait_ge(xx_ready, turn * U + (j + 1))
                for c in range(C2):
                    last = te.transpose(pb[0][:, c * P:(c + 1) * P], hex_[:, j % 2, c * 128:(c + 1) * 128], ident[0:P, 0:P])
                last.then_inc(xx_psum, 1)

            def project(turn, j):
                pe.wait_ge(xx_ready, turn * U + (j + 2))
                pe.wait_ge(g2_ready, turn * U + (j + U))
                for c in range(C2):
                    last = te.matmul(pb[3][0:P, 0:D + 2], xx_t[:, c], w2g[:, c], start=(c == 0), stop=(c == C2 - 1))
                last.then_inc(g2_psum, 1)

            def layer1_first(turn, k, use):
                pe.wait_ge(x_in[k], 32 * U)
                turn_x(turn, 0, xs[:, k])
                key_row(turn, 0, turn + 1)
                turn_x(turn, 1, xd[:, k])
                scores_of(turn)
                heads(turn, 0)
                heads(turn, 1)
                add_up(turn, 0)

            def layer1(turn, k, use):
                more = k is not None
                heads(turn, 2)
                if more:
                    pe.wait_ge(x_in[k], use * (32 * U) + 32 * U)
                    turn_x(turn + 1, 0, xs[:, k])
                add_up(turn, 1)
                heads(turn, 3)
                turn_xx(turn, 0)
                if more:
                    turn_x(turn + 1, 1, xd[:, k])
                project(turn, 0)
                add_up(turn, 2)
                turn_xx(turn, 1)
                add_up(turn, 3)
                project(turn, 1)
                if more:
                    key_row(turn + 1, 0, turn + 2)
                    pe.wait_ge(g2_ready, turn * U + (U + 2))
                    scores_of(turn + 1)
                turn_xx(turn, 2)
                if more:
                    heads(turn + 1, 0)
                    pe.wait_ge(lr_ready, turn + 3)
                project(turn, 2)
                if more:
                    heads(turn + 1, 1)
                turn_xx(turn, 3)
                if more:
                    add_up(turn + 1, 0)
                project(turn, 3)

            ahead(pe, layer1_first, layer1)

            pe.wait_ge(g2_ready, T + U)
            for o, pick in ((0, pick_last), (2, pick_first)):
                te.matmul(pb[2][0:P, o * T:(o + 1) * T], pick[:], s2_all[:], start=True, stop=True)
                last = te.matmul(pb[2][0:P, (o + 1) * T:(o + 2) * T], pick[:], key_pad[:, 0, 1:T + 1], start=True, stop=True)
            last.then_inc(s2_rows, 1)
            pe.wait_ge(s2_ready, 1)

            def add_up_rows(turn, width, round_no, w, old):
                pe.wait_ge(same_ready, turn + (round_no * TURNS + 2))
                pe.wait_ge(msg_ready, turn + (T + (round_no - 1) * TURNS + 2))
                for j in range(U):
                    pe.wait_ge(agg_ready, turn * U + (round_no * T + j + 1))
                    o = pb[3][0:P, 0:width]
                    te.matmul(o, same_of[w][:, j], msg2[:, j, 0:width], start=True, stop=False)
                    te.matmul(o, carry_of[w][:, j], agg2[:, (j - 1) % U, 0:width], start=False, stop=True).then_inc(agg_psum, 1)
                    if old is not None and j < 2:
                        hidden_half(old, j)

            def layer2(turn, k, use):
                n = turn + (CHUNKS - 1)
                old = not isinstance(turn, int) or turn > 0
                if isinstance(turn, int) and turn == TURNS - 1:
                    key_row(0, 1, 2 * TURNS + 1)
                else:
                    key_row(turn + 1, 0, turn + (TURNS + 2))
                if old:
                    turn_hin(n, res[:, 2 - k], x1_ready, turn + (CHUNKS + TURNS))
                add_up_rows(turn, D + 1, 1, k, n if old else None)
                if old:
                    output(n)

            key_row(0, 0, TURNS + 1)
            pipelined(pe, layer2)

            def network2(turn, k, use):
                n = turn + (CHUNKS + TURNS - 1)
                if not isinstance(turn, int) or turn < TURNS - 1:
                    key_row(turn + 1, 1, turn + (2 * TURNS + 2))
                if isinstance(turn, int) and turn == 0:
                    turn_hin(n, res[:, 1], x1_ready, CHUNKS + 2 * TURNS)
                else:
                    turn_hin(n, hin_d, hin_ready, turn)
                add_up_rows(turn, D, 2, 1 - k, n)
                output(n)

            pipelined(pe, network2)
            n = CHUNKS + 2 * TURNS - 1
            turn_hin(n, hin_d, hin_ready, TURNS)
            hidden(n)
            output(n)

        @block.scalar
        def _(act):
            a = nc.scalar
            a.preload_act_table_set("natural_log_exp_and_others")
            act.sem_inc(hist_open, 1)
            for used in (hot_t_ready, run_updated, end_used, found_kept):
                act.sem_inc(used, 1)
            act.sem_inc(run_used, 2)
            act.sem_inc(ranks_done, 2)
            act.sem_inc(high_ready, 2)
            act.sem_inc(hin_t_ready, 1)
            act.sem_inc(hid_ready, 2)
            act.sem_inc(y_sum, 1)
            act.sem_inc(out_free, 4)
            act.sem_inc(x1_free, 2)
            act.sem_inc(row_free, U + 1)
            act.sem_inc(g2_ready, U)
            for used in (xt_ready, xs_free, plain_free, g2_free, same_ready, agg_ready, xx_ready, lr_ready, msg_ready):
                act.sem_inc(used, 1)

            def cast_run(w):
                a.copy(run16[:, w, 0], start_tab).then_inc(run_cast, 1)

            def high_ones(turn, w):
                for j in range(U):
                    act.wait_ge(high_ready, turn * U + (j + 1))
                    for k in range(2):
                        last = a.activation(apart[:, j % 2, k], digits[:, 0:HI], ACT.Square, bias=digit[:, k, 0, ds(turn * U + j, 1)],
                                            scale=-1.0)
                    last.then_inc(apart_ready, 1)
                    act.wait_ge(apart_ready, turn * U + (j + 1))
                    a.activation(hot[:, w, j, :, 0:HI], apart[:, j % 2], ACT.Relu, bias=ones[0:P, 0:1], scale=-1.0).then_inc(high_ready, 1)

            def first_tables(turn, w, use):
                act.wait_ge(degrees_ready, 1)
                high_ones(turn, w)
                act.wait_ge(tables_ready, 1)
                cast_run(w)

            def places(turn, nxt, use):
                for half in range(2):
                    act.wait_ge(hot_t_psum, turn * 2 + (half + 1))
                    a.copy(hot_t[:, 2 * half:2 * half + 2, :, 0:P],
                           hot_t_ps[0:HH, :].rearrange("p (u o e) -> p u o e", u=2, o=4)[:, :, :, 0:P]).then_inc(hot_t_ready, 1)
                if nxt is not None:
                    act.wait_ge(run_updated, turn + 2)
                    cast_run(nxt)
                    high_ones(turn + 1, nxt)

            ahead(act, first_tables, places)

            def exp_x(n, xv, k):
                a.activation(xex[:, k], xv, ACT.Exp).then_inc(x_exp, 1)

            def rstd_of(n, mom, r, moments, log, ready, k):
                act.wait_ge(moments, n + 1)
                a.activation(r[:, k], mom[:, k, :, 1], ACT.Ln, bias=ln_eps[0:P, 0:1]).then_inc(log, 1)
                act.wait_ge(log, n + 1)
                a.activation(r[:, k], r[:, k], ACT.Exp, scale=-0.5).then_inc(ready, 1)

            def x_rstd_of(n, k):
                rstd_of(n, moment, rstd, x_moments, x_log, x_rstd, k)

            def y_rstd_of(n, k):
                rstd_of(n, post_moment, post_rstd, y_moments, y_log, y_rstd, k)

            def copy_hin(n, scaled):
                act.wait_ge(hin_turned, n + 1)
                scale = eps1[:, 0:1] if scaled else 1.0
                a.activation(hin_t[:], pb[4][:, 0:U * P], ACT.Copy if not scaled else ACT.Identity, scale=scale).then_inc(hin_t_ready, 1)

            def relu_half(n, c, k=0):
                act.wait_ge(hid_psum, n * 2 + (c + 1))
                a.activation(hid[:, k, c], pb[5 + c][:, 0:U * P], ACT.Relu, bias=b1[:, c:c + 1]).then_inc(hid_ready, 1)

            def relus(n, k=0):
                for c in range(2):
                    relu_half(n, c, k)

            act.wait_ge(weights_ready, 1)

            def result(n, k):
                act.wait_ge(y_bias, n + 1)
                act.wait_ge(out_free, n + 1)
                for j in range(U):
                    last = a.activation(outb[:, k, j], post_sum[:, k % 2, j], ACT.Identity, bias=post_bias[:, k, j:j + 1],
                                        scale=post_rstd[:, k, j:j + 1])
                last.then_inc(y_out, 1)

            def node_group(n, k, use):
                if there(n, 1):
                    relus(n + 1, (k + 1) % 2)
                if there(n, 2):
                    copy_hin(n + 2, True)
                if there(n, 3):
                    x_rstd_of(n + 3, (k + 3) % 4)
                if there(n, 5):
                    act.wait_ge(x_loaded[(k + 1) % 4], use * 16 + (48 if k == 3 else 32))
                    exp_x(n + 5, xin[:, (k + 1) % 4], (k + 1) % 4)
                if there(n, -1):
                    result(n - 1, (k + 3) % 4)
                y_rstd_of(n, k)

            for n in range(4):
                act.wait_ge(x_loaded[n], 16)
                exp_x(n, xin[:, n], n)
                if n < 3:
                    x_rstd_of(n, n)
            act.wait_ge(x_loaded[0], 32)
            exp_x(4, xin[:, 0], 0)
            copy_hin(0, True)
            relus(0, 0)
            copy_hin(1, True)
            each_group(act, node_group)
            result(CHUNKS - 1, 3)

            def copy_xt(turn, c):
                act.wait_ge(x_turned, turn * 2 + (c + 1))
                a.copy(xt[:, c], pb[1][:, 0:U * P]).then_inc(xt_ready, 1)

            def exp_scores(turn):
                act.wait_ge(lr_ready, turn + 2)
                a.activation(esc[:], lr[:], ACT.Exp, scale=-1.0).then_inc(esc_ready, 1)

            def copy_agg(turn, j):
                act.wait_ge(agg_psum, turn * U + (j + 1))
                a.copy(agg[:, j, 0:512], pb[6][0:P, :])
                a.copy(agg[:, j, 512:], pb[7][0:P, 0:HEADS]).then_inc(agg_ready, 1)

            def exp_h(turn, j):
                act.wait_ge(hp_ready, turn * U + (j + 1))
                a.activation(hex_[:, j % 2], hp[:, j % 2], ACT.Exp).then_inc(hex_ready, 1)

            def copy_xx(turn, j):
                act.wait_ge(xx_psum, turn * U + (j + 1))
                a.copy(xx_t[:], pb[0][:, 0:C2 * P].rearrange("p (c e) -> p c e", c=C2)).then_inc(xx_ready, 1)

            def copy_g2(turn, j):
                act.wait_ge(g2_psum, turn * U + (j + 1))
                if j == 0:
                    act.wait_ge(g2_free, turn + 1)
                a.copy(s2_all[:, ds(turn * U + j, 1)], pb[3][0:P, D:D + 1])
                a.copy(g2s[:, j], pb[3][0:P, 0:D + 2]).then_inc(g2_ready, 1)

            def layer1_first(turn, k, use):
                copy_xt(turn, 0)
                copy_xt(turn, 1)
                exp_x(turn, xd[:, k], 0)
                exp_scores(turn)
                copy_agg(turn, 0)
                x_rstd_of(turn + CHUNKS, 0)

            def layer1(turn, k, use):
                more = k is not None
                if more:
                    copy_xt(turn + 1, 0)
                exp_h(turn, 0)
                copy_agg(turn, 1)
                copy_xx(turn, 0)
                exp_h(turn, 1)
                if more:
                    copy_xt(turn + 1, 1)
                copy_g2(turn, 0)
                copy_agg(turn, 2)
                copy_xx(turn, 1)
                exp_h(turn, 2)
                copy_agg(turn, 3)
                copy_g2(turn, 1)
                exp_h(turn, 3)
                if more:
                    exp_x(turn + 1, xd[:, k], 0)
                    exp_scores(turn + 1)
                copy_xx(turn, 2)
                copy_g2(turn, 2)
                copy_xx(turn, 3)
                if more:
                    copy_agg(turn + 1, 0)
                    copy_g2(turn, 3)
                    x_rstd_of(turn + (CHUNKS + 1), 0)
                else:
                    copy_g2(turn, 3)

            ahead(act, layer1_first, layer1)

            def copy_agg2(turn, width, round_no, old, meanwhile, after=0):
                for j in range(U):
                    act.wait_ge(agg_psum, turn * U + (round_no * T + j + 1))
                    a.copy(agg2[:, j, 0:width], pb[3][0:P, 0:width]).then_inc(agg_ready, 1)
                    if j == after:
                        meanwhile()
                    if old is not None and j < 2:
                        relu_half(old, j)

            def exp_scores2(turn):
                act.wait_ge(sc2_ready, turn + 1)
                a.activation(msg2[:, :, D], sc2[:, 0], ACT.Exp, scale=-1.0).then_inc(e2_ready, 1)

            def layer2(turn, k, use):
                group = turn + (CHUNKS + TURNS)
                n = turn + (CHUNKS - 1)
                old = not isinstance(turn, int) or turn > 0
                if old:
                    copy_hin(n, True)
                copy_agg2(turn, D + 1, 1, n if old else None,
                          (lambda: y_rstd_of(n - 1, k)) if not isinstance(turn, int) or turn >= 2 else lambda: None)
                act.wait_ge(hp_ready, turn + (T + 1))
                exp_x(group, h2[:], 0)
                x_rstd_of(group, 0)
                if not isinstance(turn, int) or turn < TURNS - 1:
                    exp_scores2(turn + 1)

            exp_scores2(0)
            pipelined(act, layer2)

            def edge_squares(turn, k, use):
                act.wait_ge(a_in[k], use * (16 * U) + 16 * U)
                a.activation(sqr[:, 1], ra[:, k], ACT.Square).then_inc(squares, 1)
                act.wait_ge(b_in[k], use * (16 * U) + 16 * U)
                a.activation(sqr[:, 2], xb[:, k], ACT.Square).then_inc(squares, 1)

            def edge_norms(turn):
                act.wait_ge(sim_step, turn * 6 + 1)
                a.activation(simt[:, 2:4], simt[:, 0:2], ACT.Ln).then_inc(norm_log, 1)
                act.wait_ge(norm_log, turn + 1)
                a.activation(simt[:, 2:4], simt[:, 2:4], ACT.Exp, scale=0.5).then_inc(norm_ready, 1)

            def network2(turn, k, use):
                n = turn + (CHUNKS + TURNS - 1)
                edge_squares(turn, k, use)
                copy_hin(n, isinstance(turn, int) and turn == 0)
                edge_norms(turn)
                copy_agg2(turn, D, 2, n, lambda: y_rstd_of(n - 1, 1 - k), 1)
                a.copy(xb_kept[:, k], xb[:, k]).then_inc(b_kept, 1)

            pipelined(act, network2)
            n = CHUNKS + 2 * TURNS - 1
            copy_hin(n, False)
            relus(n)
            y_rstd_of(n - 1, (TURNS - 1) % 2)
            y_rstd_of(n, TURNS % 2)


_INS = ["x", "src", "dst", "edge_attr_128", "L0_gnn_W1", "L0_gnn_a1", "L0_gnn_W2", "L0_gnn_a2",
        "L1_gnn_W1", "L1_gnn_b1", "L1_gnn_W2", "L1_gnn_b2", "L1_gnn_eps"]


def kernel(**inputs):
    import numpy as _np
    import concourse.bacc as _bacc
    from concourse import mybir as _mybir
    from concourse.bass_utils import run_bass_kernel_spmd as _run

    nc = _bacc.Bacc("TRN2", target_bir_lowering=False, num_devices=1)
    arrays, args = {}, []
    for name in _INS:
        a = _np.ascontiguousarray(inputs[name])
        a = a.reshape(a.shape or (1,))
        arrays[f"in_{name}_dram"] = a
        args.append(nc.dram_tensor(f"in_{name}_dram", a.shape, _mybir.dt.from_np(a.dtype), kind="ExternalInput").ap())
    args.append(nc.dram_tensor("out_0_dram", (50000, 128), _mybir.dt.float32, kind="ExternalOutput").ap())
    build_gnn(nc, *args)
    r = _run(nc, [arrays], core_ids=[0])
    return r.results[0]["out_0_dram"]
```
